# Optimizing a Trainium2 kernel written in Bass

```python
import numpy as np
import jax
import jax.numpy as jnp

def _softmax(x, axis=-1):
    return jax.nn.softmax(x, axis=axis)

def _gelu(x):
    return jax.nn.gelu(x, approximate=True)

def _silu(x):
    return jax.nn.silu(x)

def _sigmoid(x):
    return jax.nn.sigmoid(x)

def _layernorm(x, axis=-1, eps=1e-05):
    m = jnp.mean(x, axis=axis, keepdims=True)
    v = jnp.var(x, axis=axis, keepdims=True)
    return (x - m) / jnp.sqrt(v + eps)

def _scatter_add(tgt, idx, src, axis=0):
    return tgt.at[idx].add(src)

def _segment_sum(src, seg, n):
    return jax.ops.segment_sum(src, seg, n)
kernel_name = 'mk_macaron_d2_jaxref_r8_b801ec'

def setup_inputs(seed: int=0):
    np.random.seed(seed)
    _w = jnp.asarray

    def _L0_attn_setup():
        import jax, jax.numpy as jnp
        import numpy as np
        D_MODEL = 256
        N_HEADS = 32
        N_KV = 8
        HEAD_DIM = D_MODEL // N_HEADS
        N_GROUPS = N_HEADS // N_KV
        ROPE_BASE = 10000.0
        SCALE = HEAD_DIM ** (-0.5)
        BATCH, SEQ = (2, 256)

        def _apply_rope(q, k, seq_len):
            half = HEAD_DIM // 2
            inv_freq = 1.0 / ROPE_BASE ** (jnp.arange(0, half, dtype=jnp.float32) / half)
            ang = jnp.arange(seq_len, dtype=jnp.float32)[:, None] * inv_freq[None, :]
            cos = jnp.concatenate([jnp.cos(ang), jnp.cos(ang)], axis=-1)[None, None]
            sin = jnp.concatenate([jnp.sin(ang), jnp.sin(ang)], axis=-1)[None, None]

            def rot_half(t):
                t1, t2 = jnp.split(t, 2, axis=-1)
                return jnp.concatenate([-t2, t1], axis=-1)
            q = q * cos + rot_half(q) * sin
            k = k * cos + rot_half(k) * sin
            return (q, k)
        key = jax.random.key(seed)
        k1, k2, k3, k4, k5 = jax.random.split(key, 5)
        init = 0.02
        return {'x': jax.random.normal(k1, (BATCH, SEQ, D_MODEL), jnp.float32), 'Wq': jax.random.normal(k2, (D_MODEL, D_MODEL), jnp.float32) * init, 'Wk': jax.random.normal(k3, (N_KV * HEAD_DIM, D_MODEL), jnp.float32) * init, 'Wv': jax.random.normal(k4, (N_KV * HEAD_DIM, D_MODEL), jnp.float32) * init, 'Wo': jax.random.normal(k5, (D_MODEL, D_MODEL), jnp.float32) * init}
    _L0_attn_in = _L0_attn_setup()

    def _L0_ffn_setup():
        import jax, jax.numpy as jnp
        import numpy as np
        E, TOPK, H, I = (8, 2, 256, 512)
        SOFTCAP = 30.0
        key = jax.random.key(seed)
        ks = jax.random.split(key, 5)
        s = 1.0 / np.sqrt(H)
        si = 1.0 / np.sqrt(I)
        return {'hidden_states': jax.random.normal(ks[0], (4, 256, H), jnp.float32), 'w_gate': jax.random.normal(ks[1], (H, E), jnp.float32) * s, 'w1': jax.random.normal(ks[2], (E, H, I), jnp.float32) * s, 'w3': jax.random.normal(ks[3], (E, H, I), jnp.float32) * s, 'w2': jax.random.normal(ks[4], (E, I, H), jnp.float32) * si}
    _L0_ffn_in = _L0_ffn_setup()

    def _L1_attn_setup():
        import jax, jax.numpy as jnp
        import numpy as np
        H, P, N, G, K, CH, E = (32, 128, 128, 8, 4, 32, 256)
        I = H * P
        CD = I + 2 * G * N
        PROJ = I + CD + H
        EPS = 1e-06

        def segsum(x):
            L = x.shape[-1]
            cs = jnp.cumsum(x, axis=-1)
            ss = cs[..., :, None] - cs[..., None, :]
            mask = jnp.tril(jnp.ones((L, L), dtype=bool))
            return jnp.where(mask, ss, -jnp.inf)
        key = jax.random.key(seed)
        ks = jax.random.split(key, 6)
        b, s = (2, 256)
        return {'x': jax.random.normal(ks[0], (b, s, E), jnp.float32), 'in_proj_w': jax.random.normal(ks[1], (PROJ, E), jnp.float32) / np.sqrt(E), 'conv_w': jax.random.normal(ks[2], (CD, 1, K), jnp.float32) / np.sqrt(K), 'conv_b': jax.random.normal(ks[3], (CD,), jnp.float32) * 0.02, 'dt_bias': jax.random.normal(ks[4], (H,), jnp.float32) * 0.1 + 1.0, 'A_log': jnp.log(jnp.arange(1, H + 1, dtype=jnp.float32)), 'D': jnp.ones((H,), jnp.float32), 'norm_w': jnp.ones((I,), jnp.float32), 'out_proj_w': jax.random.normal(ks[5], (E, I), jnp.float32) / np.sqrt(I)}
    _L1_attn_in = _L1_attn_setup()

    def _L1_ffn_setup():
        import jax, jax.numpy as jnp
        import numpy as np

        def _sparsify_2to4(h):
            B, S, I = h.shape
            g = h.reshape(B, S, I // 4, 4)
            a = jnp.abs(g)
            _, idx = jax.lax.top_k(a, 2)
            pos = jnp.arange(4)
            mask = (pos == idx[..., 0:1]) | (pos == idx[..., 1:2])
            return (g * mask.astype(g.dtype)).reshape(B, S, I)
        key = jax.random.key(seed)
        k1, k2, k3, k4 = jax.random.split(key, 4)
        B, S, H, I = (4, 256, 256, 1024)
        x = jax.random.normal(k1, (B, S, H), dtype=jnp.float32)
        w_gate = jax.random.normal(k2, (H, I), dtype=jnp.float32) / np.sqrt(H)
        w_up = jax.random.normal(k3, (H, I), dtype=jnp.float32) / np.sqrt(H)
        w_down = jax.random.normal(k4, (I, H), dtype=jnp.float32) / np.sqrt(I)
        return {'x': x, 'w_gate': w_gate, 'w_up': w_up, 'w_down': w_down}
    _L1_ffn_in = _L1_ffn_setup()
    _d = {'L0_attn_x': _L0_attn_in['x'], 'L0_attn_Wq': _L0_attn_in['Wq'], 'L0_attn_Wk': _L0_attn_in['Wk'], 'L0_attn_Wv': _L0_attn_in['Wv'], 'L0_attn_Wo': _L0_attn_in['Wo'], 'L0_ffn_w_gate': _L0_ffn_in['w_gate'], 'L0_ffn_w1': _L0_ffn_in['w1'], 'L0_ffn_w3': _L0_ffn_in['w3'], 'L0_ffn_w2': _L0_ffn_in['w2'], 'L1_attn_in_proj_w': _L1_attn_in['in_proj_w'], 'L1_attn_conv_w': _L1_attn_in['conv_w'], 'L1_attn_conv_b': _L1_attn_in['conv_b'], 'L1_attn_dt_bias': _L1_attn_in['dt_bias'], 'L1_attn_A_log': _L1_attn_in['A_log'], 'L1_attn_D': _L1_attn_in['D'], 'L1_attn_norm_w': _L1_attn_in['norm_w'], 'L1_attn_out_proj_w': _L1_attn_in['out_proj_w'], 'L1_ffn_w_gate': _L1_ffn_in['w_gate'], 'L1_ffn_w_up': _L1_ffn_in['w_up'], 'L1_ffn_w_down': _L1_ffn_in['w_down']}
    _x0 = _d['L0_attn_x']
    _d['L0_attn_x'] = jax.random.normal(jax.random.fold_in(jax.random.key(seed), 1), (1, 1024, 256), dtype=_x0.dtype)
    del _x0
    return _d

def reference(L0_attn_x, L0_attn_Wq, L0_attn_Wk, L0_attn_Wv, L0_attn_Wo, L0_ffn_w_gate, L0_ffn_w1, L0_ffn_w3, L0_ffn_w2, L1_attn_in_proj_w, L1_attn_conv_w, L1_attn_conv_b, L1_attn_dt_bias, L1_attn_A_log, L1_attn_D, L1_attn_norm_w, L1_attn_out_proj_w, L1_ffn_w_gate, L1_ffn_w_up, L1_ffn_w_down):

    def _L0_attn_ref(x, Wq, Wk, Wv, Wo):
        import jax, jax.numpy as jnp
        import numpy as np
        D_MODEL = 256
        N_HEADS = 32
        N_KV = 8
        HEAD_DIM = D_MODEL // N_HEADS
        N_GROUPS = N_HEADS // N_KV
        ROPE_BASE = 10000.0
        SCALE = HEAD_DIM ** (-0.5)
        BATCH, SEQ = (2, 256)

        def _apply_rope(q, k, seq_len):
            half = HEAD_DIM // 2
            inv_freq = 1.0 / ROPE_BASE ** (jnp.arange(0, half, dtype=jnp.float32) / half)
            ang = jnp.arange(seq_len, dtype=jnp.float32)[:, None] * inv_freq[None, :]
            cos = jnp.concatenate([jnp.cos(ang), jnp.cos(ang)], axis=-1)[None, None]
            sin = jnp.concatenate([jnp.sin(ang), jnp.sin(ang)], axis=-1)[None, None]

            def rot_half(t):
                t1, t2 = jnp.split(t, 2, axis=-1)
                return jnp.concatenate([-t2, t1], axis=-1)
            q = q * cos + rot_half(q) * sin
            k = k * cos + rot_half(k) * sin
            return (q, k)
        b, s, _ = x.shape
        q = jnp.einsum('bsd,ed->bse', x, Wq).reshape(b, s, N_HEADS, HEAD_DIM).transpose(0, 2, 1, 3)
        k = jnp.einsum('bsd,ed->bse', x, Wk).reshape(b, s, N_KV, HEAD_DIM).transpose(0, 2, 1, 3)
        v = jnp.einsum('bsd,ed->bse', x, Wv).reshape(b, s, N_KV, HEAD_DIM).transpose(0, 2, 1, 3)
        q, k = _apply_rope(q, k, s)
        qg = q.reshape(b, N_KV, N_GROUPS, s, HEAD_DIM)
        scores = jnp.einsum('bkgqd,bkld->bkgql', qg, k) * SCALE
        attn = jax.nn.softmax(scores, axis=-1)
        out = jnp.einsum('bkgql,bkld->bkgqd', attn, v)
        out = out.reshape(b, N_HEADS, s, HEAD_DIM).transpose(0, 2, 1, 3).reshape(b, s, D_MODEL)
        return jnp.einsum('bsd,ed->bse', out, Wo)

    def _L0_ffn_ref(hidden_states, w_gate, w1, w3, w2):
        import jax, jax.numpy as jnp
        import numpy as np
        E, TOPK, H, I = (8, 2, 256, 512)
        SOFTCAP = 30.0
        orig_shape = hidden_states.shape
        x = hidden_states.reshape(-1, H)
        logits = x @ w_gate
        logits = SOFTCAP * jnp.tanh(logits / SOFTCAP)
        probs = jax.nn.softmax(logits, axis=-1)
        _, idx = jax.lax.top_k(probs, TOPK)
        mask = jax.nn.one_hot(idx, E, dtype=probs.dtype).sum(-2)
        weights = probs * mask
        out = jnp.zeros_like(x)
        for e in range(E):
            h = jax.nn.silu(x @ w1[e]) * (x @ w3[e])
            out = out + h @ w2[e] * weights[:, e:e + 1]
        return out.reshape(orig_shape)

    def _L1_attn_ref(x, in_proj_w, conv_w, conv_b, dt_bias, A_log, D, norm_w, out_proj_w):
        import jax, jax.numpy as jnp
        import numpy as np
        H, P, N, G, K, CH, E = (32, 128, 128, 8, 4, 32, 256)
        I = H * P
        CD = I + 2 * G * N
        PROJ = I + CD + H
        EPS = 1e-06

        def segsum(x):
            L = x.shape[-1]
            cs = jnp.cumsum(x, axis=-1)
            ss = cs[..., :, None] - cs[..., None, :]
            mask = jnp.tril(jnp.ones((L, L), dtype=bool))
            return jnp.where(mask, ss, -jnp.inf)
        b, s, _ = x.shape
        proj = x @ in_proj_w.T
        gate, hbc, dt = jnp.split(proj, [I, I + CD], axis=-1)
        hbc_t = jnp.transpose(hbc, (0, 2, 1))
        conv = jax.lax.conv_general_dilated(hbc_t, conv_w, window_strides=(1,), padding=[(K - 1, 0)], feature_group_count=CD, dimension_numbers=('NCH', 'OIH', 'NCH'))
        hbc = jax.nn.silu(jnp.transpose(conv + conv_b[None, :, None], (0, 2, 1)))
        hs, B, C = jnp.split(hbc, [I, I + G * N], axis=-1)
        A = -jnp.exp(A_log.astype(jnp.float32))
        dt = jax.nn.softplus(dt.astype(jnp.float32) + dt_bias)
        dt = jnp.clip(dt, 0.0, None)
        X = hs.reshape(b, s, H, P).astype(jnp.float32)
        B = jnp.tile(B.reshape(b, s, G, N).astype(jnp.float32), (1, 1, H // G, 1))
        C = jnp.tile(C.reshape(b, s, G, N).astype(jnp.float32), (1, 1, H // G, 1))
        D_res = D[:, None] * X
        X = X * dt[..., None]
        A_bt = A * dt
        nc = s // CH
        Xc = X.reshape(b, nc, CH, H, P)
        Bc = B.reshape(b, nc, CH, H, N)
        Cc = C.reshape(b, nc, CH, H, N)
        Ac = jnp.transpose(A_bt.reshape(b, nc, CH, H), (0, 3, 1, 2))
        A_cum = jnp.cumsum(Ac, axis=-1)
        Lmat = jnp.exp(segsum(Ac))
        Y_diag = jnp.einsum('bclhn,bcshn,bhcls,bcshd->bclhd', Cc, Bc, Lmat, Xc)
        decay_states = jnp.exp(A_cum[..., -1:] - A_cum)
        states = jnp.einsum('bclhn,bhcl,bclhd->bchdn', Bc, decay_states, Xc)
        states = jnp.concatenate([jnp.zeros_like(states[:, :1]), states], axis=1)
        A_last = jnp.pad(A_cum[..., -1], ((0, 0), (0, 0), (1, 0)))
        decay_chunk = jnp.exp(segsum(A_last))
        new_states = jnp.einsum('bhij,bjhdn->bihdn', decay_chunk, states)
        states_prev = new_states[:, :-1]
        state_decay = jnp.exp(A_cum)
        Y_off = jnp.einsum('bclhn,bchdn,bhcl->bclhd', Cc, states_prev, state_decay)
        y = (Y_diag + Y_off).reshape(b, s, H, P) + D_res
        y = y.reshape(b, s, I)
        gs = I // G
        h32 = y * jax.nn.silu(gate.astype(jnp.float32))
        g = h32.reshape(b, s, I // gs, gs)
        var = jnp.mean(g * g, axis=-1, keepdims=True)
        h32 = (g * jax.lax.rsqrt(var + EPS)).reshape(b, s, I)
        return norm_w * h32 @ out_proj_w.T

    def _L1_ffn_ref(x, w_gate, w_up, w_down):
        import jax, jax.numpy as jnp
        import numpy as np

        def _sparsify_2to4(h):
            B, S, I = h.shape
            g = h.reshape(B, S, I // 4, 4)
            a = jnp.abs(g)
            _, idx = jax.lax.top_k(a, 2)
            pos = jnp.arange(4)
            mask = (pos == idx[..., 0:1]) | (pos == idx[..., 1:2])
            return (g * mask.astype(g.dtype)).reshape(B, S, I)
        h = jax.nn.silu(jnp.einsum('bsh,hi->bsi', x, w_gate)) * jnp.einsum('bsh,hi->bsi', x, w_up)
        h_sparse = _sparsify_2to4(h)
        return jnp.einsum('bsi,ih->bsh', h_sparse, w_down)
    x = L0_attn_x
    x = x + 0.5 * _L0_ffn_ref(_layernorm(x, axis=-1), L0_ffn_w_gate, L0_ffn_w1, L0_ffn_w3, L0_ffn_w2)
    x = x + _L0_attn_ref(_layernorm(x, axis=-1), L0_attn_Wq, L0_attn_Wk, L0_attn_Wv, L0_attn_Wo)
    x = x + 0.5 * _L0_ffn_ref(_layernorm(x, axis=-1), L0_ffn_w_gate, L0_ffn_w1, L0_ffn_w3, L0_ffn_w2)
    x = x + 0.5 * _L1_ffn_ref(_layernorm(x, axis=-1), L1_ffn_w_gate, L1_ffn_w_up, L1_ffn_w_down)
    x = x + _L1_attn_ref(_layernorm(x, axis=-1), L1_attn_in_proj_w, L1_attn_conv_w, L1_attn_conv_b, L1_attn_dt_bias, L1_attn_A_log, L1_attn_D, L1_attn_norm_w, L1_attn_out_proj_w)
    x = x + 0.5 * _L1_ffn_ref(_layernorm(x, axis=-1), L1_ffn_w_gate, L1_ffn_w_up, L1_ffn_w_down)
    return x

_drawn_inputs = setup_inputs


def setup_inputs(seed=0):
    import zlib

    import numpy as np

    out = dict(_drawn_inputs(seed))
    spreads = {'L1_attn_D': (1.0, 0.6), 'L1_attn_norm_w': (1.0, 0.2)}
    factors = {'L0_attn_Wq': 8.0,
     'L0_attn_Wk': 8.0,
     'L0_attn_Wv': 4.462,
     'L0_attn_Wo': 4.325,
     'L1_attn_conv_b': 2.692}
    for name, (base, spread) in spreads.items():
        noise = np.random.default_rng([zlib.crc32(name.encode()), seed]).standard_normal(out[name].shape)
        drawn = base * np.exp(spread * noise) if base else spread * noise
        out[name] = jnp.asarray(drawn.astype(out[name].dtype))
    for name, factor in factors.items():
        out[name] = (out[name] * factor).astype(out[name].dtype)
    return out
```

```python
from contextlib import ExitStack

import concourse.bass as bass
from concourse import mybir

F32 = mybir.dt.float32
F32R = mybir.dt.float32r
BF16 = mybir.dt.bfloat16
U32 = mybir.dt.uint32
ALU = mybir.AluOpType
ACT = mybir.ActivationFunctionType
AX_X = mybir.AxisListType.X

P = 128
D = 256
S = 1024
TT = S // P
KD = D // P
BANK = 512
LN_EPS = 1e-5


class Space:

    def __init__(self, nc, ctx, prefix):
        self.nc, self.ctx, self.prefix, self.sems = nc, ctx, prefix, []

    def sb(self, name, shape, dt=F32):
        return self.ctx.enter_context(self.nc.sbuf_tensor(f"{self.prefix}_{name}", shape, dt))

    def ps(self, name, shape, dt=F32):
        return self.ctx.enter_context(self.nc.psum_tensor(f"{self.prefix}_{name}", shape, dt))

    def sem(self, name):
        self.sems.append(self.ctx.enter_context(self.nc.semaphore(f"{self.prefix}_{name}")))
        return self.sems[-1]

    def clear_sems(self):
        numbers = sorted(s.num for s in self.sems)
        with self.nc.Block() as block:
            @block.gpsimd
            def _(pool):
                at = 0
                for n in range(1, len(numbers) + 1):
                    if n == len(numbers) or numbers[n] != numbers[n - 1] + 1:
                        pool.sem_clear(range(numbers[at], numbers[n - 1] + 1))
                        at = n


def matmul3(nc, out, lhs, rhs, start, stop):
    (lhs_hi, lhs_lo), (rhs_hi, rhs_lo) = lhs, rhs
    nc.tensor.matmul(out, lhs_hi, rhs_hi, start=start, stop=False)
    nc.tensor.matmul(out, lhs_hi, rhs_lo, start=False, stop=False)
    return nc.tensor.matmul(out, lhs_lo, rhs_hi, start=False, stop=stop)


def f32(ap):
    return ap.bitcast(F32)


class LayerNorm:

    def __init__(self, sp, banks, keep_f32=True, parts=None):
        self.banks = banks
        self.stats = sp.sb("ln_stats", [P, TT, 6])
        self.mv = sp.sb("ln_mean_var", [P, TT, 2])
        self.std = sp.sb("ln_std", [P, TT])
        self.rstd = sp.sb("ln_rstd", [P, TT])
        self.eps = sp.sb("ln_eps", [P, 1])
        self.xn = sp.sb("xn", [P, TT, D])
        self.xnT = sp.sb("xnT", [P, KD, S]) if keep_f32 else None
        self.hi, self.lo = parts or (sp.sb("xnT_hi", [P, KD, S], F32R), sp.sb("xnT_lo", [P, KD, S], F32R))
        self.stats_done = sp.sem("ln_stats_done")
        self.mv_done = sp.sem("ln_mv_done")
        self.std_done = sp.sem("ln_std_done")
        self.rstd_done = sp.sem("ln_rstd_done")
        self.xn_done = sp.sem("ln_xn_done")
        self.turned = sp.sem("ln_turned")
        self.hi_done = sp.sem("ln_hi_done")
        self.lo_done = sp.sem("ln_lo_done")

    PAIRS = TT // 2

    def vector(self, nc, x):
        eng = nc.vector
        eng.memset(self.eps[:], LN_EPS).then_inc(self.stats_done, 1)
        for t in range(TT):
            eng.bn_stats(self.stats[:, t, :], x[:, t, :]).then_inc(self.stats_done, 1)
        eng.wait_ge(self.stats_done, TT + 1)
        for t in range(TT):
            eng.bn_aggr(self.mv[:, t, :], self.stats[:, t, :]).then_inc(self.mv_done, 1)
        eng.wait_ge(self.std_done, 1)
        eng.reciprocal(self.rstd[:], self.std[:]).then_inc(self.rstd_done, 1)
        eng.wait_ge(self.rstd_done, 1)
        for t in range(TT):
            eng.tensor_scalar(self.xn[:, t, :], x[:, t, :], self.mv[:, t, 0:1], self.rstd[:, t:t + 1],
                              ALU.subtract, ALU.mult).then_inc(self.xn_done, 1)
        for q in range(self.PAIRS):
            eng.wait_ge(self.hi_done, q + 1)
            cols = slice(2 * P * q, 2 * P * (q + 1))
            eng.tensor_tensor(self.lo[:, :, cols], self.banks[q % 2][:, :].rearrange("p (k n) -> p k n", k=KD),
                              f32(self.hi[:, :, cols]), ALU.subtract).then_inc(self.lo_done, 1)

    def scalar(self, nc):
        eng = nc.scalar
        eng.wait_ge(self.mv_done, TT)
        eng.activation(self.std[:], self.mv[:, :, 1], ACT.Sqrt, bias=self.eps[:]).then_inc(self.std_done, 1)
        for q in range(self.PAIRS):
            eng.wait_ge(self.turned, q + 1)
            cols = slice(2 * P * q, 2 * P * (q + 1))
            bank = self.banks[q % 2][:, :].rearrange("p (k n) -> p k n", k=KD)
            if self.xnT is not None:
                eng.copy(self.xnT[:, :, cols], bank)
            eng.copy(self.hi[:, :, cols], bank).then_inc(self.hi_done, 1)

    def tensor(self, nc, ident):
        eng = nc.tensor
        for q in range(self.PAIRS):
            eng.wait_ge(self.xn_done, 2 * (q + 1))
            if q >= 2:
                eng.wait_ge(self.lo_done, q - 1)
            for k in range(KD):
                for t in range(2):
                    last = eng.transpose(self.banks[q % 2][:, (2 * k + t) * P:(2 * k + t + 1) * P],
                                         self.xn[:, 2 * q + t, k * P:(k + 1) * P], ident)
            last.then_inc(self.turned, 1)

    def ready(self, eng):
        eng.wait_ge(self.lo_done, self.PAIRS)

    def parts(self, k, cols):
        return self.hi[:, k, cols], self.lo[:, k, cols]


EXPERTS = 8
INNER = 512
KI = INNER // P
SOFTCAP = 30.0


def moe_layer(nc, xres, ident, iota8, w_gate, w1, w3, w2, tag):
    with ExitStack() as ctx:
        sp = Space(nc, ctx, tag)
        wg = sp.sb("w_gate", [P, KD, EXPERTS])
        logit = sp.sb("logit", [P, TT, EXPERTS])
        prob = sp.sb("prob", [P, TT, EXPERTS])
        row_max = sp.sb("row_max", [P, TT])
        row_sum = sp.sb("row_sum", [P, TT])
        top = sp.sb("top", [P, TT, 8])
        top_at = sp.sb("top_at", [P, TT, 8], U32)
        top_atf = sp.sb("top_atf", [P, TT, 2])
        chosen = sp.sb("chosen", [P, TT, EXPERTS])
        weight = sp.sb("weight", [P, TT, EXPERTS])
        w_up = [sp.sb(f"w_up{b}", [P, 2 * KD, INNER]) for b in range(2)]
        w_up_hi = [sp.sb(f"w_up_hi{b}", [P, 2 * KD, INNER], F32R) for b in range(2)]
        w_up_lo = [sp.sb(f"w_up_lo{b}", [P, 2 * KD, INNER], F32R) for b in range(2)]
        w_dn = [sp.sb(f"w_dn{b}", [P, KI, D]) for b in range(2)]
        w_dn_hi = [sp.sb(f"w_dn_hi{b}", [P, KI, D], F32R) for b in range(2)]
        w_dn_lo = [sp.sb(f"w_dn_lo{b}", [P, KI, D], F32R) for b in range(2)]
        g = sp.sb("silu", [P, 2, BANK])
        h = sp.sb("h", [P, 2, BANK])
        h_hi = sp.sb("h_hi", [P, KI, S], F32R)
        h_lo = sp.sb("h_lo", [P, KI, S], F32R)
        gate_ps = [sp.ps(f"gate{b}", [P, BANK]) for b in range(2)]
        up_ps = [sp.ps(f"up{b}", [P, BANK]) for b in range(2)]
        down_ps = [sp.ps(f"down{b}", [P, 2, D]) for b in range(4)]
        ln = LayerNorm(sp, gate_ps)

        loaded = [sp.sem(f"loaded{b}") for b in range(2)]
        wg_loaded = sp.sem("wg_loaded")
        w_hi_done, w_lo_done = sp.sem("w_hi_done"), sp.sem("w_lo_done")
        logits_done = sp.sem("logits_done")
        router = sp.sem("router")
        router_act = sp.sem("router_act")
        gate_done, up_done = sp.sem("gate_done"), sp.sem("up_done")
        silu_done, h_done = sp.sem("silu_done"), sp.sem("h_done")
        h_hi_done, h_lo_done = sp.sem("h_hi_done"), sp.sem("h_lo_done")
        down_done, added = sp.sem("down_done"), sp.sem("added")
        HB, BANKS = 2, 4
        UNITS = 2 * KI
        ctx.callback(sp.clear_sems)
        block = ctx.enter_context(nc.Block())

        def experts(eng, body):
            body(0, 0)
            with eng.Fori(0, EXPERTS // 2 - 1) as i:
                for b in (1, 0):
                    body(2 * i + 2 - b, b)
            body(EXPERTS - 1, 1)

        def wait(eng, sem, value):
            if not isinstance(value, int) or value > 0:
                eng.wait_ge(sem, value)

        def is_last(e):
            return isinstance(e, int) and e == EXPERTS - 1

        @block.sync
        def _(sync):
            sync.dma_start(wg[:], w_gate.rearrange("(k p) e -> p k e", p=P)).then_inc(wg_loaded, 16)

            def load(e, b):
                for n, w in enumerate((w1, w3)):
                    sync.dma_start(w_up[b][:, n * KD:(n + 1) * KD, :],
                                   w[bass.ds(e, 1)].rearrange("e (k p) n -> p (e k) n", p=P)).then_inc(loaded[b], 16)
                sync.dma_start(w_dn[b][:], w2[bass.ds(e, 1)].rearrange("e (k p) n -> p (e k) n", p=P)
                               ).then_inc(loaded[b], 16)

            load(0, 0)
            load(1, 1)
            with sync.Fori(0, EXPERTS // 2 - 1) as i:
                for b in range(2):
                    sync.wait_ge(w_lo_done, 2 * i + b + 1)
                    load(2 * i + b + 2, b)

        @block.vector
        def _(dve):
            ln.vector(nc, xres)
            step = 0

            def then(ins):
                nonlocal step
                step += 1
                ins.then_inc(router, 1)
                dve.wait_ge(router, step)

            dve.wait_ge(router_act, 1)
            then(nc.vector.tensor_reduce(row_max[:], prob[:], AX_X, ALU.max))
            then(nc.vector.tensor_tensor(logit[:], prob[:], row_max[:].unsqueeze(2).broadcast_to([P, TT, EXPERTS]), ALU.subtract))
            dve.wait_ge(router_act, 2)
            then(nc.vector.tensor_reduce(row_sum[:], prob[:], AX_X, ALU.add))
            then(nc.vector.reciprocal(row_max[:], row_sum[:]))
            then(nc.vector.tensor_tensor(prob[:], prob[:], row_max[:].unsqueeze(2).broadcast_to([P, TT, EXPERTS]), ALU.mult))
            for t in range(TT):
                nc.vector.max(top[:, t, :], prob[:, t, :]).then_inc(router, 1)
            step += TT
            dve.wait_ge(router, step)
            for t in range(TT):
                nc.vector.max_index(top_at[:, t, :], top[:, t, :], prob[:, t, :]).then_inc(router, 1)
            step += TT
            dve.wait_ge(router, step)
            then(nc.vector.tensor_copy(top_atf[:], top_at[:, :, 0:2]))
            places = iota8.unsqueeze(1).broadcast_to([P, TT, EXPERTS])
            nc.vector.tensor_tensor(chosen[:], top_atf[:, :, 0:1].broadcast_to([P, TT, EXPERTS]), places, ALU.is_equal).then_inc(router, 1)
            nc.vector.tensor_tensor(weight[:], top_atf[:, :, 1:2].broadcast_to([P, TT, EXPERTS]), places, ALU.is_equal).then_inc(router, 1)
            step += 2
            dve.wait_ge(router, step)
            then(nc.vector.tensor_tensor(chosen[:], chosen[:], weight[:], ALU.add))
            then(nc.vector.scalar_tensor_tensor(weight[:], prob[:], 0.5, chosen[:], ALU.mult, ALU.mult))

            def unit(e, u):
                n = UNITS * e + u
                half, m = divmod(u, KI)
                dve.wait_ge(silu_done, n + 1)
                dve.wait_ge(up_done, n + 1)
                nc.vector.tensor_tensor(h[:, u % HB, :], g[:, u % HB, :], up_ps[u % 2][:], ALU.mult).then_inc(h_done, 1)
                dve.wait_ge(h_hi_done, n + 1)
                nc.vector.tensor_tensor(h_lo[:, m, half * BANK:(half + 1) * BANK], h[:, u % HB, :],
                                        f32(h_hi[:, m, half * BANK:(half + 1) * BANK]), ALU.subtract).then_inc(h_lo_done, 1)

            def add_pair(e, q):
                dve.wait_ge(down_done, BANKS * e + q + 1)
                for j in range(2):
                    t = 2 * q + j
                    last = nc.vector.scalar_tensor_tensor(xres[:, t, :], down_ps[q][:, j, :],
                                                          weight[:, t, bass.ds(e, 1)], xres[:, t, :],
                                                          ALU.mult, ALU.add)
                last.then_inc(added, 1)

            def expert(e, b):
                more = not is_last(e)
                for u in range(1, KI + 1):
                    unit(e, u)
                add_pair(e, 0)
                for u in range(KI + 1, UNITS):
                    unit(e, u)
                    if u == KI + 1:
                        add_pair(e, 1)
                if more:
                    unit(e + 1, 0)
                add_pair(e, 2)
                add_pair(e, 3)

            unit(0, 0)
            experts(dve, expert)
            dve.wait_ge(added, BANKS * EXPERTS)

        @block.gpsimd
        def _(pool):
            def split_low(e, b):
                pool.wait_ge(w_hi_done, e + 1)
                nc.gpsimd.tensor_tensor(w_up_lo[b][:], w_up[b][:], f32(w_up_hi[b][:]), ALU.subtract)
                nc.gpsimd.tensor_tensor(w_dn_lo[b][:], w_dn[b][:], f32(w_dn_hi[b][:]), ALU.subtract).then_inc(w_lo_done, 1)

            split_low(0, 0)
            split_low(1, 1)
            with pool.Fori(0, EXPERTS // 2 - 1) as i:
                for b in range(2):
                    split_low(2 * i + b + 2, b)

        @block.scalar
        def _(act):
            ln.scalar(nc)
            act.wait_ge(logits_done, 1)
            nc.scalar.activation(prob[:], down_ps[0][:, 0, 0:TT * EXPERTS].rearrange("p (t e) -> p t e", e=EXPERTS),
                                 ACT.Tanh, scale=1.0 / SOFTCAP).then_inc(router_act, 1)
            act.wait_ge(router, 2)
            nc.scalar.activation(prob[:], logit[:], ACT.Exp, scale=SOFTCAP).then_inc(router_act, 1)

            def split_high(e, b):
                act.wait_ge(loaded[b], 3 * 16 * (e // 2 + 1) if isinstance(e, int) else 24 * (e - b) + 48)
                nc.scalar.copy(w_up_hi[b][:], w_up[b][:])
                nc.scalar.copy(w_dn_hi[b][:], w_dn[b][:]).then_inc(w_hi_done, 1)

            def unit(e, u):
                n = UNITS * e + u
                half, m = divmod(u, KI)
                act.wait_ge(gate_done, n + 1)
                nc.scalar.activation(g[:, u % HB, :], gate_ps[u % 2][:], ACT.Silu).then_inc(silu_done, 1)
                act.wait_ge(h_done, n + 1)
                nc.scalar.copy(h_hi[:, m, half * BANK:(half + 1) * BANK], h[:, u % HB, :]).then_inc(h_hi_done, 1)

            def expert(e, b):
                more = not is_last(e)
                for u in range(1, KI):
                    unit(e, u)
                if more:
                    wait(act, down_done, BANKS * e)
                    split_high(e + 1, 1 - b)
                for u in range(KI, UNITS):
                    if u == KI:
                        wait(act, down_done, BANKS * e)
                    unit(e, u)
                if more:
                    act.wait_ge(down_done, BANKS * e + 2)
                    unit(e + 1, 0)

            split_high(0, 0)
            unit(0, 0)
            experts(act, expert)

        @block.tensor
        def _(pe):
            ln.tensor(nc, ident)
            ln.ready(pe)
            pe.wait_ge(wg_loaded, 16)
            for t in range(TT):
                for k in range(KD):
                    last = nc.tensor.matmul(down_ps[0][:, 0, t * EXPERTS:(t + 1) * EXPERTS],
                                            ln.xnT[:, k, t * P:(t + 1) * P], wg[:, k, :],
                                            start=(k == 0), stop=(k == KD - 1))
            last.then_inc(logits_done, 1)

            def ups(e, b, u):
                n = UNITS * e + u
                half, m = divmod(u, KI)
                if u >= 2:
                    pe.wait_ge(silu_done, n - 1)
                    pe.wait_ge(h_done, n - 1)
                else:
                    wait(pe, silu_done, UNITS * e)
                    wait(pe, h_done, UNITS * e)
                for n_w, (bank, done) in enumerate(((gate_ps[u % 2], gate_done), (up_ps[u % 2], up_done))):
                    for k in range(KD):
                        w = n_w * KD + k, slice(m * P, (m + 1) * P)
                        last = matmul3(nc, bank[:], (w_up_hi[b][:, w[0], w[1]], w_up_lo[b][:, w[0], w[1]]),
                                       ln.parts(k, slice(half * BANK, (half + 1) * BANK)),
                                       start=(k == 0), stop=(k == KD - 1))
                    last.then_inc(done, 1)

            def down(e, b, half):
                pe.wait_ge(h_lo_done, UNITS * e + KI * (half + 1))
                for q in range(2 * half, 2 * half + 2):
                    wait(pe, added, BANKS * e)
                    for j in range(2):
                        cols = slice((2 * q + j) * P, (2 * q + j + 1) * P)
                        for k in range(KI):
                            last = matmul3(nc, down_ps[q][:, j, :], (h_hi[:, k, cols], h_lo[:, k, cols]),
                                           (w_dn_hi[b][:, k, :], w_dn_lo[b][:, k, :]),
                                           start=(k == 0), stop=(k == KI - 1))
                    last.then_inc(down_done, 1)

            def expert(e, b):
                more = not is_last(e)
                for u in range(1, KI + 1):
                    ups(e, b, u)
                down(e, b, 0)
                for u in range(KI + 1, UNITS):
                    ups(e, b, u)
                if more:
                    pe.wait_ge(w_lo_done, e + 2)
                    ups(e + 1, 1 - b, 0)
                down(e, b, 1)

            pe.wait_ge(w_lo_done, 1)
            ups(0, 0, 0)
            experts(pe, expert)


HEADS = 32
KV = 8
GQ = HEADS // KV
HD = D // HEADS
ROT = HD // 2
QKW = (HEADS + KV) * HD
QKVW = QKW + KV * HD
STACK = 32
NEG_HI, NEG_LO = 3 * HD, 3 * HD + 1
SCALE = HD ** -0.5
KT_TILES = S // P
SLOTS = 2 * KT_TILES
CHUNKS = GQ * TT * 2
PER_SLOT = 5


def attention_layer(nc, xres, ident, cos_t, sin_t, w_qkv, w_o, tag):
    with ExitStack() as ctx:
        sp = Space(nc, ctx, tag)
        cos = sp.sb("cos", [P, TT, ROT])
        sin = sp.sb("sin", [P, TT, ROT])
        w_raw = sp.sb("w_qkv", [P, KD, QKVW])
        w_hi = sp.sb("w_qkv_hi", [P, KD, QKVW], F32R)
        w_lo = sp.sb("w_qkv_lo", [P, KD, QKVW], F32R)
        wo_raw = sp.sb("w_o", [P, KD, D])
        wo_hi = sp.sb("w_o_hi", [P, KD, D], F32R)
        wo_lo = sp.sb("w_o_lo", [P, KD, D], F32R)
        qk_cos = [sp.sb(f"qk_cos{b}", [P, QKW]) for b in range(2)]
        qk_sin = [sp.sb(f"qk_sin{b}", [P, QKW]) for b in range(2)]
        roped = sp.sb("roped", [P, TT, QKW])
        q_stack = sp.sb("q_stack", [P, TT, KV, GQ * STACK])
        k_stack = sp.sb("k_stack", [P, TT, KV * STACK])
        kT = sp.sb("kT", [P, 2, S], F32R)
        kz = [sp.sb(f"k_picks{b}", [P, GQ, S], F32R) for b in range(2)]
        v_all = sp.sb("v_all", [P, TT, KV, STACK])
        vg = [sp.sb(f"v_group{b}", [P, TT, STACK]) for b in range(2)]
        qg = [sp.sb(f"q_group{b}", [P, TT, GQ * STACK]) for b in range(2)]
        qm = sp.sb("qT_pass1", [P, S], F32R)
        qe = [sp.sb(f"qT_pass2_{b}", [P, S], F32R) for b in range(2)]
        rmax2 = sp.sb("max_halves", [P, TT, GQ, 2])
        rmax = sp.sb("max", [P, TT, GQ])
        probs = [sp.sb(f"probs{b}", [P, GQ, BANK]) for b in range(2)]
        oT = sp.sb("oT", [P, BANK])
        recip = sp.sb("recip", [P, 4, GQ])

        st_ps = [sp.ps(f"scoresT{b}", [P, 2, BANK]) for b in range(2)]
        mx_ps = [sp.ps(f"scores{b}", [P, BANK]) for b in range(2)]
        o_ps = sp.ps("o", [P, BANK])
        turn_ps = sp.ps("turn", [P, 4, P])
        ln = LayerNorm(sp, mx_ps, keep_f32=False)
        o_tok, oT_hi, oT_lo = ln.xn, ln.hi, ln.lo

        w_in, wo_in, tab_in = sp.sem("w_in"), sp.sem("wo_in"), sp.sem("tab_in")
        zeroed = sp.sem("zeroed")
        wh, wl = sp.sem("w_hi_done"), sp.sem("w_lo_done")
        qkv_done, rope_step, roped_done = sp.sem("qkv_done"), sp.sem("rope_step"), sp.sem("roped_done")
        v_done, stack_hi, stack_lo = sp.sem("v_done"), sp.sem("stack_hi"), sp.sem("stack_lo")
        k_turned, kT_done = sp.sem("k_turned"), sp.sem("kT_done")
        kz_in = [sp.sem(f"kz_in{b}") for b in range(2)]
        qg_in, vg_in = sp.sem("q_group_in"), sp.sem("v_group_in")
        q1_turned, q1_done = sp.sem("q1_turned"), sp.sem("q1_done")
        q2_turned, q2_done = sp.sem("q2_turned"), sp.sem("q2_done")
        scores_done, reduced, maxed, negated = (sp.sem(n) for n in ("scores_done", "reduced", "maxed", "negated"))
        scoresT_done, exp_done, pv_done = sp.sem("scoresT_done"), sp.sem("exp_done"), sp.sem("pv_done")
        o_copied, o_turned, o_step, o_norm = (sp.sem(n) for n in ("o_copied", "o_turned", "o_step", "o_norm"))
        f_turned, f_hi, f_lo, f_done = (sp.sem(n) for n in ("f_turned", "f_hi", "f_lo", "f_done"))
        fin = sp.sem("added")
        ctx.callback(sp.clear_sems)
        block = ctx.enter_context(nc.Block())

        def groups(eng, body):
            body(0, 0)
            with eng.Fori(0, KV // 2 - 1) as i:
                for b in (1, 0):
                    body(2 * i + 2 - b, b)
            body(KV - 1, 1)

        def edge(g):
            return (isinstance(g, int) and g == 0), (isinstance(g, int) and g == KV - 1)

        def chunks(s):
            lo, hi = min(CHUNKS, max(0, PER_SLOT * (s - 1))), min(CHUNKS, max(0, PER_SLOT * s))
            return [(n, n // (2 * TT), n // 2 % TT, n % 2) for n in range(lo, hi)]

        @block.sync
        def _(sync):
            sync.dma_start(w_raw[:], w_qkv.rearrange("(k p) n -> p k n", p=P)).then_inc(w_in, 16)
            sync.dma_start(cos[:], cos_t.rearrange("(t p) r -> p t r", p=P)).then_inc(tab_in, 16)
            sync.dma_start(sin[:], sin_t.rearrange("(t p) r -> p t r", p=P)).then_inc(tab_in, 16)
            sync.dma_start(wo_raw[:], w_o.rearrange("(k p) n -> p k n", p=P)).then_inc(wo_in, 16)
            sync.wait_ge(kT_done, 4)
            sync.wait_ge(zeroed, 5)
            for g in range(KV):
                if g >= 2:
                    sync.wait_ge(scoresT_done, 2 * SLOTS * (g - 1))
                for j in range(GQ):
                    src = (g % 4) * STACK
                    sync.dma_start(f32(kz[g % 2][j * STACK:(j + 1) * STACK, j, :]),
                                   f32(kT[src:src + STACK, g // 4, :])).then_inc(kz_in[g % 2], 16)

        @block.gpsimd
        def _(pool):
            for n, t in enumerate((k_stack, v_all, q_stack, kz[0], kz[1])):
                view = t[:].bitcast(F32) if n >= 3 else t[:]
                nc.gpsimd.memset(view, 0.0).then_inc(zeroed, 1)
            for n, (hi, lo, raw) in enumerate(((w_hi, w_lo, w_raw), (wo_hi, wo_lo, wo_raw))):
                pool.wait_ge(wh, n + 1)
                nc.gpsimd.tensor_tensor(lo[:], raw[:], f32(hi[:]), ALU.subtract).then_inc(wl, 1)
            pool.wait_ge(zeroed, 2)
            ks = k_stack[:].rearrange("p t (h r) -> p (t h) r", r=STACK)
            nc.gpsimd.memset(ks[:, :, NEG_HI:NEG_LO + 1], 1.0).then_inc(zeroed, 1)
            nc.gpsimd.memset(v_all[:, :, :, HD], 1.0).then_inc(zeroed, 1)

            def copy_q(g, b):
                pool.wait_ge(stack_lo, 2)
                nc.gpsimd.tensor_copy(qg[b][:].unsqueeze(2), q_stack[:, :, bass.ds(g, 1), :]).then_inc(qg_in, 1)

            def copy_v(g, b):
                pool.wait_ge(v_done, TT)
                nc.gpsimd.tensor_copy(vg[b][:].unsqueeze(2), v_all[:, :, bass.ds(g, 1), :]).then_inc(vg_in, 1)

            pool.wait_ge(stack_lo, 2)
            pool.wait_ge(stack_hi, 4)
            pool.wait_ge(v_done, TT)
            for g in range(2):
                copy_q(g, g)
                copy_v(g, g)
            with pool.Fori(0, KV // 2 - 1) as i:
                for b in range(2):
                    pool.wait_ge(q2_turned, 2 * (2 * i + b + 1))
                    copy_q(2 * i + b + 2, b)
                    pool.wait_ge(pv_done, SLOTS * (2 * i + b + 1))
                    copy_v(2 * i + b + 2, b)

        @block.vector
        def _(dve):
            ln.vector(nc, xres)
            dve.wait_ge(tab_in, 32)
            for t in range(TT):
                b = t % 2
                x = st_ps[b][:, 0, 0:QKW].rearrange("p (h s r) -> p h s r", s=2, r=ROT)
                c = cos[:, t, :].unsqueeze(1).unsqueeze(1).broadcast_to([P, HEADS + KV, 2, ROT])
                s1 = sin[:, t, :].unsqueeze(1).broadcast_to([P, HEADS + KV, ROT])
                xs = qk_sin[b][:].rearrange("p (h s r) -> p h s r", s=2, r=ROT)
                dve.wait_ge(qkv_done, t + 1)
                dve.wait_ge(v_done, t + 1)
                nc.vector.tensor_tensor(qk_cos[b][:].rearrange("p (h s r) -> p h s r", s=2, r=ROT), x, c, ALU.mult)
                nc.vector.scalar_tensor_tensor(xs[:, :, 0, :], x[:, :, 1, :], -1.0, s1, ALU.mult, ALU.mult)
                nc.vector.tensor_tensor(xs[:, :, 1, :], x[:, :, 0, :], s1, ALU.mult).then_inc(rope_step, 1)
                dve.wait_ge(rope_step, t + 1)
                nc.vector.tensor_tensor(roped[:, t, :], qk_cos[b][:], qk_sin[b][:], ALU.add).then_inc(roped_done, 1)
            ks = k_stack[:].rearrange("p t (h r) -> p t h r", r=STACK)
            qs = q_stack[:].rearrange("p t g (j r) -> p t (g j) r", r=STACK)
            kr = roped[:, :, HEADS * HD:].rearrange("p t (h r) -> p t h r", r=HD)
            qr = roped[:, :, 0:HEADS * HD].rearrange("p t (h r) -> p t h r", r=HD)
            dve.wait_ge(stack_hi, 1)
            nc.vector.tensor_tensor(ks[:, :, :, 2 * HD:3 * HD], kr, ks[:, :, :, 0:HD], ALU.subtract).then_inc(stack_lo, 1)
            dve.wait_ge(stack_hi, 3)
            nc.vector.tensor_tensor(qs[:, :, :, HD:2 * HD], qr, qs[:, :, :, 0:HD], ALU.subtract).then_inc(stack_lo, 1)

            def reduce(g, n, j, t, c):
                dve.wait_ge(scores_done, CHUNKS * g + n + 1)
                return nc.vector.tensor_reduce(rmax2[:, t, j, c:c + 1], mx_ps[n % 2][:], AX_X, ALU.max).then_inc(reduced, 1)

            def negate(g, b):
                dve.wait_ge(reduced, CHUNKS * (g + 1))
                nc.vector.tensor_tensor(rmax[:], rmax2[:, :, :, 0], rmax2[:, :, :, 1], ALU.max).then_inc(maxed, 1)
                stack = qg[b][:].rearrange("p t (j r) -> p t j r", r=STACK)
                dve.wait_ge(maxed, 2 * g + 1)
                dve.wait_ge(q1_turned, 2 * (g + 1))
                nc.vector.tensor_scalar(stack[:, :, :, NEG_HI].bitcast(F32R), rmax[:], -1.0, None, ALU.mult).then_inc(maxed, 1)
                dve.wait_ge(maxed, 2 * g + 2)
                nc.vector.scalar_tensor_tensor(stack[:, :, :, NEG_LO], rmax[:], -1.0, stack[:, :, :, NEG_HI],
                                               ALU.mult, ALU.subtract).then_inc(negated, 1)

            def copy_o(g, half):
                dve.wait_ge(pv_done, SLOTS * g + KT_TILES * (half + 1))
                dve.wait_ge(o_turned, 2 * g + half)
                nc.vector.tensor_copy(oT[:], o_ps[:]).then_inc(o_copied, 1)

            def normalize(g, half):
                rows = turn_ps[:].rearrange("p t (j r) -> p t j r", r=STACK)
                dve.wait_ge(o_turned, 2 * g + half + 1)
                nc.vector.reciprocal(recip[:], rows[:, :, :, HD]).then_inc(o_step, 1)
                dve.wait_ge(o_step, 2 * g + half + 1)
                for t in range(4):
                    out = o_tok[:, 4 * half + t, bass.ds(g * GQ * HD, GQ * HD)].rearrange("p (j r) -> p j r", r=HD)
                    last = nc.vector.tensor_tensor(out, rows[:, t, :, 0:HD],
                                                   recip[:, t, :].unsqueeze(2).broadcast_to([P, GQ, HD]), ALU.mult)
                last.then_inc(o_norm, 1)

            def body(g, b):
                first, last = edge(g)
                if not first:
                    copy_o(g - 1, 1)
                for s in range(SLOTS):
                    if not last:
                        for n, j, t, c in chunks(s):
                            reduce(g + 1, n, j, t, c)
                    if s == 2 and not first:
                        normalize(g - 1, 1)
                    if s == KT_TILES:
                        copy_o(g, 0)
                    if s == KT_TILES + 2:
                        normalize(g, 0)
                    if s == SLOTS - 2 and not last:
                        negate(g + 1, 1 - b)

            for n in range(CHUNKS):
                reduce(0, n, n // (2 * TT), n // 2 % TT, n % 2)
            negate(0, 0)
            groups(dve, body)
            copy_o(KV - 1, 1)
            normalize(KV - 1, 1)
            for q in range(4):
                dve.wait_ge(f_hi, q + 1)
                cols = slice(2 * P * q, 2 * P * (q + 1))
                nc.vector.tensor_tensor(oT_lo[:, :, cols], mx_ps[q % 2][:].rearrange("p (k n) -> p k n", k=KD),
                                        f32(oT_hi[:, :, cols]), ALU.subtract).then_inc(f_lo, 1)
            for t in range(TT):
                dve.wait_ge(f_done, t + 1)
                nc.vector.tensor_tensor(xres[:, t, :], st_ps[t % 2][:, 0, 0:D], xres[:, t, :], ALU.add).then_inc(fin, 1)
            dve.wait_ge(fin, TT)

        @block.scalar
        def _(act):
            act.wait_ge(w_in, 16)
            nc.scalar.copy(w_hi[:], w_raw[:]).then_inc(wh, 1)
            act.wait_ge(wo_in, 16)
            nc.scalar.copy(wo_hi[:], wo_raw[:]).then_inc(wh, 1)
            ln.scalar(nc)
            act.wait_ge(zeroed, 7)
            for t in range(TT):
                act.wait_ge(qkv_done, t + 1)
                nc.scalar.copy(v_all[:, t, :, 0:HD], st_ps[t % 2][:, 0, QKW:QKVW].rearrange("p (h r) -> p h r", r=HD)
                               ).then_inc(v_done, 1)
            ks = k_stack[:].rearrange("p t (h r) -> p t h r", r=STACK)
            qs = q_stack[:].rearrange("p t g (j r) -> p t (g j) r", r=STACK)
            kr = roped[:, :, HEADS * HD:].rearrange("p t (h r) -> p t h r", r=HD)
            qr = roped[:, :, 0:HEADS * HD].rearrange("p t (h r) -> p t h r", r=HD)
            act.wait_ge(roped_done, TT)
            nc.scalar.copy(ks[:, :, :, 0:HD].bitcast(F32R), kr).then_inc(stack_hi, 1)
            nc.scalar.copy(ks[:, :, :, HD:2 * HD].bitcast(F32R), kr).then_inc(stack_hi, 1)
            nc.scalar.copy(qs[:, :, :, 0:HD].bitcast(F32R), qr).then_inc(stack_hi, 1)
            nc.scalar.copy(qs[:, :, :, 2 * HD:3 * HD].bitcast(F32R), qr).then_inc(stack_hi, 1)
            for n in range(4):
                act.wait_ge(k_turned, n + 1)
                cols = slice(2 * P * n, 2 * P * (n + 1))
                nc.scalar.copy(kT[:, :, cols], mx_ps[n % 2][:].rearrange("p (a n) -> p a n", a=2)).then_inc(kT_done, 1)

            def turned_for_pass1(g):
                for half in range(2):
                    act.wait_ge(q1_turned, 2 * g + half + 1)
                    act.wait_ge(scores_done, CHUNKS * g)
                    nc.scalar.copy(qm[:, half * BANK:(half + 1) * BANK], turn_ps[:].rearrange("p t n -> p (t n)")).then_inc(q1_done, 1)

            def turned_for_pass2(g, b):
                for half in range(2):
                    act.wait_ge(q2_turned, 2 * g + half + 1)
                    nc.scalar.copy(qe[b][:, half * BANK:(half + 1) * BANK], turn_ps[:].rearrange("p t n -> p (t n)")).then_inc(q2_done, 1)

            def exp_pair(g, s, pair):
                n = SLOTS * g + s
                act.wait_ge(scoresT_done, 2 * n + pair + 1)
                if not (isinstance(n, int) and n < 2):
                    act.wait_ge(pv_done, n - 1)
                nc.scalar.activation(probs[s % 2][:, 2 * pair:2 * pair + 2, :], st_ps[pair][:], ACT.Exp,
                                     scale=SCALE).then_inc(exp_done, 1)

            def body(g, b):
                first, last = edge(g)
                for s in range(SLOTS):
                    for pair in range(2):
                        exp_pair(g, s, pair)
                    if s == SLOTS - 2 and not (last or (isinstance(g, int) and g == KV - 2)):
                        turned_for_pass1(g + 2)
                    if s == SLOTS - 1 and not last:
                        turned_for_pass2(g + 1, 1 - b)

            turned_for_pass1(0)
            turned_for_pass2(0, 0)
            turned_for_pass1(1)
            body(0, 0)
            with act.Fori(0, KV // 2 - 2) as i:
                for b in (1, 0):
                    body(2 * i + 2 - b, b)
            for g in range(KV - 3, KV):
                body(g, g % 2)
            for q in range(4):
                act.wait_ge(f_turned, q + 1)
                cols = slice(2 * P * q, 2 * P * (q + 1))
                nc.scalar.copy(oT_hi[:, :, cols], mx_ps[q % 2][:].rearrange("p (k n) -> p k n", k=KD)).then_inc(f_hi, 1)

        @block.tensor
        def _(pe):
            ln.tensor(nc, ident)
            ln.ready(pe)
            pe.wait_ge(wl, 1)
            for t in range(TT):
                if t >= 2:
                    pe.wait_ge(rope_step, t - 1)
                for k in range(KD):
                    last = matmul3(nc, st_ps[t % 2][:, 0, 0:QKVW], ln.parts(k, slice(t * P, (t + 1) * P)),
                                   (w_hi[:, k, :], w_lo[:, k, :]), start=(k == 0), stop=(k == KD - 1))
                last.then_inc(qkv_done, 1)
            pe.wait_ge(stack_lo, 1)
            pe.wait_ge(stack_hi, 2)
            for n in range(4):
                if n >= 2:
                    pe.wait_ge(kT_done, n - 1)
                for a in range(2):
                    for t in range(2):
                        last = nc.tensor.transpose(mx_ps[n % 2][:, (2 * a + t) * P:(2 * a + t + 1) * P],
                                                   k_stack[:, 2 * n + t, a * P:(a + 1) * P], ident)
                last.then_inc(k_turned, 1)

            def turn_q(g, b, half, done, free):
                free()
                for t in range(4):
                    last = nc.tensor.transpose(turn_ps[:, t, :], qg[b][:, 4 * half + t, :], ident)
                last.then_inc(done, 1)

            def pass1_stack(g, b):
                pe.wait_ge(qg_in, g + 1)
                turn_q(g, b, 0, q1_turned, lambda: None)
                turn_q(g, b, 1, q1_turned, lambda: pe.wait_ge(q1_done, 2 * g + 1))

            def pass2_stack(g, b):
                pe.wait_ge(negated, g + 1)
                turn_q(g, b, 0, q2_turned, lambda: None)
                turn_q(g, b, 1, q2_turned, lambda: pe.wait_ge(q2_done, 2 * g + 1))

            def kz_ready(g, b):
                pe.wait_ge(kz_in[b], 16 * GQ + 8 * GQ * (g - b))

            def score_chunk(g, b, n, j, t, c):
                m = CHUNKS * g + n
                if not (isinstance(m, int) and m < 2):
                    pe.wait_ge(reduced, m - 1)
                nc.tensor.matmul(mx_ps[n % 2][:], qm[:, t * P:(t + 1) * P], kz[b][:, j, c * BANK:(c + 1) * BANK],
                                 start=True, stop=True).then_inc(scores_done, 1)

            def scoresT(g, b, s, pair):
                half, kt = divmod(s, KT_TILES)
                n = SLOTS * g + s
                if not (isinstance(n, int) and n == 0):
                    pe.wait_ge(exp_done, 2 * n - 1 + pair)
                for j in (2 * pair, 2 * pair + 1):
                    last = nc.tensor.matmul(st_ps[pair][:, j % 2, :], kz[b][:, j, kt * P:(kt + 1) * P],
                                            qe[b][:, half * BANK:(half + 1) * BANK], start=True, stop=True)
                last.then_inc(scoresT_done, 1)

            def values(g, b, s):
                half, kt = divmod(s, KT_TILES)
                pe.wait_ge(exp_done, 2 * (SLOTS * g + s) + 2)
                if s == 0:
                    pe.wait_ge(vg_in, g + 1)
                if kt == 0:
                    pe.wait_ge(o_copied, 2 * g + half)
                for j in range(GQ):
                    last = nc.tensor.matmul(o_ps[j * STACK:(j + 1) * STACK, :], vg[b][:, kt, :], probs[s % 2][:, j, :],
                                            start=(kt == 0), stop=(kt == KT_TILES - 1))
                last.then_inc(pv_done, 1)

            def turn_o(g, half):
                pe.wait_ge(o_copied, 2 * g + half + 1)
                for t in range(4):
                    last = nc.tensor.transpose(turn_ps[:, t, :], oT[:, t * P:(t + 1) * P], ident)
                last.then_inc(o_turned, 1)

            def body(g, b):
                first, last = edge(g)
                before_last = isinstance(g, int) and g == KV - 2
                pe.wait_ge(q2_done, 2 * (g + 1))
                for s in range(SLOTS):
                    todo = [] if last else chunks(s)

                    def some(count):
                        for n, j, t, c in todo[:count]:
                            score_chunk(g + 1, 1 - b, n, j, t, c)
                        del todo[:count]

                    if s == 1 and not last:
                        kz_ready(g + 1, 1 - b)
                        pe.wait_ge(q1_done, 2 * (g + 2))
                    some(1)
                    scoresT(g, b, s, 0)
                    some(1)
                    scoresT(g, b, s, 1)
                    some(1)
                    if s > 0:
                        values(g, b, s - 1)
                    some(PER_SLOT)
                    if s == 1 and not first:
                        turn_o(g - 1, 1)
                    if s == KT_TILES + 1:
                        turn_o(g, 0)
                    if s == SLOTS - 2 and not last and not before_last:
                        pe.wait_ge(o_norm, 2 * g + 1)
                        pass1_stack(g + 2, b)
                pe.wait_ge(o_norm, 2 * g + 1)
                if not last:
                    if not before_last:
                        pe.wait_ge(q1_done, 2 * (g + 3))
                    pass2_stack(g + 1, 1 - b)
                values(g, b, SLOTS - 1)

            pe.wait_ge(kT_done, 4)
            pass1_stack(0, 0)
            kz_ready(0, 0)
            pe.wait_ge(q1_done, 2)
            for n in range(CHUNKS):
                score_chunk(0, 0, n, n // (2 * TT), n // 2 % TT, n % 2)
            pass2_stack(0, 0)
            pe.wait_ge(q2_done, 2)
            pass1_stack(1, 1)
            body(0, 0)
            with pe.Fori(0, KV // 2 - 2) as i:
                for b in (1, 0):
                    body(2 * i + 2 - b, b)
            for g in range(KV - 3, KV):
                body(g, g % 2)
            turn_o(KV - 1, 1)
            pe.wait_ge(o_norm, 2 * KV)
            for q in range(4):
                if q >= 2:
                    pe.wait_ge(f_lo, q - 1)
                for k in range(KD):
                    for t in range(2):
                        last = nc.tensor.transpose(mx_ps[q % 2][:, (2 * k + t) * P:(2 * k + t + 1) * P],
                                                   o_tok[:, 2 * q + t, k * P:(k + 1) * P], ident)
                last.then_inc(f_turned, 1)
            pe.wait_ge(wl, 2)
            for t in range(TT):
                pe.wait_ge(f_lo, t // 2 + 1)
                if t >= 2:
                    pe.wait_ge(fin, t - 1)
                cols = slice(t * P, (t + 1) * P)
                for k in range(KD):
                    last = matmul3(nc, st_ps[t % 2][:, 0, 0:D], (oT_hi[:, k, cols], oT_lo[:, k, cols]),
                                   (wo_hi[:, k, :], wo_lo[:, k, :]), start=(k == 0), stop=(k == KD - 1))
                last.then_inc(f_done, 1)


FFN = 1024
KF = FFN // P
QUAD = FFN // 4


def sparse_ffn_layer(nc, xres, ident, w_gate, w_up, w_down, tag):
    with ExitStack() as ctx:
        sp = Space(nc, ctx, tag)
        stats = sp.sb("stats", [P, TT, 6])
        mv = sp.sb("mean_var", [P, TT, 2])
        std = sp.sb("std", [P, TT])
        rstd = sp.sb("rstd", [P, TT])
        eps = sp.sb("eps", [P, 1])
        xn = [sp.sb(f"xn{b}", [P, D]) for b in range(2)]
        xT_hi = [sp.sb(f"xT_hi{b}", [P, KD, P], F32R) for b in range(2)]
        xT_lo = [sp.sb(f"xT_lo{b}", [P, KD, P], F32R) for b in range(2)]
        w_names = ("gate", "up", "down")
        w_shape = {"gate": (KD, FFN), "up": (KD, FFN), "down": (KF, D)}
        w_src = {"gate": w_gate, "up": w_up, "down": w_down}
        w_raw = {n: sp.sb(f"w_{n}", [P, *w_shape[n]]) for n in w_names}
        w_hi = {n: sp.sb(f"w_{n}_hi", [P, *w_shape[n]], F32R) for n in w_names}
        w_lo = {n: sp.sb(f"w_{n}_lo", [P, *w_shape[n]], F32R) for n in w_names}
        g = [sp.sb(f"silu{c}", [P, BANK]) for c in range(2)]
        h = [sp.sb(f"h{b}", [P, FFN]) for b in range(2)]
        mag = sp.sb("magnitude", [P, FFN])
        c02_13 = sp.sb("c02_13", [P, 2, QUAD], BF16)
        c03_12 = sp.sb("c03_12", [P, 2, QUAD], BF16)
        c01_23 = sp.sb("c01_23", [P, 2, QUAD], BF16)
        wins = sp.sb("wins", [P, 2, QUAD], BF16)
        losses = sp.sb("losses", [P, 2, QUAD], BF16)
        score = sp.sb("score", [P, 4, QUAD], BF16)
        hT_hi = sp.sb("hT_hi", [P, KF, P], F32R)
        hT_lo = sp.sb("hT_lo", [P, KF, P], F32R)
        gate_ps = [sp.ps(f"gate{c}", [P, BANK]) for c in range(2)]
        up_ps = [sp.ps(f"up{c}", [P, BANK]) for c in range(2)]
        hT_ps = [sp.ps(f"hT{c}", [P, 4, P]) for c in range(2)]
        xT_ps = sp.ps("xT", [P, KD, P])
        out_ps = sp.ps("out", [P, D])

        loaded = {n: sp.sem(f"{n}_loaded") for n in w_names}
        w_hi_done, w_lo_done = sp.sem("w_hi_done"), sp.sem("w_lo_done")
        stats_done, mv_done, std_done, rstd_done = (sp.sem(n) for n in ("stats_done", "mv_done", "std_done", "rstd_done"))
        xn_done, x_turned, x_hi_done, x_lo_done = (sp.sem(n) for n in ("xn_done", "x_turned", "x_hi_done", "x_lo_done"))
        gate_done, up_done, silu_done, h_done = (sp.sem(n) for n in ("gate_done", "up_done", "silu_done", "h_done"))
        mag_done, sparse, steps = sp.sem("mag_done"), sp.sem("sparse"), sp.sem("sparsify_steps")
        h_turned, hT_hi_done, hT_lo_done = (sp.sem(n) for n in ("h_turned", "hT_hi_done", "hT_lo_done"))
        out_done, added = sp.sem("out_done"), sp.sem("added")
        ctx.callback(sp.clear_sems)
        block = ctx.enter_context(nc.Block())

        def tiles(eng, body):
            body(0, 0)
            with eng.Fori(0, TT // 2 - 1) as i:
                for b in (1, 0):
                    body(2 * i + 2 - b, b)
            body(TT - 1, 1)

        def static(t):
            return isinstance(t, int)

        @block.sync
        def _(sync):
            for n in w_names:
                sync.dma_start(w_raw[n][:], w_src[n].rearrange("(k p) n -> p k n", p=P)).then_inc(loaded[n], 16)

        @block.gpsimd
        def _(pool):
            for i, n in enumerate(w_names):
                pool.wait_ge(w_hi_done, i + 1)
                nc.gpsimd.tensor_tensor(w_lo[n][:], w_raw[n][:], f32(w_hi[n][:]), ALU.subtract).then_inc(w_lo_done, 1)

        @block.vector
        def _(dve):
            nc.vector.memset(eps[:], LN_EPS).then_inc(stats_done, 1)
            for t in range(TT):
                nc.vector.bn_stats(stats[:, t, :], xres[:, t, :]).then_inc(stats_done, 1)
            dve.wait_ge(stats_done, TT + 1)
            for t in range(TT):
                nc.vector.bn_aggr(mv[:, t, :], stats[:, t, :]).then_inc(mv_done, 1)
            dve.wait_ge(std_done, 1)
            nc.vector.reciprocal(rstd[:], std[:]).then_inc(rstd_done, 1)
            dve.wait_ge(rstd_done, 1)

            def normalize(t, b):
                if not static(t) or t >= 2:
                    dve.wait_ge(x_turned, t - 1)
                nc.vector.tensor_scalar(xn[b][:].unsqueeze(1), xres[:, bass.ds(t, 1), :], mv[:, bass.ds(t, 1), 0],
                                        rstd[:, bass.ds(t, 1)], ALU.subtract, ALU.mult).then_inc(xn_done, 1)

            def x_low(t, b):
                dve.wait_ge(x_hi_done, t + 1)
                nc.vector.tensor_tensor(xT_lo[b][:], xT_ps[:], f32(xT_hi[b][:]), ALU.subtract).then_inc(x_lo_done, 1)

            def product(t, b, c):
                dve.wait_ge(silu_done, 2 * t + c + 1)
                dve.wait_ge(up_done, 2 * t + c + 1)
                if c == 0 and (not static(t) or t >= 2):
                    dve.wait_ge(h_turned, 2 * (t - 1))
                nc.vector.tensor_tensor(h[b][:, c * BANK:(c + 1) * BANK], g[c][:], up_ps[c][:], ALU.mult).then_inc(h_done, 1)

            def turned_low(t):
                for c in range(2):
                    dve.wait_ge(hT_hi_done, 2 * t + c + 1)
                    nc.vector.tensor_tensor(hT_lo[:, 4 * c:4 * c + 4, :], hT_ps[c][:],
                                            f32(hT_hi[:, 4 * c:4 * c + 4, :]), ALU.subtract).then_inc(hT_lo_done, 1)

            def sparsify(t, b):
                a = mag[:].rearrange("p (q w) -> p w q", w=4)
                hq = h[b][:].rearrange("p (q w) -> p w q", w=4)
                dve.wait_ge(mag_done, t + 1)
                nc.vector.tensor_tensor(c02_13[:], a[:, 0:2], a[:, 2:4], ALU.is_ge)
                nc.vector.tensor_tensor(c03_12[:, 0], a[:, 0], a[:, 3], ALU.is_ge)
                nc.vector.tensor_tensor(c03_12[:, 1], a[:, 1], a[:, 2], ALU.is_ge)
                nc.vector.tensor_tensor(c01_23[:], a[:, 0:4:2], a[:, 1:4:2], ALU.is_ge).then_inc(steps, 1)
                dve.wait_ge(steps, 3 * t + 1)
                nc.vector.tensor_tensor(wins[:], c02_13[:], c03_12[:], ALU.add)
                nc.vector.tensor_tensor(losses[:, 0], c02_13[:, 0], c03_12[:, 1], ALU.add)
                nc.vector.tensor_tensor(losses[:, 1], c03_12[:, 0], c02_13[:, 1], ALU.add).then_inc(steps, 1)
                dve.wait_ge(steps, 3 * t + 2)
                nc.vector.tensor_tensor(score[:, 0], wins[:, 0], c01_23[:, 0], ALU.add)
                nc.vector.tensor_tensor(score[:, 1], wins[:, 1], c01_23[:, 0], ALU.subtract)
                nc.vector.tensor_tensor(score[:, 2], losses[:, 0], c01_23[:, 1], ALU.subtract)
                nc.vector.tensor_tensor(score[:, 3], losses[:, 1], c01_23[:, 1], ALU.add).then_inc(steps, 1)
                dve.wait_ge(steps, 3 * t + 3)
                for w, (op, bound) in enumerate(((ALU.is_ge, 2.0), (ALU.is_ge, 1.0), (ALU.is_le, 0.0), (ALU.is_le, 1.0))):
                    last = nc.vector.scalar_tensor_tensor(hq[:, w], score[:, w], bound, hq[:, w], op, ALU.mult)
                last.then_inc(sparse, 1)

            def add(t):
                dve.wait_ge(out_done, t + 1)
                nc.vector.scalar_tensor_tensor(xres[:, bass.ds(t, 1), :], out_ps[:].unsqueeze(1), 0.5,
                                               xres[:, bass.ds(t, 1), :], ALU.mult, ALU.add).then_inc(added, 1)

            def body(t, b):
                first, last = static(t) and t == 0, static(t) and t == TT - 1
                product(t, b, 0)
                if not first:
                    turned_low(t - 1)
                product(t, b, 1)
                if not last:
                    x_low(t + 1, 1 - b)
                sparsify(t, b)
                if not first:
                    add(t - 1)
                if not last:
                    pass

            normalize(0, 0)
            normalize(1, 1)
            x_low(0, 0)
            body(0, 0)
            normalize(2, 0)
            with dve.Fori(0, TT // 2 - 2) as i:
                for b in (1, 0):
                    body(2 * i + 2 - b, b)
                    normalize(2 * i + 4 - b, b)
            for t in range(TT - 3, TT):
                body(t, t % 2)
                if t + 2 < TT:
                    normalize(t + 2, t % 2)
            turned_low(TT - 1)
            add(TT - 1)
            dve.wait_ge(added, TT)

        @block.scalar
        def _(act):
            for n in w_names[:1]:
                act.wait_ge(loaded[n], 16)
                nc.scalar.copy(w_hi[n][:], w_raw[n][:]).then_inc(w_hi_done, 1)
            act.wait_ge(mv_done, TT)
            nc.scalar.activation(std[:], mv[:, :, 1], ACT.Sqrt, bias=eps[:]).then_inc(std_done, 1)

            def x_high(t, b):
                act.wait_ge(x_turned, t + 1)
                nc.scalar.copy(xT_hi[b][:], xT_ps[:]).then_inc(x_hi_done, 1)

            def turned_high(t):
                for c in range(2):
                    act.wait_ge(h_turned, 2 * t + c + 1)
                    act.wait_ge(out_done, t)
                    nc.scalar.copy(hT_hi[:, 4 * c:4 * c + 4, :], hT_ps[c][:]).then_inc(hT_hi_done, 1)

            x_high(0, 0)
            for n in w_names[1:]:
                act.wait_ge(loaded[n], 16)
                nc.scalar.copy(w_hi[n][:], w_raw[n][:]).then_inc(w_hi_done, 1)

            def body(t, b):
                first, last = static(t) and t == 0, static(t) and t == TT - 1
                for c in range(2):
                    act.wait_ge(gate_done, 2 * t + c + 1)
                    if not first:
                        act.wait_ge(h_done, 2 * t - 1 + c)
                    nc.scalar.activation(g[c][:], gate_ps[c][:], ACT.Silu).then_inc(silu_done, 1)
                    if c == 0 and not first:
                        turned_high(t - 1)
                if not last:
                    x_high(t + 1, 1 - b)
                act.wait_ge(h_done, 2 * t + 2)
                act.wait_ge(sparse, t)
                nc.scalar.activation(mag[:], h[b][:], ACT.Abs).then_inc(mag_done, 1)

            tiles(act, body)
            turned_high(TT - 1)

        @block.tensor
        def _(pe):
            def turn_x(t, b):
                pe.wait_ge(xn_done, t + 1)
                pe.wait_ge(x_lo_done, t)
                for k in range(KD):
                    last = nc.tensor.transpose(xT_ps[:, k, :], xn[b][:, k * P:(k + 1) * P], ident)
                last.then_inc(x_turned, 1)

            def ups(t, b, c):
                pe.wait_ge(x_lo_done, t + 1)
                if not (static(t) and t == 0):
                    pe.wait_ge(silu_done, 2 * t - 1 + c)
                    pe.wait_ge(h_done, 2 * t - 1 + c)
                for n, bank, done in (("gate", gate_ps[c], gate_done), ("up", up_ps[c], up_done)):
                    if static(t) and t == 0 and c == 0:
                        pe.wait_ge(w_lo_done, w_names.index(n) + 1)
                    for k in range(KD):
                        cols = slice(c * BANK, (c + 1) * BANK)
                        last = matmul3(nc, bank[:], (xT_hi[b][:, k, :], xT_lo[b][:, k, :]),
                                       (w_hi[n][:, k, cols], w_lo[n][:, k, cols]), start=(k == 0), stop=(k == KD - 1))
                    last.then_inc(done, 1)

            def turn_h(t, b):
                pe.wait_ge(sparse, t + 1)
                pe.wait_ge(hT_lo_done, 2 * t)
                for c in range(2):
                    for k in range(4):
                        at = (4 * c + k) * P
                        last = nc.tensor.transpose(hT_ps[c][:, k, :], h[b][:, at:at + P], ident)
                    last.then_inc(h_turned, 1)

            def down(t):
                pe.wait_ge(hT_lo_done, 2 * t + 2)
                pe.wait_ge(added, t)
                for k in range(KF):
                    last = matmul3(nc, out_ps[:], (hT_hi[:, k, :], hT_lo[:, k, :]),
                                   (w_hi["down"][:, k, :], w_lo["down"][:, k, :]), start=(k == 0), stop=(k == KF - 1))
                last.then_inc(out_done, 1)

            def body(t, b):
                first, last = static(t) and t == 0, static(t) and t == TT - 1
                ups(t, b, 0)
                if not first:
                    turn_h(t - 1, 1 - b)
                ups(t, b, 1)
                if not last:
                    turn_x(t + 1, 1 - b)
                if not first:
                    down(t - 1)

            turn_x(0, 0)
            body(0, 0)
            pe.wait_ge(w_lo_done, 3)
            with pe.Fori(0, TT // 2 - 1) as i:
                for b in (1, 0):
                    body(2 * i + 2 - b, b)
            body(TT - 1, 1)
            turn_h(TT - 1, 1)
            down(TT - 1)


HM = 32
PD = 128
NS_ = 128
G = 8
IN = HM * PD
TAPS = 4
CONV_TILES = (IN + 2 * G * NS_) // P
X0, B0, C0, DT0 = IN, 2 * IN, 2 * IN + G * NS_, 2 * IN + 2 * G * NS_
NORM_HEADS = IN // G // PD
NC = S // P
NORM_EPS = 1e-6
MASKED = -1e30


def conv_scalar(nc, out, ps, w, bias):
    return nc.scalar.activation(out, ps, ACT.Identity, bias=bias, scale=w(TAPS - 1))


def conv_tap(nc, out, ps, w, k):
    shift = TAPS - 1 - k
    return nc.vector.scalar_tensor_tensor(out[:, shift:], ps[:, :S - shift], w(k), out[:, shift:], ALU.mult, ALU.add)


def mamba_layer(nc, xres, ident, triangle, mask, in_w, conv_w, conv_b, dt_bias, a_log, d_skip, norm_w, out_w, tag):
    with ExitStack() as ctx:
        sp = Space(nc, ctx, tag)
        keep = dict(
            xhi=sp.sb("xnT_hi", [P, KD, S], F32R), xlo=sp.sb("xnT_lo", [P, KD, S], F32R),
            cT=sp.sb("cT", [P, G, S]),
            b_tok=sp.sb("b_tok", [P, G, NC - 1, NS_]),
            cb=sp.sb("cb", [P, G, NC, P]),
            dt=sp.sb("dt", [P, NC, HM]), ncum=sp.sb("neg_cum", [P, NC, HM]),
            to_end=sp.sb("decay_to_end", [P, NC, HM]), chunk_decay=sp.sb("chunk_decay", [P, NC, HM]),
            cumT=sp.sb("cumT", [P, S], F32R),
            w_conv=sp.sb("w_conv", [P, CONV_TILES, TAPS]), b_conv=sp.sb("b_conv", [P, CONV_TILES]),
            d_skip=sp.sb("d_skip", [P, HM]), norm_w=sp.sb("norm_w", [P, HM]),
        )
        prepare(nc, xres, ident, triangle, in_w, conv_w, conv_b, dt_bias, a_log, d_skip, norm_w, keep, tag + "_prep")
        scan_heads(nc, xres, ident, mask, in_w, out_w, keep, tag + "_scan")


def prepare(nc, xres, ident, triangle, in_w, conv_w, conv_b, dt_bias, a_log, d_skip, norm_w, keep, tag):
    with ExitStack() as ctx:
        sp = Space(nc, ctx, tag)
        cT, b_tok, cb = keep["cT"], keep["b_tok"], keep["cb"]
        dt, ncum, w_conv, b_conv = keep["dt"], keep["ncum"], keep["w_conv"], keep["b_conv"]
        wdt = sp.sb("w_dt", [P, KD, HM])
        wdt_hi = sp.sb("w_dt_hi", [P, KD, HM], F32R)
        wdt_lo = sp.sb("w_dt_lo", [P, KD, HM], F32R)
        bias = sp.sb("dt_bias", [P, HM])
        alog = sp.sb("a_log", [P, HM])
        a = sp.sb("a", [P, HM])
        tri = sp.sb("triangle", [P, P])
        ones = sp.sb("ones", [P, P])
        z = sp.sb("z", [P, NC, HM])
        z2 = sp.sb("z2", [P, NC, HM])
        adt = sp.sb("a_dt", [P, NC, HM])
        total = sp.sb("total", [P, NC, HM])
        cstack = sp.sb("cum_stack", [P, NC, P])
        w_raw = [sp.sb(f"w_bc{b}", [P, KD, 2, P]) for b in range(2)]
        w_hi = [sp.sb(f"w_bc_hi{b}", [P, KD, 2, P], F32R) for b in range(2)]
        w_lo = [sp.sb(f"w_bc_lo{b}", [P, KD, 2, P], F32R) for b in range(2)]
        pre = [sp.sb(f"conv{n}", [P, S]) for n in range(2)]
        bT = [sp.sb(f"bT{b}", [P, S]) for b in range(2)]
        proj_ps = [sp.ps(f"proj{n}", [P, S]) for n in range(2)]
        turn_ps = [sp.ps(f"turn{n}", [P, 4, P]) for n in range(2)]
        cb_ps = [sp.ps(f"cb{n}", [P, 4, P]) for n in range(2)]
        ln = LayerNorm(sp, [turn_ps_flat(t) for t in turn_ps], keep_f32=False, parts=(keep["xhi"], keep["xlo"]))

        small_in, wdt_in, wdt_split = sp.sem("small_in"), sp.sem("w_dt_in"), sp.sem("w_dt_split")
        w_in = [sp.sem(f"w_in{b}") for b in range(2)]
        w_hi_done, w_lo_done = sp.sem("w_hi_done"), sp.sem("w_lo_done")
        dt_mm, cum_mm, cum_turned = sp.sem("dt_mm"), sp.sem("cum_mm"), sp.sem("cum_turned")
        step, act_step, cumT_done = sp.sem("vector_step"), sp.sem("scalar_step"), sp.sem("cumT_done")
        consts = sp.sem("consts")
        projected, first_tap, tapped, silu_done = (sp.sem(n) for n in ("projected", "first_tap", "tapped", "silu_done"))
        b_turned, b_copied, cb_mm, cb_copied = (sp.sem(n) for n in ("b_turned", "b_copied", "cb_mm", "cb_copied"))
        ctx.callback(sp.clear_sems)
        block = ctx.enter_context(nc.Block())

        def edge(g):
            return (isinstance(g, int) and g == 0), (isinstance(g, int) and g == G - 1)

        def groups(eng, body):
            body(0, 0)
            with eng.Fori(0, G // 2 - 1) as i:
                for b in (1, 0):
                    body(2 * i + 2 - b, b)
            body(G - 1, 1)

        @block.sync
        def _(sync):
            sync.dma_start(wdt[:], in_w[:, DT0:DT0 + HM].rearrange("(k p) n -> p k n", p=P)).then_inc(wdt_in, 16)
            small = ((bias[:], dt_bias.partition_broadcast(P)), (alog[:], a_log.partition_broadcast(P)),
                     (keep["d_skip"][:], d_skip.partition_broadcast(P)), (tri[:], triangle),
                     (w_conv[:], conv_w), (b_conv[:], conv_b), (keep["norm_w"][:], norm_w))
            for dst, src in small:
                sync.dma_start(dst, src).then_inc(small_in, 16)

            def load(g, b):
                for n, col in enumerate((B0, C0)):
                    src = in_w[:, bass.ds(col + g * NS_, NS_)].rearrange("(k p) n -> p k n", p=P)
                    sync.dma_start(w_raw[b][:, :, n, :], src).then_inc(w_in[b], 16)

            load(0, 0)
            load(1, 1)
            with sync.Fori(0, G // 2 - 1) as i:
                for b in range(2):
                    sync.wait_ge(w_lo_done, 2 * i + b + 1)
                    load(2 * i + b + 2, b)

        @block.gpsimd
        def _(pool):
            nc.gpsimd.memset(ones[:], 1.0).then_inc(consts, 1)
            nc.gpsimd.memset(cstack[:], 0.0).then_inc(consts, 1)
            pool.wait_ge(wdt_split, 1)
            nc.gpsimd.tensor_tensor(wdt_lo[:], wdt[:], f32(wdt_hi[:]), ALU.subtract).then_inc(wdt_split, 1)

            def low(g, b):
                pool.wait_ge(w_hi_done, g + 1)
                nc.gpsimd.tensor_tensor(w_lo[b][:], w_raw[b][:], f32(w_hi[b][:]), ALU.subtract).then_inc(w_lo_done, 1)

            with pool.Fori(0, G // 2) as i:
                for b in range(2):
                    low(2 * i + b, b)

        @block.vector
        def _(dve):
            ln.vector(nc, xres)
            heads = [P, NC, HM]
            n = 0

            def then(ins):
                nonlocal n
                n += 1
                ins.then_inc(step, 1)
                dve.wait_ge(step, n)

            dve.wait_ge(small_in, 7 * 16)
            dve.wait_ge(dt_mm, 1)
            then(nc.vector.tensor_tensor(z[:], cb_ps[0][:, 0:2, :].rearrange("p c (e h) -> p (c e) h", h=HM),
                                         bias[:].unsqueeze(1).broadcast_to(heads), ALU.add))
            then(nc.vector.scalar_tensor_tensor(z2[:], z[:], -1.0, z[:], ALU.mult, ALU.min))
            dve.wait_ge(act_step, 2)
            then(nc.vector.scalar_tensor_tensor(dt[:], z[:], 0.0, z2[:], ALU.max, ALU.add))
            then(nc.vector.scalar_tensor_tensor(adt[:], dt[:], -1.0, a[:].unsqueeze(1).broadcast_to(heads), ALU.mult, ALU.mult))
            dve.wait_ge(cum_mm, 1)
            flat = cb_ps[1][:].rearrange("p c n -> p (c n)")
            cum = flat[:, 0:NC * HM].rearrange("p (c h) -> p c h", h=HM)
            tot = flat[:, NC * HM:2 * NC * HM].rearrange("p (c h) -> p c h", h=HM)
            dve.wait_ge(consts, 2)
            then(nc.vector.tensor_scalar(ncum[:], cum, -1.0, None, ALU.mult))
            nc.vector.tensor_copy(total[:], tot)
            nc.vector.tensor_copy(cstack[:, :, 0:HM].bitcast(F32R), cum)
            then(nc.vector.tensor_tensor(z2[:], tot, ncum[:], ALU.add))
            then(nc.vector.tensor_tensor(cstack[:, :, HM:2 * HM], cum, cstack[:, :, 0:HM], ALU.subtract))

            def w(tile):
                return lambda k: w_conv[:, bass.ds(tile, 1), k]

            def taps(g, n):
                tile = HM + G * n + g
                for k in (2, 1, 0):
                    dve.wait_ge(first_tap, 2 * g + n + 1) if k == 2 else dve.wait_ge(tapped, 6 * g + 3 * n + 2 - k)
                    conv_tap(nc, pre[n][:], proj_ps[n][:], w(tile), k).then_inc(tapped, 1)

            def copy_cb(g):
                for half in range(2):
                    dve.wait_ge(cb_mm, 2 * g + half + 1)
                    nc.vector.tensor_copy(cb[:, bass.ds(g, 1), 4 * half:4 * half + 4, :], cb_ps[half][:].unsqueeze(1)).then_inc(cb_copied, 1)

            def body(g, b):
                taps(g, 0)
                taps(g, 1)
                if not edge(g)[0]:
                    copy_cb(g - 1)

            groups(dve, body)
            copy_cb(G - 1)

        @block.scalar
        def _(act):
            act.wait_ge(wdt_in, 16)
            nc.scalar.copy(wdt_hi[:], wdt[:]).then_inc(wdt_split, 1)

            def high(g, b):
                act.wait_ge(w_in[b], 32 * (g // 2 + 1) if isinstance(g, int) else 16 * (g - b) + 32)
                if not isinstance(g, int) or g >= 2:
                    act.wait_ge(projected, 2 * (g - 1))
                nc.scalar.copy(w_hi[b][:], w_raw[b][:]).then_inc(w_hi_done, 1)

            high(0, 0)
            ln.scalar(nc)
            act.wait_ge(small_in, 7 * 16)
            act.wait_ge(step, 2)
            nc.scalar.activation(z2[:], z2[:], ACT.Exp).then_inc(act_step, 1)
            act.wait_ge(consts, 1)
            act.wait_ge(act_step, 1)
            nc.scalar.activation(a[:], alog[:], ACT.Exp)
            nc.scalar.activation(z2[:], z2[:], ACT.Ln, bias=ones[:, 0:1]).then_inc(act_step, 1)
            act.wait_ge(step, 6)
            nc.scalar.activation(keep["to_end"][:], z2[:], ACT.Exp)
            nc.scalar.activation(keep["chunk_decay"][:], total[:], ACT.Exp)
            for half in range(2):
                act.wait_ge(cum_turned, half + 1)
                nc.scalar.copy(keep["cumT"][:, half * BANK:(half + 1) * BANK],
                               turn_ps[half][:].rearrange("p c n -> p (c n)")).then_inc(cumT_done, 1)

            def tap(g, n):
                tile = HM + G * n + g
                act.wait_ge(projected, 2 * g + n + 1)
                act.wait_ge(silu_done, 2 * g)
                conv_scalar(nc, pre[n][:].unsqueeze(1), proj_ps[n][:].unsqueeze(1), lambda k: w_conv[:, bass.ds(tile, 1), k],
                            b_conv[:, bass.ds(tile, 1)]).then_inc(first_tap, 1)

            def silu(g, b, n):
                act.wait_ge(tapped, 6 * g + 3 * n + 3)
                if n == 0:
                    if not isinstance(g, int) or g >= 2:
                        act.wait_ge(cb_mm, 2 * (g - 1))
                    out = bT[b][:].unsqueeze(1)
                else:
                    out = cT[:, bass.ds(g, 1), :]
                nc.scalar.activation(out, pre[n][:].unsqueeze(1), ACT.Silu).then_inc(silu_done, 1)

            def copy_b(g):
                for half in range(2):
                    act.wait_ge(b_turned, 2 * g + half + 1)
                    c = 4 - half
                    nc.scalar.copy(b_tok[:, bass.ds(g, 1), 4 * half:4 * half + c, :],
                                   turn_ps[half][:, 0:c, :].unsqueeze(1)).then_inc(b_copied, 1)

            def body(g, b):
                first, last = edge(g)
                tap(g, 0)
                tap(g, 1)
                if not last:
                    high(g + 1, 1 - b)
                if not first:
                    copy_b(g - 1)
                silu(g, b, 0)
                silu(g, b, 1)

            groups(act, body)
            copy_b(G - 1)

        @block.tensor
        def _(pe):
            ln.tensor(nc, ident)
            ln.ready(pe)
            pe.wait_ge(wdt_split, 2)
            flat = cb_ps[0][:].rearrange("p c n -> p (c n)")
            for c in range(NC):
                for k in range(KD):
                    last = matmul3(nc, flat[:, c * HM:(c + 1) * HM], ln.parts(k, slice(c * P, (c + 1) * P)),
                                   (wdt_hi[:, k, :], wdt_lo[:, k, :]), start=(k == 0), stop=(k == KD - 1))
            last.then_inc(dt_mm, 1)
            pe.wait_ge(consts, 1)
            pe.wait_ge(step, 4)
            flat = cb_ps[1][:].rearrange("p c n -> p (c n)")
            rhs = adt[:].rearrange("p c h -> p (c h)")
            nc.tensor.matmul(flat[:, 0:NC * HM], tri[:], rhs, start=True, stop=True)
            nc.tensor.matmul(flat[:, NC * HM:2 * NC * HM], ones[:], rhs, start=True, stop=True).then_inc(cum_mm, 1)

            def project(g, b, n):
                pe.wait_ge(w_lo_done, g + 1)
                pe.wait_ge(tapped, 6 * g - 3 + 3 * n) if not edge(g)[0] else None
                for half in range(2):
                    cols = slice(half * BANK, (half + 1) * BANK)
                    for k in range(KD):
                        last = matmul3(nc, proj_ps[n][:, cols], (w_hi[b][:, k, n, :], w_lo[b][:, k, n, :]),
                                       ln.parts(k, cols), start=(k == 0), stop=(k == KD - 1))
                last.then_inc(projected, 1)

            def turn_b(g, b):
                pe.wait_ge(silu_done, 2 * g + 1)
                if not edge(g)[0]:
                    pe.wait_ge(b_copied, 2 * g)
                for half in range(2):
                    for c in range(4 - half):
                        at = (4 * half + c) * P
                        last = nc.tensor.transpose(turn_ps[half][:, c, :], bT[b][:, at:at + P], ident)
                    last.then_inc(b_turned, 1)

            def products(g, b):
                pe.wait_ge(silu_done, 2 * g + 2)
                if not edge(g)[0]:
                    pe.wait_ge(cb_copied, 2 * g)
                for half in range(2):
                    for c in range(4):
                        at = (4 * half + c) * P
                        last = nc.tensor.matmul(cb_ps[half][:, c, :].unsqueeze(1), bT[b][:, at:at + P],
                                                cT[:, bass.ds(g, 1), at:at + P], start=True, stop=True)
                    last.then_inc(cb_mm, 1)

            def body(g, b):
                project(g, b, 0)
                if not edge(g)[0]:
                    turn_b(g - 1, 1 - b)
                project(g, b, 1)
                if not edge(g)[0]:
                    products(g - 1, 1 - b)

            project(0, 0, 0)
            project(0, 0, 1)
            pe.wait_ge(step, 7)
            for half in range(2):
                for c in range(4):
                    last = nc.tensor.transpose(turn_ps[half][:, c, :], cstack[:, 4 * half + c, :], ident)
                last.then_inc(cum_turned, 1)
            pe.wait_ge(cumT_done, 2)
            with pe.Fori(0, G // 2 - 1) as i:
                for b in (1, 0):
                    body(2 * i + 2 - b, b)
            body(G - 1, 1)
            turn_b(G - 1, 1)
            products(G - 1, 1)


def turn_ps_flat(t):
    return t[:].rearrange("p c n -> p (c n)")


def scan_heads(nc, xres, ident, mask, in_w, out_w, keep, tag):
    with ExitStack() as ctx:
        sp = Space(nc, ctx, tag)
        xhi, xlo, cT, b_tok, cb = (keep[n] for n in ("xhi", "xlo", "cT", "b_tok", "cb"))
        dt, ncum, to_end, chunk_decay = (keep[n] for n in ("dt", "ncum", "to_end", "chunk_decay"))
        cumT, w_conv, b_conv, d_skip, norm_w = (keep[n] for n in ("cumT", "w_conv", "b_conv", "d_skip", "norm_w"))
        w_hi = [sp.sb(f"w_in_hi{b}", [P, KD, 2, P], F32R) for b in range(2)]
        w_lo = [sp.sb(f"w_in_lo{b}", [P, KD, 2, P], F32R) for b in range(2)]
        w_raw = sp.sb("w_in", [P, KD, 2, P])
        w_out = sp.sb("w_out", [P, NORM_HEADS, D])
        xs = [sp.sb(f"x{b}", [P, S]) for b in range(2)]
        gs = [sp.sb(f"gate{b}", [P, S]) for b in range(2)]
        xdt = sp.sb("x_dt", [P, NC, PD])
        xend = sp.sb("x_to_end", [P, NC - 1, PD])
        sel = sp.sb("select", [P, P], F32R)
        grow = sp.sb("exp_cum", [P, S])
        cgrow = sp.sb("c_exp_cum", [P, S - P])
        decay = sp.sb("decay", [P, NC, P])
        states = sp.sb("states", [P, NC - 1, PD])
        v = sp.sb("v", [P, NORM_HEADS + 2, S])
        squares = sp.sb("squares", [P, S])
        ones = sp.sb("ones", [P, 2])
        eps = sp.sb("eps", [P, 1])
        sums = sp.sb("sums", [P, TT])
        std = sp.sb("std", [P, TT])
        rnorm = sp.sb("rnorm", [P, TT])
        bmask = sp.sb("mask", [P, P], BF16)
        bident = sp.sb("ident_bf16", [P, P], BF16)
        mask_f32 = decay[:, 0, :]
        proj_ps = sp.ps("proj", [P, S])
        turn_ps = [sp.ps(f"turn{n}", [P, 4, P]) for n in range(2)]
        y_ps = sp.ps("y", [P, S])
        cum_ps = sp.ps("cum", [P, 4, P])
        out_ps = sp.ps("out", [P, 2, D])

        tail_ps = [out_ps] + [proj_ps[:, n * BANK:(n + 1) * BANK].rearrange("p (m d) -> p m d", m=2) for n in range(2)]
        tail_ps.append(cum_ps[:].rearrange("p (m c) n -> p m (c n)", m=2))

        names = ("w_hi_done", "w_lo_done", "w_out_scaled", "consts", "selected", "x_projected", "first_tap", "tapped",
                 "x_done", "gate_projected", "gate_done", "x_turned", "xdt_done", "xend_done", "cum_spread",
                 "grow_done", "cum_masked", "decay_done", "cgrow_done", "weighed", "in_chunk", "state_mm",
                 "state_done", "y_mm", "y_done", "v_done", "squared", "summed", "norm_mm", "sums_done", "std_done",
                 "rnorm_done", "out_mm", "added")
        q = {n: sp.sem(n) for n in names}
        w_in = [sp.sem(f"w_in{b}") for b in range(2)]
        w_out_in = sp.sem("w_out_in")
        mask_in = sp.sem("mask_in")
        ctx.callback(sp.clear_sems)
        block = ctx.enter_context(nc.Block())
        LAST = HM - 1
        PAIRS = TT // 2
        OUT_PAIRS = ((0, None), (1, 2), (3, None), (None, None))
        SUMS = NORM_HEADS - 1

        def is_at(n, k):
            return isinstance(n, int) and n == k

        def after(n, k):
            return not isinstance(n, int) or n >= k

        def v_row(j):
            jn = j % NORM_HEADS
            return jn + 2 if jn >= 2 else 2 * (j // NORM_HEADS) + jn

        def heads(eng, body):
            for n in range(G):
                body(n, n, n // NORM_HEADS)
            with eng.Fori(1, HM // G - 1) as i:
                for j in range(G):
                    body(i * G + j, j, i * (G // NORM_HEADS) + j // NORM_HEADS)
            for n in range(HM - G, HM):
                body(n, n % G, n // NORM_HEADS)

        @block.sync
        def _(sync):
            sync.dma_start(mask_f32, mask).then_inc(mask_in, 16)

            def load(n, b):
                if after(n, 1):
                    sync.wait_ge(q["w_lo_done"], n)
                for m, col in enumerate((X0, 0)):
                    src = in_w[:, bass.ds(col + n * PD, PD)].rearrange("(k p) n -> p k n", p=P)
                    sync.dma_start(w_raw[:, :, m, :], src).then_inc(w_in[b], 16)

            def load_out(gw):
                if after(gw, 1):
                    sync.wait_ge(q["out_mm"], PAIRS * gw)
                src = out_w[bass.ds(gw * NORM_HEADS * PD, NORM_HEADS * PD), :].rearrange("(j p) d -> p j d", p=P)
                sync.dma_start(w_out[:], src).then_inc(w_out_in, 16)

            for n in range(G):
                load(n, n % 2)
                if n == NORM_HEADS + 1:
                    load_out(0)
            with sync.Fori(1, HM // G) as i:
                for j in range(G):
                    load(i * G + j, j % 2)
                    if j % NORM_HEADS == 1:
                        load_out(2 * i - 1 + j // NORM_HEADS)
            load_out(G - 1)

        @block.gpsimd
        def _(pool):
            nc.gpsimd.memset(ones[:], 1.0).then_inc(q["consts"], 1)
            nc.gpsimd.memset(eps[:], NORM_EPS).then_inc(q["consts"], 1)
            nc.gpsimd.tensor_copy(bident[:], ident).then_inc(q["consts"], 1)
            pool.wait_ge(mask_in, 16)
            nc.gpsimd.tensor_copy(bmask[:], mask_f32).then_inc(q["consts"], 1)

            def low(n, b):
                pool.wait_ge(q["w_hi_done"], n + 1)
                nc.gpsimd.tensor_tensor(w_lo[b][:], w_raw[:], f32(w_hi[b][:]), ALU.subtract).then_inc(q["w_lo_done"], 1)

            def select(n):
                if after(n, 1):
                    pool.wait_ge(q["cum_spread"], 2 * n)
                nc.gpsimd.tensor_tensor(sel[:], ident[:, bass.ds(n, 1)].broadcast_to([P, P]),
                                        ident[:, bass.ds(n + HM, 1)].broadcast_to([P, P]), ALU.add).then_inc(q["selected"], 1)

            def cgrow_of(n, g):
                pool.wait_ge(q["grow_done"], 2 * n + 2)
                if after(n, 1):
                    pool.wait_ge(q["y_mm"], n)
                nc.gpsimd.tensor_tensor(cgrow[:], cT[:, g, P:], grow[:, P:], ALU.mult).then_inc(q["cgrow_done"], 1)

            def xend_of(n):
                pool.wait_ge(q["xdt_done"], 2 * n + 2)
                if after(n, 1):
                    pool.wait_ge(q["state_mm"], n)
                nc.gpsimd.tensor_tensor(xend[:], xdt[:, 0:NC - 1, :], to_end[:, 0:NC - 1, bass.ds(n, 1)].broadcast_to([P, NC - 1, PD]),
                                        ALU.mult).then_inc(q["xend_done"], 1)

            def sum_squares(n, j, gw):
                jn = j % NORM_HEADS
                if jn:
                    pool.wait_ge(q["squared"], n + 1)
                    pool.wait_ge(q["summed"], SUMS * gw + jn - 1)
                    nc.gpsimd.tensor_tensor(squares[:], squares[:], gs[j % 2][:], ALU.add).then_inc(q["summed"], 1)

            def scale_out(gw):
                pool.wait_ge(w_out_in, 16 * (gw + 1))
                nc.gpsimd.tensor_tensor(w_out[:], w_out[:], norm_w[:, bass.ds(gw * NORM_HEADS, NORM_HEADS)]
                                        .unsqueeze(2).broadcast_to([P, NORM_HEADS, D]), ALU.mult).then_inc(q["w_out_scaled"], 1)

            def body(n, j, gw):
                if not (is_at(n, LAST) or is_at(n, LAST - 1)):
                    low(n + 2, j % 2)
                    select(n + 2)
                if j % NORM_HEADS == NORM_HEADS - 1:
                    scale_out(gw)
                if not is_at(n, LAST):
                    cgrow_of(n + 1, (j + 1) % G)
                    xend_of(n + 1)
                sum_squares(n, j, gw)

            low(0, 0)
            low(1, 1)
            select(0)
            cgrow_of(0, 0)
            select(1)
            xend_of(0)
            heads(pool, body)

        @block.vector
        def _(dve):
            def w(n):
                return lambda k: w_conv[:, bass.ds(n, 1), k]

            def taps(n, j):
                for k in (2, 1, 0):
                    if k == 2:
                        dve.wait_ge(q["first_tap"], n + 1)
                    else:
                        dve.wait_ge(q["tapped"], 3 * n + 2 - k)
                    conv_tap(nc, xs[j % 2][:], proj_ps[:], w(n), k).then_inc(q["tapped"], 1)

            def scale_x(n):
                for half in range(2):
                    dve.wait_ge(q["x_turned"], 2 * n + half + 1)
                    if after(n, 1):
                        dve.wait_ge(q["state_mm"], n)
                        dve.wait_ge(q["xend_done"], n)
                    nc.vector.tensor_tensor(xdt[:, 4 * half:4 * half + 4, :], turn_ps[half][:],
                                            dt[:, 4 * half:4 * half + 4, bass.ds(n, 1)].broadcast_to([P, 4, PD]),
                                            ALU.mult).then_inc(q["xdt_done"], 1)

            def weigh(n, g):
                dve.wait_ge(q["decay_done"], 2 * n + 2)
                nc.vector.tensor_tensor(decay[:], decay[:], cb[:, g, :, :], ALU.mult).then_inc(q["weighed"], 1)

            def scan_states(n):
                dve.wait_ge(q["state_mm"], n + 1)
                if after(n, 1):
                    dve.wait_ge(q["y_mm"], n)
                for c in range(NC - 1):
                    new = turn_ps[c // 4][:, c % 4, :]
                    if c == 0:
                        nc.vector.tensor_copy(states[:, 0, :], new).then_inc(q["state_done"], 1)
                    else:
                        dve.wait_ge(q["state_done"], (NC - 1) * n + c)
                        nc.vector.scalar_tensor_tensor(states[:, c, :], states[:, c - 1, :],
                                                       chunk_decay[:, c, bass.ds(n, 1)], new,
                                                       ALU.mult, ALU.add).then_inc(q["state_done"], 1)

            def finish(n, j, gw):
                b, jn = j % 2, j % NORM_HEADS
                dve.wait_ge(q["y_mm"], n + 1)
                nc.vector.scalar_tensor_tensor(xs[b][:], xs[b][:], d_skip[:, bass.ds(n, 1)], y_ps[:],
                                               ALU.mult, ALU.add).then_inc(q["y_done"], 1)
                dve.wait_ge(q["y_done"], n + 1)
                dve.wait_ge(q["gate_done"], n + 1)
                if jn == 2 and after(gw, 1):
                    dve.wait_ge(q["out_mm"], PAIRS * gw)
                nc.vector.tensor_tensor(v[:, v_row(j), :], xs[b][:], gs[b][:], ALU.mult).then_inc(q["v_done"], 1)

            def copy_sums(gw):
                dve.wait_ge(q["norm_mm"], gw + 1)
                if after(gw, 1):
                    dve.wait_ge(q["std_done"], gw)
                nc.vector.tensor_copy(sums[:], turn_ps[1][:, 3, 0:TT]).then_inc(q["sums_done"], 1)

            def norm(gw):
                dve.wait_ge(q["std_done"], gw + 1)
                nc.vector.reciprocal(rnorm[:], std[:]).then_inc(q["rnorm_done"], 1)
                dve.wait_ge(q["rnorm_done"], gw + 1)

            def add_out(gw, p, out=out_ps):
                if p is None:
                    return
                dve.wait_ge(q["out_mm"], PAIRS * gw + p + 1)
                for m in range(2):
                    t = 2 * p + m
                    last = nc.vector.scalar_tensor_tensor(xres[:, t, :], out[:, m, :], rnorm[:, t:t + 1],
                                                          xres[:, t, :], ALU.mult, ALU.add)
                last.then_inc(q["added"], 1)

            def body(n, j, gw):
                pairs = OUT_PAIRS[j % NORM_HEADS] if after(gw, 1) else (None, None)
                if not is_at(n, LAST):
                    taps(n + 1, j + 1)
                scan_states(n)
                if pairs[0] == 0:
                    copy_sums(gw - 1)
                if pairs[1] is not None:
                    add_out(gw - 1, pairs[0])
                if not is_at(n, LAST):
                    weigh(n + 1, (j + 1) % G)
                finish(n, j, gw)
                if not is_at(n, LAST):
                    scale_x(n + 1)
                if pairs[0] == 0:
                    norm(gw - 1)
                add_out(gw - 1, pairs[0] if pairs[1] is None else pairs[1])

            taps(0, 0)
            scale_x(0)
            weigh(0, 0)
            heads(dve, body)
            copy_sums(G - 1)
            norm(G - 1)
            for p in range(PAIRS):
                add_out(G - 1, p, tail_ps[p])
            dve.wait_ge(q["added"], PAIRS * G)

        @block.scalar
        def _(act):
            def high(n, b):
                act.wait_ge(w_in[b], 32 * (n // 2 + 1) if isinstance(n, int) else 16 * (n - b) + 32)
                if after(n, 2):
                    act.wait_ge(q["gate_projected"], n - 1)
                nc.scalar.copy(w_hi[b][:], w_raw[:]).then_inc(q["w_hi_done"], 1)

            def tap(n, j):
                act.wait_ge(q["x_projected"], n + 1)
                if after(n, 2):
                    act.wait_ge(q["v_done"], n - 1)
                conv_scalar(nc, xs[j % 2][:].unsqueeze(1), proj_ps[:].unsqueeze(1), lambda k: w_conv[:, bass.ds(n, 1), k],
                            b_conv[:, bass.ds(n, 1)]).then_inc(q["first_tap"], 1)

            def x_of(n, j):
                act.wait_ge(q["tapped"], 3 * n + 3)
                nc.scalar.activation(xs[j % 2][:], xs[j % 2][:], ACT.Silu).then_inc(q["x_done"], 1)

            def gate_of(n, j, gw):
                act.wait_ge(q["gate_projected"], n + 1)
                jn2 = (j - 2) % NORM_HEADS
                if after(n, 2):
                    if jn2 == 0:
                        act.wait_ge(q["v_done"], n - 1)
                    else:
                        act.wait_ge(q["summed"], SUMS * (gw - (j % NORM_HEADS < 2)) + jn2)
                nc.scalar.activation(gs[j % 2][:], proj_ps[:], ACT.Silu).then_inc(q["gate_done"], 1)

            def grow_of(n, half):
                act.wait_ge(q["cum_spread"], 2 * n + half + 1)
                if after(n, 1):
                    act.wait_ge(q["cgrow_done"], n)
                nc.scalar.activation(grow[:, half * BANK:(half + 1) * BANK], cum_ps[:].rearrange("p c n -> p (c n)"),
                                     ACT.Exp).then_inc(q["grow_done"], 1)

            def decay_of(n, half):
                act.wait_ge(q["cum_masked"], 2 * n + half + 1)
                if after(n, 1):
                    act.wait_ge(q["in_chunk"], n)
                for c in range(4):
                    m = 4 * half + c
                    last = nc.scalar.activation(decay[:, m, :], cum_ps[:, c, :], ACT.Exp, bias=ncum[:, m, bass.ds(n, 1)])
                last.then_inc(q["decay_done"], 1)

            def square(n, j, gw):
                jn = j % NORM_HEADS
                act.wait_ge(q["v_done"], n + 1)
                if jn == 0 and after(n, 1):
                    act.wait_ge(q["norm_mm"], gw)
                nc.scalar.activation((gs[j % 2] if jn else squares)[:], v[:, v_row(j), :], ACT.Square).then_inc(q["squared"], 1)

            def norm(gw):
                act.wait_ge(q["sums_done"], gw + 1)
                if after(gw, 1):
                    act.wait_ge(q["rnorm_done"], gw)
                nc.scalar.activation(std[:], sums[:], ACT.Sqrt, bias=eps[:], scale=1.0 / (NORM_HEADS * PD)).then_inc(q["std_done"], 1)

            def ahead(n, j, gw, norm_of=None):
                tap(n, j)
                if after(n, 1) and not is_at(n, LAST):
                    high(n + 1, 1 - j % 2)
                for half in range(2):
                    grow_of(n, half)
                    decay_of(n, half)
                if norm_of is not None:
                    norm(norm_of)
                x_of(n, j)
                gate_of(n, j, gw)

            def body(n, j, gw):
                if not is_at(n, LAST):
                    ahead(n + 1, j + 1, gw + (j % NORM_HEADS == NORM_HEADS - 1), gw - 1 if j % NORM_HEADS == 0 and after(n, 1) else None)
                square(n, j, gw)

            high(0, 0)
            high(1, 1)
            act.wait_ge(q["consts"], 4)
            ahead(0, 0, 0)
            heads(act, body)
            norm(G - 1)

        @block.tensor
        def _(pe):
            def project(n, j, m):
                b = j % 2
                if m == 0:
                    pe.wait_ge(q["w_lo_done"], n + 1)
                    if after(n, 1):
                        pe.wait_ge(q["gate_done"], n)
                else:
                    pe.wait_ge(q["tapped"], 3 * n + 3)
                for half in range(2):
                    cols = slice(half * BANK, (half + 1) * BANK)
                    for k in range(KD):
                        last = matmul3(nc, proj_ps[:, cols], (w_hi[b][:, k, m, :], w_lo[b][:, k, m, :]),
                                       (xhi[:, k, cols], xlo[:, k, cols]), start=(k == 0), stop=(k == KD - 1))
                last.then_inc(q[("x_projected", "gate_projected")[m]], 1)

            def spread(n, half):
                if half == 0:
                    pe.wait_ge(q["selected"], n + 1)
                if half or after(n, 1):
                    pe.wait_ge(q["decay_done"], 2 * n + half)
                nc.tensor.matmul(cum_ps[:].rearrange("p c n -> p (c n)"), sel[:], cumT[:, half * BANK:(half + 1) * BANK],
                                 start=True, stop=True).then_inc(q["cum_spread"], 1)

            def mask_out(n, half):
                pe.wait_ge(q["grow_done"], 2 * n + half + 1)
                nc.tensor.matmul(cum_ps[:], bident[:], bmask[:].unsqueeze(1).broadcast_to([P, 4, P]),
                                 start=False, stop=True, skip_group_check=True).then_inc(q["cum_masked"], 1)

            def turn(n, j, gw):
                pe.wait_ge(q["x_done"], n + 1)
                if after(gw, 1) and (j - 1) % NORM_HEADS == 0:
                    pe.wait_ge(q["sums_done"], gw)
                if after(n, 1):
                    pe.wait_ge(q["state_done"], (NC - 1) * n)
                for half in range(2):
                    for c in range(4):
                        at = (4 * half + c) * P
                        last = nc.tensor.transpose(turn_ps[half][:, c, :], xs[j % 2][:, at:at + P], ident)
                    last.then_inc(q["x_turned"], 1)

            def in_chunks(n):
                pe.wait_ge(q["weighed"], n + 1)
                pe.wait_ge(q["xdt_done"], 2 * n + 2)
                if after(n, 1):
                    pe.wait_ge(q["y_done"], n)
                for c in range(NC):
                    last = nc.tensor.matmul(y_ps[:, c * P:(c + 1) * P], xdt[:, c, :], decay[:, c, :],
                                            start=(c % 4 == 0), stop=False, skip_group_check=True)
                last.then_inc(q["in_chunk"], 1)

            def new_states(n, g, sums_of):
                pe.wait_ge(q["xend_done"], n + 1)
                for c in range(NC - 1):
                    if c == NC - 2 and sums_of is not None:
                        norm_sums(sums_of)
                    last = nc.tensor.matmul(turn_ps[c // 4][:, c % 4, :], b_tok[:, g, c, :], xend[:, c, :],
                                            start=True, stop=True)
                last.then_inc(q["state_mm"], 1)

            def from_states(n):
                pe.wait_ge(q["state_done"], (NC - 1) * (n + 1))
                pe.wait_ge(q["cgrow_done"], n + 1)
                for c in range(1, NC):
                    last = nc.tensor.matmul(y_ps[:, c * P:(c + 1) * P], states[:, c - 1, :], cgrow[:, (c - 1) * P:c * P],
                                            start=False, stop=True, skip_group_check=True)
                last.then_inc(q["y_mm"], 1)

            def norm_sums(gw):
                pe.wait_ge(q["summed"], SUMS * (gw + 1))
                for t in range(TT):
                    last = nc.tensor.matmul(turn_ps[1][:, 3, t:t + 1], squares[:, t * P:(t + 1) * P], ones[:, 0:1],
                                            start=True, stop=True)
                last.then_inc(q["norm_mm"], 1)

            def project_out(gw, b, p, m, out=out_ps):
                if p is None:
                    return
                if p == 0 and m == 0:
                    pe.wait_ge(q["w_out_scaled"], gw + 1)
                    pe.wait_ge(q["v_done"], NORM_HEADS * (gw + 1))
                if m == 0 and out is out_ps and (p or after(gw, 1)):
                    pe.wait_ge(q["added"], PAIRS * gw + p)
                cols = slice((2 * p + m) * P, (2 * p + m + 1) * P)
                for jn in range(NORM_HEADS):
                    last = nc.tensor.matmul(out[:, m, :], v[:, v_row(b * NORM_HEADS + jn), cols],
                                            w_out[:, jn, :], start=(jn == 0), stop=(jn == NORM_HEADS - 1))
                if m == 1:
                    last.then_inc(q["out_mm"], 1)

            def body(n, j, gw):
                b = (j // NORM_HEADS + 1) % 2
                pairs = OUT_PAIRS[j % NORM_HEADS] if after(gw, 1) else (None, None)
                more = not is_at(n, LAST)
                if more:
                    project(n + 1, j + 1, 0)
                    spread(n + 1, 0)
                in_chunks(n)
                if more:
                    mask_out(n + 1, 0)
                new_states(n, j, gw - 1 if pairs[0] == 0 else None)
                project_out(gw - 1, b, pairs[0], 0)
                if more:
                    spread(n + 1, 1)
                project_out(gw - 1, b, pairs[0], 1)
                if more:
                    mask_out(n + 1, 1)
                    project(n + 1, j + 1, 1)
                for m in range(2):
                    project_out(gw - 1, b, pairs[1], m)
                from_states(n)
                if more:
                    turn(n + 1, j + 1, gw)

            pe.wait_ge(q["consts"], 4)
            project(0, 0, 0)
            for half in range(2):
                spread(0, half)
                mask_out(0, half)
            project(0, 0, 1)
            turn(0, 0, 0)
            heads(pe, body)
            norm_sums(G - 1)
            for p in range(PAIRS):
                for m in range(2):
                    project_out(G - 1, (G - 1) % 2, p, m, tail_ps[p])


def macaron_kernel(nc, x, out, ident_in, triangle, mask, places, cos_t, sin_t, moe_gate, moe_w1, moe_w3, moe_w2,
                   w_qkv, w_o, ffn_gate, ffn_up, ffn_down, in_w, conv_w, conv_b, dt_bias, a_log, d_skip, norm_w, out_w):
    with ExitStack() as ctx:
        sp = Space(nc, ctx, "main")
        xres = sp.sb("residual", [P, TT, D])
        ident = sp.sb("ident", [P, P])
        iota8 = sp.sb("places", [P, EXPERTS])
        loaded, stored = sp.sem("loaded"), sp.sem("stored")
        with nc.Block() as block:
            @block.sync
            def _(sync):
                sync.dma_start(xres[:], x.rearrange("b (t p) d -> p (b t) d", p=P)).then_inc(loaded, 16)
                sync.dma_start(ident[:], ident_in).then_inc(loaded, 16)
                sync.dma_start(iota8[:], places.partition_broadcast(P)).then_inc(loaded, 16)
                sync.wait_ge(loaded, 48)

        moe_layer(nc, xres[:], ident[:], iota8[:], moe_gate, moe_w1, moe_w3, moe_w2, "moe0")
        attention_layer(nc, xres[:], ident[:], cos_t, sin_t, w_qkv, w_o, "attn")
        moe_layer(nc, xres[:], ident[:], iota8[:], moe_gate, moe_w1, moe_w3, moe_w2, "moe1")
        sparse_ffn_layer(nc, xres[:], ident[:], ffn_gate, ffn_up, ffn_down, "ffn0")
        mamba_layer(nc, xres[:], ident[:], triangle, mask, in_w, conv_w, conv_b, dt_bias, a_log, d_skip, norm_w,
                    out_w, "ssm")
        sparse_ffn_layer(nc, xres[:], ident[:], ffn_gate, ffn_up, ffn_down, "ffn1")

        with nc.Block() as block:
            @block.sync
            def _(sync):
                sync.dma_start(out.rearrange("b (t p) d -> p (b t) d", p=P), xres[:]).then_inc(stored, 16)
                sync.wait_ge(stored, 16)


def kernel(**inputs):
    import numpy as np
    import concourse.bacc as bacc
    from concourse.bass_utils import run_bass_kernel_spmd

    given = {name: np.asarray(value) for name, value in inputs.items()}
    rows = np.arange(P, dtype=np.float32)
    half = np.arange(ROT, dtype=np.float32)
    inv_freq = (np.float32(1.0) / np.float32(10000.0) ** (half / np.float32(ROT))).astype(np.float32)
    angle = np.arange(S, dtype=np.float32)[:, None] * inv_freq[None, :]
    arrays = {
        "x": given["L0_attn_x"],
        "identity": np.eye(P, dtype=np.float32),
        "triangle": (rows[:, None] <= rows[None, :]).astype(np.float32),
        "mask": np.where(rows[None, :] < rows[:, None], np.float32(MASKED), np.float32(0.0)),
        "places": np.arange(EXPERTS, dtype=np.float32),
        "cos": np.cos(angle), "sin": np.sin(angle),
        "moe_gate": given["L0_ffn_w_gate"], "moe_w1": given["L0_ffn_w1"], "moe_w3": given["L0_ffn_w3"],
        "moe_w2": given["L0_ffn_w2"],
        "w_qkv": np.concatenate([given["L0_attn_Wq"], given["L0_attn_Wk"], given["L0_attn_Wv"]], axis=0).T,
        "w_o": given["L0_attn_Wo"].T,
        "ffn_gate": given["L1_ffn_w_gate"], "ffn_up": given["L1_ffn_w_up"], "ffn_down": given["L1_ffn_w_down"],
        "in_w": given["L1_attn_in_proj_w"].T,
        "conv_w": given["L1_attn_conv_w"].reshape(CONV_TILES, P, TAPS).transpose(1, 0, 2),
        "conv_b": given["L1_attn_conv_b"].reshape(CONV_TILES, P).T,
        "dt_bias": given["L1_attn_dt_bias"], "a_log": given["L1_attn_A_log"], "d_skip": given["L1_attn_D"],
        "norm_w": given["L1_attn_norm_w"].reshape(HM, PD).T,
        "out_w": given["L1_attn_out_proj_w"].T,
    }
    nc = bacc.Bacc("TRN2", target_bir_lowering=False, num_devices=1)
    aps, in_map = {}, {}
    for name, a in arrays.items():
        in_map[f"in_{name}"] = np.ascontiguousarray(a)
        aps[name] = nc.dram_tensor(f"in_{name}", a.shape, mybir.dt.from_np(a.dtype), kind="ExternalInput").ap()
    out = nc.dram_tensor("out_0", (1, S, D), F32, kind="ExternalOutput").ap()
    x = aps.pop("x")
    macaron_kernel(nc, x, out, *aps.values())
    result = run_bass_kernel_spmd(nc, [in_map], core_ids=[0])
    return result.results[0]["out_0"]
```

```python
from contextlib import ExitStack

import concourse.bass as bass
from concourse import mybir

F32 = mybir.dt.float32
F32R = mybir.dt.float32r
BF16 = mybir.dt.bfloat16
U32 = mybir.dt.uint32
ALU = mybir.AluOpType
ACT = mybir.ActivationFunctionType
AX_X = mybir.AxisListType.X

P = 128
D = 256
S = 1024
TT = S // P
KD = D // P
BANK = 512
LN_EPS = 1e-5


class Space:

    def __init__(self, nc, ctx, prefix):
        self.nc, self.ctx, self.prefix, self.sems = nc, ctx, prefix, []

    def sb(self, name, shape, dt=F32):
        return self.ctx.enter_context(self.nc.sbuf_tensor(f"{self.prefix}_{name}", shape, dt))

    def ps(self, name, shape, dt=F32):
        return self.ctx.enter_context(self.nc.psum_tensor(f"{self.prefix}_{name}", shape, dt))

    def sem(self, name):
        self.sems.append(self.ctx.enter_context(self.nc.semaphore(f"{self.prefix}_{name}")))
        return self.sems[-1]

    def clear_sems(self):
        numbers = sorted(s.num for s in self.sems)
        with self.nc.Block() as block:
            @block.gpsimd
            def _(pool):
                at = 0
                for n in range(1, len(numbers) + 1):
                    if n == len(numbers) or numbers[n] != numbers[n - 1] + 1:
                        pool.sem_clear(range(numbers[at], numbers[n - 1] + 1))
                        at = n


def matmul3(nc, out, lhs, rhs, start, stop):
    (lhs_hi, lhs_lo), (rhs_hi, rhs_lo) = lhs, rhs
    nc.tensor.matmul(out, lhs_hi, rhs_hi, start=start, stop=False)
    nc.tensor.matmul(out, lhs_hi, rhs_lo, start=False, stop=False)
    return nc.tensor.matmul(out, lhs_lo, rhs_hi, start=False, stop=stop)


def f32(ap):
    return ap.bitcast(F32)


class LayerNorm:

    def __init__(self, sp, banks, keep_f32=True, parts=None):
        self.banks = banks
        self.stats = sp.sb("ln_stats", [P, TT, 6])
        self.mv = sp.sb("ln_mean_var", [P, TT, 2])
        self.std = sp.sb("ln_std", [P, TT])
        self.rstd = sp.sb("ln_rstd", [P, TT])
        self.eps = sp.sb("ln_eps", [P, 1])
        self.xn = sp.sb("xn", [P, TT, D])
        self.xnT = sp.sb("xnT", [P, KD, S]) if keep_f32 else None
        self.hi, self.lo = parts or (sp.sb("xnT_hi", [P, KD, S], F32R), sp.sb("xnT_lo", [P, KD, S], F32R))
        self.stats_done = sp.sem("ln_stats_done")
        self.mv_done = sp.sem("ln_mv_done")
        self.std_done = sp.sem("ln_std_done")
        self.rstd_done = sp.sem("ln_rstd_done")
        self.xn_done = sp.sem("ln_xn_done")
        self.turned = sp.sem("ln_turned")
        self.hi_done = sp.sem("ln_hi_done")
        self.lo_done = sp.sem("ln_lo_done")

    PAIRS = TT // 2

    def tiles(self, half):
        return range(TT // 2 * half, TT // 2 * (half + 1))

    def vector(self, nc, x, before_low_parts=lambda: None):
        eng = nc.vector
        eng.memset(self.eps[:], LN_EPS).then_inc(self.stats_done, 1)
        for half in range(2):
            for t in self.tiles(half):
                eng.bn_stats(self.stats[:, t, :], x[:, t, :]).then_inc(self.stats_done, 1)
            eng.wait_ge(self.stats_done, TT // 2 * (half + 1) + 1)
            for t in self.tiles(half):
                eng.bn_aggr(self.mv[:, t, :], self.stats[:, t, :]).then_inc(self.mv_done, 1)
        for half in range(2):
            ts = self.tiles(half)
            eng.wait_ge(self.std_done, half + 1)
            eng.reciprocal(self.rstd[:, ts.start:ts.stop], self.std[:, ts.start:ts.stop]).then_inc(self.rstd_done, 1)
            eng.wait_ge(self.rstd_done, half + 1)
            for t in ts:
                eng.tensor_scalar(self.xn[:, t, :], x[:, t, :], self.mv[:, t, 0:1], self.rstd[:, t:t + 1],
                                  ALU.subtract, ALU.mult).then_inc(self.xn_done, 1)
        before_low_parts()
        for q in range(self.PAIRS):
            eng.wait_ge(self.hi_done, q + 1)
            cols = slice(2 * P * q, 2 * P * (q + 1))
            eng.tensor_tensor(self.lo[:, :, cols], self.banks[q][:, :].rearrange("p (k n) -> p k n", k=KD),
                              f32(self.hi[:, :, cols]), ALU.subtract).then_inc(self.lo_done, 1)

    def scalar(self, nc, before_copies=lambda: None):
        eng = nc.scalar
        for half in range(2):
            ts = slice(TT // 2 * half, TT // 2 * (half + 1))
            eng.wait_ge(self.mv_done, ts.stop)
            eng.activation(self.std[:, ts], self.mv[:, ts, 1], ACT.Sqrt, bias=self.eps[:]).then_inc(self.std_done, 1)
        before_copies()
        for q in range(self.PAIRS):
            eng.wait_ge(self.turned, q + 1)
            cols = slice(2 * P * q, 2 * P * (q + 1))
            bank = self.banks[q][:, :].rearrange("p (k n) -> p k n", k=KD)
            if self.xnT is not None:
                eng.copy(self.xnT[:, :, cols], bank)
            eng.copy(self.hi[:, :, cols], bank).then_inc(self.hi_done, 1)

    def tensor(self, nc, ident):
        eng = nc.tensor
        for q in range(self.PAIRS):
            eng.wait_ge(self.xn_done, 2 * (q + 1))
            for k in range(KD):
                for t in range(2):
                    last = eng.transpose(self.banks[q][:, (2 * k + t) * P:(2 * k + t + 1) * P],
                                         self.xn[:, 2 * q + t, k * P:(k + 1) * P], ident)
            last.then_inc(self.turned, 1)

    def ready(self, eng, tokens=S):
        eng.wait_ge(self.lo_done, -(-tokens // (2 * P)))

    def parts(self, k, cols):
        return self.hi[:, k, cols], self.lo[:, k, cols]


EXPERTS = 8
INNER = 512
KI = INNER // P
SOFTCAP = 30.0


def moe_layer(nc, xres, ident, iota8, w_gate, w1, w3, w2, tag):
    with ExitStack() as ctx:
        sp = Space(nc, ctx, tag)
        wg = sp.sb("w_gate", [P, KD, EXPERTS])
        logit = sp.sb("logit", [P, TT, EXPERTS])
        prob = sp.sb("prob", [P, TT, EXPERTS])
        row_max = sp.sb("row_max", [P, TT])
        row_sum = sp.sb("row_sum", [P, TT])
        top = sp.sb("top", [P, TT, 8])
        top_at = sp.sb("top_at", [P, TT, 8], U32)
        top_atf = sp.sb("top_atf", [P, TT, 2])
        chosen = sp.sb("chosen", [P, TT, EXPERTS])
        weight = sp.sb("weight", [P, TT, EXPERTS])
        w_up = [sp.sb(f"w_up{b}", [P, 2 * KD, INNER]) for b in range(2)]
        w_up_hi = [sp.sb(f"w_up_hi{b}", [P, 2 * KD, INNER], F32R) for b in range(2)]
        w_up_lo = [sp.sb(f"w_up_lo{b}", [P, 2 * KD, INNER], F32R) for b in range(2)]
        w_dn = [sp.sb(f"w_dn{b}", [P, KI, D]) for b in range(2)]
        w_dn_hi = [sp.sb(f"w_dn_hi{b}", [P, KI, D], F32R) for b in range(2)]
        w_dn_lo = [sp.sb(f"w_dn_lo{b}", [P, KI, D], F32R) for b in range(2)]
        g = sp.sb("silu", [P, 2, BANK])
        h = sp.sb("h", [P, 2, BANK])
        h_hi = sp.sb("h_hi", [P, KI, S], F32R)
        h_lo = sp.sb("h_lo", [P, KI, S], F32R)
        gate_ps = [sp.ps(f"gate{b}", [P, BANK]) for b in range(2)]
        up_ps = [sp.ps(f"up{b}", [P, BANK]) for b in range(2)]
        down_ps = [sp.ps(f"down{b}", [P, 2, D]) for b in range(4)]
        ln = LayerNorm(sp, [bank[:].rearrange("p t d -> p (t d)") for bank in down_ps])

        loaded = [[sp.sem(f"loaded{b}_{n}") for n in range(3)] for b in range(2)]
        wg_loaded = sp.sem("wg_loaded")
        w_hi_done, w_lo_done = sp.sem("w_hi_done"), sp.sem("w_lo_done")
        logits_done = sp.sem("logits_done")
        router = sp.sem("router")
        router_act = sp.sem("router_act")
        gate_done, up_done = sp.sem("gate_done"), sp.sem("up_done")
        silu_done, h_done = sp.sem("silu_done"), sp.sem("h_done")
        h_hi_done, h_lo_done = sp.sem("h_hi_done"), sp.sem("h_lo_done")
        down_done, added = sp.sem("down_done"), sp.sem("added")
        HB, BANKS = 2, 4
        UNITS = 2 * KI
        ctx.callback(sp.clear_sems)
        block = ctx.enter_context(nc.Block())

        def experts(eng, body):
            body(0, 0)
            with eng.Fori(0, EXPERTS // 2 - 1) as i:
                for b in (1, 0):
                    body(2 * i + 2 - b, b)
            body(EXPERTS - 1, 1)

        def wait(eng, sem, value):
            if not isinstance(value, int) or value > 0:
                eng.wait_ge(sem, value)

        def is_last(e):
            return isinstance(e, int) and e == EXPERTS - 1

        def w_part(n, up, down, b):
            return down[b][:] if n == 2 else up[b][:, n * KD:(n + 1) * KD, :]

        @block.sync
        def _(sync):
            sync.dma_start(wg[:], w_gate.rearrange("(k p) e -> p k e", p=P)).then_inc(wg_loaded, 16)

            def load(e, b):
                for n, w in enumerate((w1, w3, w2)):
                    sync.dma_start(w_part(n, w_up, w_dn, b), w[bass.ds(e, 1)].rearrange("e (k p) n -> p (e k) n", p=P)
                                   ).then_inc(loaded[b][n], 16)

            load(0, 0)
            load(1, 1)
            with sync.Fori(0, EXPERTS // 2 - 1) as i:
                for b in range(2):
                    sync.wait_ge(w_lo_done, 3 * (2 * i + b + 1))
                    load(2 * i + b + 2, b)

        @block.vector
        def _(dve):
            def split_first_up():
                dve.wait_ge(loaded[0][1], 16)
                dve.wait_ge(w_hi_done, 1)
                nc.vector.tensor_copy(w_part(1, w_up_hi, w_dn_hi, 0), w_part(1, w_up, w_dn, 0)).then_inc(w_hi_done, 1)

            ln.vector(nc, xres, before_low_parts=split_first_up)
            step = 0

            def then(ins):
                nonlocal step
                step += 1
                ins.then_inc(router, 1)
                dve.wait_ge(router, step)

            def take_max():
                dve.wait_ge(router_act, 1)
                then(nc.vector.tensor_reduce(row_max[:], prob[:], AX_X, ALU.max))
                then(nc.vector.tensor_tensor(logit[:], prob[:], row_max[:].unsqueeze(2).broadcast_to([P, TT, EXPERTS]), ALU.subtract))

            def softmax_and_top():
                nonlocal step
                dve.wait_ge(router_act, 2)
                then(nc.vector.tensor_reduce(row_sum[:], prob[:], AX_X, ALU.add))
                then(nc.vector.reciprocal(row_max[:], row_sum[:]))
                then(nc.vector.tensor_tensor(prob[:], prob[:], row_max[:].unsqueeze(2).broadcast_to([P, TT, EXPERTS]), ALU.mult))
                for t in range(TT):
                    nc.vector.max(top[:, t, :], prob[:, t, :]).then_inc(router, 1)
                step += TT

            def top_places():
                nonlocal step
                dve.wait_ge(router, step)
                for t in range(TT):
                    nc.vector.max_index(top_at[:, t, :], top[:, t, :], prob[:, t, :]).then_inc(router, 1)
                step += TT

            def weights():
                nonlocal step
                dve.wait_ge(router, step)
                then(nc.vector.tensor_copy(top_atf[:], top_at[:, :, 0:2]))
                places = iota8.unsqueeze(1).broadcast_to([P, TT, EXPERTS])
                nc.vector.tensor_tensor(chosen[:], top_atf[:, :, 0:1].broadcast_to([P, TT, EXPERTS]), places, ALU.is_equal).then_inc(router, 1)
                nc.vector.tensor_tensor(weight[:], top_atf[:, :, 1:2].broadcast_to([P, TT, EXPERTS]), places, ALU.is_equal).then_inc(router, 1)
                step += 2
                dve.wait_ge(router, step)
                then(nc.vector.tensor_tensor(chosen[:], chosen[:], weight[:], ALU.add))
                then(nc.vector.scalar_tensor_tensor(weight[:], prob[:], 0.5, chosen[:], ALU.mult, ALU.mult))

            def unit(e, u):
                n = UNITS * e + u
                half, m = divmod(u, KI)
                dve.wait_ge(silu_done, n + 1)
                dve.wait_ge(up_done, n + 1)
                nc.vector.tensor_tensor(h[:, u % HB, :], g[:, u % HB, :], up_ps[u % 2][:], ALU.mult).then_inc(h_done, 1)
                dve.wait_ge(h_hi_done, n + 1)
                nc.vector.tensor_tensor(h_lo[:, m, half * BANK:(half + 1) * BANK], h[:, u % HB, :],
                                        f32(h_hi[:, m, half * BANK:(half + 1) * BANK]), ALU.subtract).then_inc(h_lo_done, 1)

            def add_pair(e, q):
                dve.wait_ge(down_done, BANKS * e + q + 1)
                for j in range(2):
                    t = 2 * q + j
                    last = nc.vector.scalar_tensor_tensor(xres[:, t, :], down_ps[q][:, j, :],
                                                          weight[:, t, bass.ds(e, 1)], xres[:, t, :],
                                                          ALU.mult, ALU.add)
                last.then_inc(added, 1)

            def expert(e, b):
                more = not is_last(e)
                router_parts = (take_max, softmax_and_top, top_places, weights)
                for u in range(1, KI + 1):
                    if isinstance(e, int) and e == 0:
                        router_parts[u - 1]()
                    unit(e, u)
                add_pair(e, 0)
                for u in range(KI + 1, UNITS):
                    unit(e, u)
                    if u == KI + 1:
                        add_pair(e, 1)
                if more:
                    unit(e + 1, 0)
                add_pair(e, 2)
                add_pair(e, 3)

            unit(0, 0)
            experts(dve, expert)
            dve.wait_ge(added, BANKS * EXPERTS)

        @block.gpsimd
        def _(pool):
            def split_low(e, b):
                for n in range(3):
                    pool.wait_ge(w_hi_done, 3 * e + n + 1)
                    nc.gpsimd.tensor_tensor(w_part(n, w_up_lo, w_dn_lo, b), w_part(n, w_up, w_dn, b),
                                            f32(w_part(n, w_up_hi, w_dn_hi, b)), ALU.subtract).then_inc(w_lo_done, 1)

            split_low(0, 0)
            split_low(1, 1)
            with pool.Fori(0, EXPERTS // 2 - 1) as i:
                for b in range(2):
                    split_low(2 * i + b + 2, b)

        @block.scalar
        def _(act):
            def tanh():
                act.wait_ge(logits_done, 1)
                nc.scalar.activation(prob[:], down_ps[0][:, 0, 0:TT * EXPERTS].rearrange("p (t e) -> p t e", e=EXPERTS),
                                     ACT.Tanh, scale=1.0 / SOFTCAP).then_inc(router_act, 1)

            def exp():
                act.wait_ge(router, 2)
                nc.scalar.activation(prob[:], logit[:], ACT.Exp, scale=SOFTCAP).then_inc(router_act, 1)

            def split_high(e, b, n):
                act.wait_ge(loaded[b][n], 16 * (e // 2 + 1) if isinstance(e, int) else 8 * (e - b) + 16)
                nc.scalar.copy(w_part(n, w_up_hi, w_dn_hi, b), w_part(n, w_up, w_dn, b)).then_inc(w_hi_done, 1)

            def unit(e, u):
                n = UNITS * e + u
                half, m = divmod(u, KI)
                act.wait_ge(gate_done, n + 1)
                nc.scalar.activation(g[:, u % HB, :], gate_ps[u % 2][:], ACT.Silu).then_inc(silu_done, 1)
                act.wait_ge(h_done, n + 1)
                nc.scalar.copy(h_hi[:, m, half * BANK:(half + 1) * BANK], h[:, u % HB, :]).then_inc(h_hi_done, 1)

            def expert(e, b):
                more = not is_last(e)
                for u in range(1, KI):
                    if u == 1 and isinstance(e, int) and e == 0:
                        tanh()
                        exp()
                    unit(e, u)
                if more:
                    wait(act, down_done, BANKS * e)
                    for n in range(3):
                        split_high(e + 1, 1 - b, n)
                for u in range(KI, UNITS):
                    if u == KI:
                        wait(act, down_done, BANKS * e)
                    unit(e, u)
                if more:
                    act.wait_ge(down_done, BANKS * e + 2)
                    unit(e + 1, 0)

            ln.scalar(nc, before_copies=lambda: split_high(0, 0, 0))
            act.wait_ge(w_hi_done, 2)
            split_high(0, 0, 2)
            unit(0, 0)
            experts(act, expert)

        @block.tensor
        def _(pe):
            ln.tensor(nc, ident)

            def ups(e, b, u):
                n = UNITS * e + u
                half, m = divmod(u, KI)
                wait(pe, silu_done, n - 1)
                wait(pe, h_done, n - 1)
                for n_w, (bank, done) in enumerate(((gate_ps[u % 2], gate_done), (up_ps[u % 2], up_done))):
                    if isinstance(e, int) and e == 0 and u % KI == 0:
                        ln.ready(pe, (half + 1) * BANK)
                    if isinstance(e, int) and e == 0 and u == 0:
                        pe.wait_ge(w_lo_done, n_w + 1)
                    for k in range(KD):
                        w = n_w * KD + k, slice(m * P, (m + 1) * P)
                        last = matmul3(nc, bank[:], (w_up_hi[b][:, w[0], w[1]], w_up_lo[b][:, w[0], w[1]]),
                                       ln.parts(k, slice(half * BANK, (half + 1) * BANK)),
                                       start=(k == 0), stop=(k == KD - 1))
                    last.then_inc(done, 1)

            def down(e, b, half):
                pe.wait_ge(h_lo_done, UNITS * e + KI * (half + 1))
                if isinstance(e, int) and e == 0 and half == 0:
                    pe.wait_ge(router_act, 1)
                    pe.wait_ge(w_lo_done, 3)
                for q in range(2 * half, 2 * half + 2):
                    wait(pe, added, BANKS * e)
                    for j in range(2):
                        cols = slice((2 * q + j) * P, (2 * q + j + 1) * P)
                        for k in range(KI):
                            last = matmul3(nc, down_ps[q][:, j, :], (h_hi[:, k, cols], h_lo[:, k, cols]),
                                           (w_dn_hi[b][:, k, :], w_dn_lo[b][:, k, :]),
                                           start=(k == 0), stop=(k == KI - 1))
                    last.then_inc(down_done, 1)

            def expert(e, b):
                more = not is_last(e)
                for u in range(1, KI + 1):
                    ups(e, b, u)
                down(e, b, 0)
                for u in range(KI + 1, UNITS):
                    ups(e, b, u)
                if more:
                    pe.wait_ge(w_lo_done, 3 * (e + 2))
                    ups(e + 1, 1 - b, 0)
                down(e, b, 1)

            ups(0, 0, 0)
            ln.ready(pe)
            pe.wait_ge(wg_loaded, 16)
            for t in range(TT):
                for k in range(KD):
                    last = nc.tensor.matmul(down_ps[0][:, 0, t * EXPERTS:(t + 1) * EXPERTS],
                                            ln.xnT[:, k, t * P:(t + 1) * P], wg[:, k, :],
                                            start=(k == 0), stop=(k == KD - 1))
            last.then_inc(logits_done, 1)
            experts(pe, expert)


HEADS = 32
KV = 8
GQ = HEADS // KV
HD = D // HEADS
ROT = HD // 2
QKW = (HEADS + KV) * HD
QKVW = QKW + KV * HD
STACK = 32
NEG_HI, NEG_LO = 3 * HD, 3 * HD + 1
SCALE = HD ** -0.5
KT_TILES = S // P
SLOTS = 2 * KT_TILES
HALF = GQ * TT
CHUNKS = 2 * HALF
Q1_SLOTS = (3, 4)
FINAL_SLOTS = (11, 12)
PER_SLOT = CHUNKS // SLOTS
LEAD = HALF + 2 * PER_SLOT


def attention_layer(nc, xres, ident, cos_t, sin_t, w_qkv, w_o, tag):
    with ExitStack() as ctx:
        sp = Space(nc, ctx, tag)
        cos = sp.sb("cos", [P, TT, ROT])
        sin = sp.sb("sin", [P, TT, ROT])
        w_raw = sp.sb("w_qkv", [P, KD, QKVW])
        w_hi = sp.sb("w_qkv_hi", [P, KD, QKVW], F32R)
        w_lo = sp.sb("w_qkv_lo", [P, KD, QKVW], F32R)
        wo_raw = sp.sb("w_o", [P, KD, D])
        wo_hi = sp.sb("w_o_hi", [P, KD, D], F32R)
        wo_lo = sp.sb("w_o_lo", [P, KD, D], F32R)
        qk_cos = [sp.sb(f"qk_cos{b}", [P, QKW]) for b in range(2)]
        qk_sin = [sp.sb(f"qk_sin{b}", [P, QKW]) for b in range(2)]
        roped = sp.sb("roped", [P, TT, QKW])
        q_stack = sp.sb("q_stack", [P, TT, KV, GQ * STACK])
        k_stack = sp.sb("k_stack", [P, TT, KV * STACK])
        kT = sp.sb("kT", [P, 2, S], F32R)
        kz = [sp.sb(f"k_picks{b}", [P, GQ, S], F32R) for b in range(2)]
        v_all = sp.sb("v_all", [P, TT, KV, STACK])
        vg = [sp.sb(f"v_group{b}", [P, TT, STACK]) for b in range(2)]
        qg = [sp.sb(f"q_group{b}", [P, TT, GQ * STACK]) for b in range(2)]
        qm = [sp.sb(f"qT_pass1_{b}", [P, S], F32R) for b in range(2)]
        qe = [sp.sb(f"qT_pass2_{b}", [P, S], F32R) for b in range(2)]
        rmax2 = sp.sb("max_halves", [P, TT, GQ, 2])
        rmax = sp.sb("max", [P, TT, GQ])
        probs = [sp.sb(f"probs{b}", [P, GQ, BANK]) for b in range(2)]
        oT = sp.sb("oT", [P, BANK])
        recip = sp.sb("recip", [P, 4, GQ])

        st_ps = [sp.ps(f"scoresT{b}", [P, 2, BANK]) for b in range(2)]
        mx_ps = [sp.ps(f"scores{b}", [P, BANK]) for b in range(2)]
        o_ps = sp.ps("o", [P, BANK])
        turn_ps = sp.ps("turn", [P, 4, P])
        ln = LayerNorm(sp, [mx_ps[0], mx_ps[1], o_ps, turn_ps[:].rearrange("p t n -> p (t n)")], keep_f32=False)
        o_tok, oT_hi, oT_lo = ln.xn, ln.hi, ln.lo

        w_in, wo_in, tab_in = sp.sem("w_in"), sp.sem("wo_in"), sp.sem("tab_in")
        zeroed = sp.sem("zeroed")
        wh, wl = sp.sem("w_hi_done"), sp.sem("w_lo_done")
        qkv_done, rope_step, roped_done = sp.sem("qkv_done"), sp.sem("rope_step"), sp.sem("roped_done")
        v_done, stack_hi, stack_lo = sp.sem("v_done"), sp.sem("stack_hi"), sp.sem("stack_lo")
        k_turned, kT_done = sp.sem("k_turned"), sp.sem("kT_done")
        kz_in = [sp.sem(f"kz_in{b}") for b in range(2)]
        qg_in, vg_in = sp.sem("q_group_in"), sp.sem("v_group_in")
        q1_turned, q1_done = sp.sem("q1_turned"), sp.sem("q1_done")
        q2_turned, q2_done = sp.sem("q2_turned"), sp.sem("q2_done")
        scores_done, reduced, maxed, negated = (sp.sem(n) for n in ("scores_done", "reduced", "maxed", "negated"))
        scoresT_done, exp_done, pv_done = sp.sem("scoresT_done"), sp.sem("exp_done"), sp.sem("pv_done")
        o_copied, o_turned, o_step, o_norm = (sp.sem(n) for n in ("o_copied", "o_turned", "o_step", "o_norm"))
        f_turned, f_hi, f_lo, f_done = (sp.sem(n) for n in ("f_turned", "f_hi", "f_lo", "f_done"))
        fin = sp.sem("added")
        ctx.callback(sp.clear_sems)
        block = ctx.enter_context(nc.Block())

        def groups(eng, body):
            body(0, 0)
            with eng.Fori(0, KV // 2 - 1) as i:
                for b in (1, 0):
                    body(2 * i + 2 - b, b)
            body(KV - 1, 1)

        def edge(g):
            return (isinstance(g, int) and g == 0), (isinstance(g, int) and g == KV - 1)

        def chunk(n):
            half, r = divmod(n, HALF)
            return r // TT, half * (TT // 2) + r % TT // 2, r % 2

        def chunk_bank(g, n):
            if isinstance(g, int) and g == 0 and n < LEAD - 2:
                return st_ps[n % 4 // 2][:, n % 2, :]
            return mx_ps[n % 2][:]

        def last_of(n):
            return (n - LEAD) // PER_SLOT

        def chunks(s, last):
            found = [divmod(LEAD + PER_SLOT * s + i, CHUNKS) for i in range(PER_SLOT)]
            return [f for f in found if not (last and f[0])]

        def stack_views(t):
            return (k_stack[:, t, :].rearrange("p (h r) -> p h r", r=STACK),
                    q_stack[:, t, :, :].rearrange("p g (j r) -> p (g j) r", r=STACK),
                    roped[:, t, HEADS * HD:].rearrange("p (h r) -> p h r", r=HD),
                    roped[:, t, 0:HEADS * HD].rearrange("p (h r) -> p h r", r=HD))

        @block.sync
        def _(sync):
            sync.dma_start(w_raw[:], w_qkv.rearrange("(k p) n -> p k n", p=P)).then_inc(w_in, 16)
            sync.dma_start(cos[:], cos_t.rearrange("(t p) r -> p t r", p=P)).then_inc(tab_in, 16)
            sync.dma_start(sin[:], sin_t.rearrange("(t p) r -> p t r", p=P)).then_inc(tab_in, 16)
            sync.dma_start(wo_raw[:], w_o.rearrange("(k p) n -> p k n", p=P)).then_inc(wo_in, 16)
            sync.wait_ge(kT_done, 4)
            for g in range(KV):
                if g < 2:
                    sync.wait_ge(zeroed, 6 + g)
                if g >= 2:
                    sync.wait_ge(scoresT_done, 2 * SLOTS * (g - 1))
                for j in range(GQ):
                    src = (g % 4) * STACK
                    sync.dma_start(f32(kz[g % 2][j * STACK:(j + 1) * STACK, j, :]),
                                   f32(kT[src:src + STACK, g // 4, :])).then_inc(kz_in[g % 2], 16)

        @block.gpsimd
        def _(pool):
            def zero(view):
                nc.gpsimd.memset(view, 0.0).then_inc(zeroed, 1)

            def split(n, hi, lo, raw):
                pool.wait_ge(wh, n + 1)
                nc.gpsimd.tensor_tensor(lo[:], raw[:], f32(hi[:]), ALU.subtract).then_inc(wl, 1)

            rows = k_stack[:].rearrange("p t (h r) -> p (t h) r", r=STACK)
            nc.gpsimd.memset(rows[:, :, NEG_HI:NEG_LO + 1], 1.0).then_inc(zeroed, 1)
            zero(rows[:, :, NEG_LO + 1:])
            nc.gpsimd.memset(v_all[:, :, :, HD], 1.0).then_inc(zeroed, 1)
            zero(v_all[:, :, :, HD + 1:])
            split(0, w_hi, w_lo, w_raw)
            zero(q_stack[:].rearrange("p t g (j r) -> p (t g j) r", r=STACK)[:, :, NEG_HI:])
            zero(f32(kz[0][:]))
            for t in range(TT):
                ks, qs, kr, qr = stack_views(t)
                pool.wait_ge(stack_hi, 4 * t + 1)
                nc.gpsimd.tensor_tensor(ks[:, :, 2 * HD:3 * HD], kr, ks[:, :, 0:HD], ALU.subtract).then_inc(stack_lo, 1)
                pool.wait_ge(stack_hi, 4 * t + 3)
                nc.gpsimd.tensor_tensor(qs[:, :, HD:2 * HD], qr, qs[:, :, 0:HD], ALU.subtract).then_inc(stack_lo, 1)

            def copy_q(g, b):
                pool.wait_ge(stack_lo, 2 * TT)
                nc.gpsimd.tensor_copy(qg[b][:].unsqueeze(2), q_stack[:, :, bass.ds(g, 1), :]).then_inc(qg_in, 1)

            def copy_v(g, b):
                pool.wait_ge(v_done, TT)
                nc.gpsimd.tensor_copy(vg[b][:].unsqueeze(2), v_all[:, :, bass.ds(g, 1), :]).then_inc(vg_in, 1)

            pool.wait_ge(stack_lo, 2 * TT)
            pool.wait_ge(stack_hi, 4 * TT)
            pool.wait_ge(v_done, TT)
            copy_q(0, 0)
            copy_v(0, 0)
            zero(f32(kz[1][:]))
            copy_q(1, 1)
            copy_v(1, 1)
            split(1, wo_hi, wo_lo, wo_raw)
            with pool.Fori(0, KV // 2 - 1) as i:
                for b in range(2):
                    pool.wait_ge(q2_turned, 2 * (2 * i + b + 1))
                    copy_q(2 * i + b + 2, b)
                    pool.wait_ge(pv_done, SLOTS * (2 * i + b + 1))
                    copy_v(2 * i + b + 2, b)

        @block.vector
        def _(dve):
            ln.vector(nc, xres)
            dve.wait_ge(tab_in, 32)
            for t in range(TT):
                b = t % 2
                x = st_ps[b][:, 0, 0:QKW].rearrange("p (h s r) -> p h s r", s=2, r=ROT)
                c = cos[:, t, :].unsqueeze(1).unsqueeze(1).broadcast_to([P, HEADS + KV, 2, ROT])
                s1 = sin[:, t, :].unsqueeze(1).broadcast_to([P, HEADS + KV, ROT])
                xs = qk_sin[b][:].rearrange("p (h s r) -> p h s r", s=2, r=ROT)
                dve.wait_ge(qkv_done, t + 1)
                dve.wait_ge(v_done, t + 1)
                nc.vector.tensor_tensor(qk_cos[b][:].rearrange("p (h s r) -> p h s r", s=2, r=ROT), x, c, ALU.mult)
                nc.vector.scalar_tensor_tensor(xs[:, :, 0, :], x[:, :, 1, :], -1.0, s1, ALU.mult, ALU.mult)
                nc.vector.tensor_tensor(xs[:, :, 1, :], x[:, :, 0, :], s1, ALU.mult).then_inc(rope_step, 1)
                dve.wait_ge(rope_step, t + 1)
                nc.vector.tensor_tensor(roped[:, t, :], qk_cos[b][:], qk_sin[b][:], ALU.add).then_inc(roped_done, 1)
            def reduce(g, n):
                j, t, c = chunk(n)
                dve.wait_ge(scores_done, CHUNKS * g + n + 1)
                return nc.vector.tensor_reduce(rmax2[:, t, j, c:c + 1], chunk_bank(g, n), AX_X, ALU.max).then_inc(reduced, 1)

            def negate(g, b, half):
                ts = slice(half * (TT // 2), (half + 1) * (TT // 2))
                dve.wait_ge(reduced, CHUNKS * g + HALF * (half + 1))
                nc.vector.tensor_tensor(rmax[:, ts], rmax2[:, ts, :, 0], rmax2[:, ts, :, 1], ALU.max).then_inc(maxed, 1)
                stack = qg[b][:, ts, :].rearrange("p t (j r) -> p t j r", r=STACK)
                dve.wait_ge(maxed, 4 * g + 2 * half + 1)
                dve.wait_ge(q1_turned, 2 * (g + 1))
                nc.vector.tensor_scalar(stack[:, :, :, NEG_HI].bitcast(F32R), rmax[:, ts], -1.0, None, ALU.mult).then_inc(maxed, 1)
                dve.wait_ge(maxed, 4 * g + 2 * half + 2)
                nc.vector.scalar_tensor_tensor(stack[:, :, :, NEG_LO], rmax[:, ts], -1.0, stack[:, :, :, NEG_HI],
                                               ALU.mult, ALU.subtract).then_inc(negated, 1)

            def copy_o(g, half):
                dve.wait_ge(pv_done, SLOTS * g + KT_TILES * (half + 1))
                dve.wait_ge(o_turned, 2 * g + half)
                nc.vector.tensor_copy(oT[:], o_ps[:]).then_inc(o_copied, 1)

            def normalize(g, half):
                rows = turn_ps[:].rearrange("p t (j r) -> p t j r", r=STACK)
                dve.wait_ge(o_turned, 2 * g + half + 1)
                nc.vector.reciprocal(recip[:], rows[:, :, :, HD]).then_inc(o_step, 1)
                dve.wait_ge(o_step, 2 * g + half + 1)
                for t in range(4):
                    out = o_tok[:, 4 * half + t, bass.ds(g * GQ * HD, GQ * HD)].rearrange("p (j r) -> p j r", r=HD)
                    last = nc.vector.tensor_tensor(out, rows[:, t, :, 0:HD],
                                                   recip[:, t, :].unsqueeze(2).broadcast_to([P, GQ, HD]), ALU.mult)
                last.then_inc(o_norm, 1)

            def turned_low(p):
                dve.wait_ge(f_hi, p + 1)
                cols = slice(2 * P * p, 2 * P * (p + 1))
                nc.vector.tensor_tensor(oT_lo[:, :, cols], mx_ps[p % 2][:].rearrange("p (k n) -> p k n", k=KD),
                                        f32(oT_hi[:, :, cols]), ALU.subtract).then_inc(f_lo, 1)

            def add_projected(p):
                dve.wait_ge(f_done, p + 1)
                tiles = xres[:, 2 * p:2 * p + 2, :]
                nc.vector.tensor_tensor(tiles, mx_ps[p % 2][:].rearrange("p (t d) -> p t d", t=2), tiles, ALU.add).then_inc(fin, 1)

            def body(g, b):
                first, last = edge(g)
                for s in range(SLOTS):
                    for ahead, n in chunks(s, last):
                        reduce(g + ahead, n)
                    if s == 0 and not first:
                        copy_o(g - 1, 1)
                    if s == 2 and not first:
                        normalize(g - 1, 1)
                    if s == last_of(CHUNKS - 1):
                        negate(g, b, 1)
                    if s == KT_TILES:
                        copy_o(g, 0)
                    if s == KT_TILES + 2:
                        normalize(g, 0)
                    if s == last_of(CHUNKS + HALF - 1) and not last:
                        negate(g + 1, 1 - b, 0)
                    if last:
                        for p in range(2):
                            if s == FINAL_SLOTS[p] + 1:
                                turned_low(p)
                            if s == FINAL_SLOTS[p] + 3:
                                add_projected(p)

            for n in range(LEAD):
                reduce(0, n)
                if n == HALF - 1:
                    negate(0, 0, 0)
            groups(dve, body)
            copy_o(KV - 1, 1)
            normalize(KV - 1, 1)
            for p in range(2, 4):
                turned_low(p)
            for p in range(2, 4):
                add_projected(p)
            dve.wait_ge(fin, 4)

        @block.scalar
        def _(act):
            act.wait_ge(w_in, 16)
            nc.scalar.copy(w_hi[:], w_raw[:]).then_inc(wh, 1)
            ln.scalar(nc)
            act.wait_ge(zeroed, 5)

            def stack_high(t):
                ks, qs, kr, qr = stack_views(t)
                act.wait_ge(roped_done, t + 1)
                for dst, src in ((ks[:, :, 0:HD], kr), (ks[:, :, HD:2 * HD], kr), (qs[:, :, 0:HD], qr), (qs[:, :, 2 * HD:3 * HD], qr)):
                    nc.scalar.copy(dst.bitcast(F32R), src).then_inc(stack_hi, 1)

            for t in range(TT):
                act.wait_ge(qkv_done, t + 1)
                nc.scalar.copy(v_all[:, t, :, 0:HD], st_ps[t % 2][:, 0, QKW:QKVW].rearrange("p (h r) -> p h r", r=HD)
                               ).then_inc(v_done, 1)
                if t:
                    stack_high(t - 1)
            stack_high(TT - 1)
            for n in range(4):
                act.wait_ge(k_turned, n + 1)
                cols = slice(2 * P * n, 2 * P * (n + 1))
                nc.scalar.copy(kT[:, :, cols], mx_ps[n % 2][:].rearrange("p (a n) -> p a n", a=2)).then_inc(kT_done, 1)

            def copy_q1(g, b, half):
                act.wait_ge(q1_turned, 2 * g + half + 1)
                nc.scalar.copy(qm[b][:, half * BANK:(half + 1) * BANK], turn_ps[:].rearrange("p t n -> p (t n)")).then_inc(q1_done, 1)

            def copy_q2(g, b, half):
                act.wait_ge(q2_turned, 2 * g + half + 1)
                nc.scalar.copy(qe[b][:, half * BANK:(half + 1) * BANK], turn_ps[:].rearrange("p t n -> p (t n)")).then_inc(q2_done, 1)

            def exp_pair(g, s, pair):
                n = SLOTS * g + s
                act.wait_ge(scoresT_done, 2 * n + pair + 1)
                if not (isinstance(n, int) and n < 2):
                    act.wait_ge(pv_done, n - 1)
                nc.scalar.activation(probs[s % 2][:, 2 * pair:2 * pair + 2, :], st_ps[pair][:], ACT.Exp,
                                     scale=SCALE).then_inc(exp_done, 1)

            def turned_high(p):
                act.wait_ge(f_turned, p + 1)
                cols = slice(2 * P * p, 2 * P * (p + 1))
                nc.scalar.copy(oT_hi[:, :, cols], mx_ps[p % 2][:].rearrange("p (k n) -> p k n", k=KD)).then_inc(f_hi, 1)

            def body(g, b):
                first, last = edge(g)
                for s in range(SLOTS):
                    exp_pair(g, s, 0)
                    if s in Q1_SLOTS and not last:
                        copy_q1(g + 1, 1 - b, Q1_SLOTS.index(s))
                    if s == KT_TILES - 1:
                        copy_q2(g, b, 1)
                    if s == SLOTS - 1 and not last:
                        copy_q2(g + 1, 1 - b, 0)
                    exp_pair(g, s, 1)
                    for p in range(2):
                        if last and s == FINAL_SLOTS[p]:
                            turned_high(p)

            for half in range(2):
                copy_q1(0, 0, half)
            act.wait_ge(wo_in, 16)
            nc.scalar.copy(wo_hi[:], wo_raw[:]).then_inc(wh, 1)
            copy_q2(0, 0, 0)
            groups(act, body)
            for p in range(2, 4):
                turned_high(p)

        @block.tensor
        def _(pe):
            ln.tensor(nc, ident)
            pe.wait_ge(wl, 1)
            for t in range(TT):
                if t >= 2:
                    pe.wait_ge(rope_step, t - 1)
                ln.ready(pe, (t + 1) * P)
                for k in range(KD):
                    last = matmul3(nc, st_ps[t % 2][:, 0, 0:QKVW], ln.parts(k, slice(t * P, (t + 1) * P)),
                                   (w_hi[:, k, :], w_lo[:, k, :]), start=(k == 0), stop=(k == KD - 1))
                last.then_inc(qkv_done, 1)
            for n in range(4):
                pe.wait_ge(stack_hi, 8 * n + 6)
                pe.wait_ge(stack_lo, 4 * n + 3)
                if n >= 2:
                    pe.wait_ge(kT_done, n - 1)
                for a in range(2):
                    for t in range(2):
                        last = nc.tensor.transpose(mx_ps[n % 2][:, (2 * a + t) * P:(2 * a + t + 1) * P],
                                                   k_stack[:, 2 * n + t, a * P:(a + 1) * P], ident)
                last.then_inc(k_turned, 1)

            def turn_q(g, b, half, done):
                for t in range(4):
                    last = nc.tensor.transpose(turn_ps[:, t, :], qg[b][:, 4 * half + t, :], ident)
                last.then_inc(done, 1)

            def turn_q1(g, b, half):
                if half == 0:
                    pe.wait_ge(qg_in, g + 1)
                    if not edge(g)[0]:
                        pe.wait_ge(o_norm, 2 * (g - 1))
                else:
                    pe.wait_ge(q1_done, 2 * g + 1)
                turn_q(g, b, half, q1_turned)

            def turn_q2(g, b, half):
                pe.wait_ge(negated, 2 * g + half + 1)
                if half:
                    if not edge(g)[1]:
                        pe.wait_ge(q1_done, 2 * (g + 2))
                elif edge(g)[0]:
                    pe.wait_ge(q1_done, 2)
                else:
                    pe.wait_ge(o_norm, 2 * g - 1)
                turn_q(g, b, half, q2_turned)

            def kz_ready(g, b):
                pe.wait_ge(kz_in[b], 16 * GQ + 8 * GQ * (g - b))

            def score_chunk(g, b, n):
                m = CHUNKS * g + n
                j, t, c = chunk(n)
                if n == 0:
                    kz_ready(g, b)
                    pe.wait_ge(q1_done, 2 * (g + 1))
                if isinstance(m, int) and m < LEAD:
                    if 4 <= m < LEAD - 2:
                        pe.wait_ge(reduced, m - 3)
                else:
                    pe.wait_ge(reduced, m - 1)
                nc.tensor.matmul(chunk_bank(g, n), qm[b][:, t * P:(t + 1) * P], kz[b][:, j, c * BANK:(c + 1) * BANK],
                                 start=True, stop=True).then_inc(scores_done, 1)

            def scoresT(g, b, s, pair, between=lambda: None):
                half, kt = divmod(s, KT_TILES)
                n = SLOTS * g + s
                if pair == 0 and kt == 0:
                    pe.wait_ge(q2_done, 2 * g + half + 1)
                if isinstance(n, int) and n == 0:
                    pe.wait_ge(reduced, LEAD - 2)
                else:
                    pe.wait_ge(exp_done, 2 * n - 1 + pair)
                for j in (2 * pair, 2 * pair + 1):
                    last = nc.tensor.matmul(st_ps[pair][:, j % 2, :], kz[b][:, j, kt * P:(kt + 1) * P],
                                            qe[b][:, half * BANK:(half + 1) * BANK], start=True, stop=True)
                    if j % 2 == 0:
                        between()
                last.then_inc(scoresT_done, 1)

            def values(g, b, s):
                half, kt = divmod(s, KT_TILES)
                pe.wait_ge(exp_done, 2 * (SLOTS * g + s) + 2)
                if s == 0:
                    pe.wait_ge(vg_in, g + 1)
                if kt == 0:
                    pe.wait_ge(o_copied, 2 * g + half)
                for j in range(GQ):
                    last = nc.tensor.matmul(o_ps[j * STACK:(j + 1) * STACK, :], vg[b][:, kt, :], probs[s % 2][:, j, :],
                                            start=(kt == 0), stop=(kt == KT_TILES - 1))
                last.then_inc(pv_done, 1)

            def turn_o(g, half):
                pe.wait_ge(o_copied, 2 * g + half + 1)
                if not (edge(g)[1] and half):
                    pe.wait_ge(q2_done, 2 * g + half + 2)
                for t in range(4):
                    last = nc.tensor.transpose(turn_ps[:, t, :], oT[:, t * P:(t + 1) * P], ident)
                last.then_inc(o_turned, 1)

            def turn_final(p):
                pe.wait_ge(o_norm, 2 * (KV - 1) + p // 2 + 1)
                if p >= 2:
                    pe.wait_ge(fin, p - 1)
                else:
                    pe.wait_ge(reduced, KV * CHUNKS)
                for k in range(KD):
                    for t in range(2):
                        last = nc.tensor.transpose(mx_ps[p % 2][:, (2 * k + t) * P:(2 * k + t + 1) * P],
                                                   o_tok[:, 2 * p + t, k * P:(k + 1) * P], ident)
                last.then_inc(f_turned, 1)

            def project_final(p):
                pe.wait_ge(wl, 2)
                pe.wait_ge(f_lo, p + 1)
                for t in range(2):
                    cols = slice((2 * p + t) * P, (2 * p + t + 1) * P)
                    for k in range(KD):
                        last = matmul3(nc, mx_ps[p % 2][:, t * D:(t + 1) * D], (oT_hi[:, k, cols], oT_lo[:, k, cols]),
                                       (wo_hi[:, k, :], wo_lo[:, k, :]), start=(k == 0), stop=(k == KD - 1))
                last.then_inc(f_done, 1)

            def body(g, b):
                first, last = edge(g)
                for s in range(SLOTS):
                    todo = chunks(s, last)

                    def one():
                        if todo:
                            ahead, n = todo.pop(0)
                            score_chunk(g + ahead, (1 - b) if ahead else b, n)

                    scoresT(g, b, s, 0)
                    if s in Q1_SLOTS and not last:
                        turn_q1(g + 1, 1 - b, Q1_SLOTS.index(s))
                    if s == KT_TILES - 1:
                        turn_q2(g, b, 1)
                    if s == SLOTS - 1 and not last:
                        turn_q2(g + 1, 1 - b, 0)
                    scoresT(g, b, s, 1, one)
                    one()
                    if s > 0:
                        values(g, b, s - 1)
                    elif not first:
                        values(g - 1, 1 - b, SLOTS - 1)
                    one()
                    one()
                    if s == 1 and not first:
                        turn_o(g - 1, 1)
                    if s == KT_TILES + 1:
                        turn_o(g, 0)
                    if last:
                        for p in range(2):
                            if s == FINAL_SLOTS[p]:
                                turn_final(p)
                            if s == FINAL_SLOTS[p] + 2:
                                project_final(p)

            pe.wait_ge(kT_done, 4)
            turn_q1(0, 0, 0)
            turn_q1(0, 0, 1)
            for n in range(LEAD):
                if n == HALF + 2:
                    turn_q2(0, 0, 0)
                score_chunk(0, 0, n)
            groups(pe, body)
            values(KV - 1, 1, SLOTS - 1)
            turn_o(KV - 1, 1)
            for p in range(2, 4):
                turn_final(p)
            for p in range(2, 4):
                project_final(p)


FFN = 1024
KF = FFN // P
QUAD = FFN // 4


def sparse_ffn_layer(nc, xres, ident, w_gate, w_up, w_down, tag):
    with ExitStack() as ctx:
        sp = Space(nc, ctx, tag)
        stats = sp.sb("stats", [P, TT, 6])
        mv = sp.sb("mean_var", [P, TT, 2])
        std = sp.sb("std", [P, TT])
        rstd = sp.sb("rstd", [P, TT])
        eps = sp.sb("eps", [P, 1])
        xn = [sp.sb(f"xn{b}", [P, D]) for b in range(2)]
        xT_hi = [sp.sb(f"xT_hi{b}", [P, KD, P], F32R) for b in range(2)]
        xT_lo = [sp.sb(f"xT_lo{b}", [P, KD, P], F32R) for b in range(2)]
        w_names = ("gate", "up", "down")
        w_shape = {"gate": (KD, FFN), "up": (KD, FFN), "down": (KF, D)}
        w_src = {"gate": w_gate, "up": w_up, "down": w_down}
        w_raw = {n: sp.sb(f"w_{n}", [P, *w_shape[n]]) for n in w_names}
        w_hi = {n: sp.sb(f"w_{n}_hi", [P, *w_shape[n]], F32R) for n in w_names}
        w_lo = {n: sp.sb(f"w_{n}_lo", [P, *w_shape[n]], F32R) for n in w_names}
        g = [sp.sb(f"silu{c}", [P, BANK]) for c in range(2)]
        h = [sp.sb(f"h{b}", [P, FFN]) for b in range(2)]
        mag = sp.sb("magnitude", [P, FFN])
        c02_13 = sp.sb("c02_13", [P, 2, QUAD], BF16)
        c03_12 = sp.sb("c03_12", [P, 2, QUAD], BF16)
        c01_23 = sp.sb("c01_23", [P, 2, QUAD], BF16)
        wins = sp.sb("wins", [P, 2, QUAD], BF16)
        losses = sp.sb("losses", [P, 2, QUAD], BF16)
        score = sp.sb("score", [P, 4, QUAD], BF16)
        hT_hi = sp.sb("hT_hi", [P, KF, P], F32R)
        hT_lo = sp.sb("hT_lo", [P, KF, P], F32R)
        gate_ps = [sp.ps(f"gate{c}", [P, BANK]) for c in range(2)]
        up_ps = [sp.ps(f"up{c}", [P, BANK]) for c in range(2)]
        hT_ps = [sp.ps(f"hT{c}", [P, 4, P]) for c in range(2)]
        xT_ps = sp.ps("xT", [P, KD, P])
        out_ps = sp.ps("out", [P, D])

        loaded = {n: sp.sem(f"{n}_loaded") for n in w_names}
        w_hi_done = sp.sem("w_hi_done")
        w_lo_done = {n: sp.sem(f"w_{n}_lo_done") for n in w_names}
        stats_done, mv_done, std_done, rstd_done = (sp.sem(n) for n in ("stats_done", "mv_done", "std_done", "rstd_done"))
        xn_done, x_turned, x_hi_done, x_lo_done = (sp.sem(n) for n in ("xn_done", "x_turned", "x_hi_done", "x_lo_done"))
        gate_done, up_done, silu_done, h_done = (sp.sem(n) for n in ("gate_done", "up_done", "silu_done", "h_done"))
        mag_done, sparse, steps = sp.sem("mag_done"), sp.sem("sparse"), sp.sem("sparsify_steps")
        h_turned, hT_hi_done, hT_lo_done = (sp.sem(n) for n in ("h_turned", "hT_hi_done", "hT_lo_done"))
        out_done, added = sp.sem("out_done"), sp.sem("added")
        ctx.callback(sp.clear_sems)
        block = ctx.enter_context(nc.Block())

        def tiles(eng, body):
            for t in range(3):
                body(t, t % 2)
            with eng.Fori(1, TT // 2 - 1) as i:
                for b in (1, 0):
                    body(2 * i + 2 - b, b)
            body(TT - 1, 1)

        def static(t):
            return isinstance(t, int)

        @block.sync
        def _(sync):
            for n in w_names:
                sync.dma_start(w_raw[n][:], w_src[n].rearrange("(k p) n -> p k n", p=P)).then_inc(loaded[n], 16)

        @block.gpsimd
        def _(pool):
            for n in ("gate", "down"):
                pool.wait_ge(w_hi_done, w_names.index(n) + 1)
                nc.gpsimd.tensor_tensor(w_lo[n][:], w_raw[n][:], f32(w_hi[n][:]), ALU.subtract).then_inc(w_lo_done[n], 1)

        @block.vector
        def _(dve):
            nc.vector.memset(eps[:], LN_EPS).then_inc(stats_done, 1)
            for t in range(TT):
                nc.vector.bn_stats(stats[:, t, :], xres[:, t, :]).then_inc(stats_done, 1)
            dve.wait_ge(stats_done, TT + 1)
            for t in range(TT):
                nc.vector.bn_aggr(mv[:, t, :], stats[:, t, :]).then_inc(mv_done, 1)
            dve.wait_ge(std_done, 1)
            nc.vector.reciprocal(rstd[:], std[:]).then_inc(rstd_done, 1)
            dve.wait_ge(rstd_done, 1)

            def normalize(t, b):
                if not static(t) or t >= 2:
                    dve.wait_ge(x_turned, t - 1)
                nc.vector.tensor_scalar(xn[b][:].unsqueeze(1), xres[:, bass.ds(t, 1), :], mv[:, bass.ds(t, 1), 0],
                                        rstd[:, bass.ds(t, 1)], ALU.subtract, ALU.mult).then_inc(xn_done, 1)

            def x_low(t, b):
                dve.wait_ge(x_hi_done, t + 1)
                nc.vector.tensor_tensor(xT_lo[b][:], xT_ps[:], f32(xT_hi[b][:]), ALU.subtract).then_inc(x_lo_done, 1)

            def product(t, b, c):
                dve.wait_ge(silu_done, 2 * t + c + 1)
                dve.wait_ge(up_done, 2 * t + c + 1)
                if c == 0 and (not static(t) or t >= 2):
                    dve.wait_ge(h_turned, 2 * (t - 1))
                nc.vector.tensor_tensor(h[b][:, c * BANK:(c + 1) * BANK], g[c][:], up_ps[c][:], ALU.mult).then_inc(h_done, 1)

            def turned_low(t):
                for c in range(2):
                    dve.wait_ge(hT_hi_done, 2 * t + c + 1)
                    nc.vector.tensor_tensor(hT_lo[:, 4 * c:4 * c + 4, :], hT_ps[c][:],
                                            f32(hT_hi[:, 4 * c:4 * c + 4, :]), ALU.subtract).then_inc(hT_lo_done, 1)

            def sparsify(t, b):
                a = mag[:].rearrange("p (q w) -> p w q", w=4)
                hq = h[b][:].rearrange("p (q w) -> p w q", w=4)
                dve.wait_ge(mag_done, t + 1)
                nc.vector.tensor_tensor(c02_13[:], a[:, 0:2], a[:, 2:4], ALU.is_ge)
                nc.vector.tensor_tensor(c03_12[:, 0], a[:, 0], a[:, 3], ALU.is_ge)
                nc.vector.tensor_tensor(c03_12[:, 1], a[:, 1], a[:, 2], ALU.is_ge)
                nc.vector.tensor_tensor(c01_23[:], a[:, 0:4:2], a[:, 1:4:2], ALU.is_ge).then_inc(steps, 1)
                dve.wait_ge(steps, 3 * t + 1)
                nc.vector.tensor_tensor(wins[:], c02_13[:], c03_12[:], ALU.add)
                nc.vector.tensor_tensor(losses[:, 0], c02_13[:, 0], c03_12[:, 1], ALU.add)
                nc.vector.tensor_tensor(losses[:, 1], c03_12[:, 0], c02_13[:, 1], ALU.add).then_inc(steps, 1)
                dve.wait_ge(steps, 3 * t + 2)
                nc.vector.tensor_tensor(score[:, 0], wins[:, 0], c01_23[:, 0], ALU.add)
                nc.vector.tensor_tensor(score[:, 1], wins[:, 1], c01_23[:, 0], ALU.subtract)
                nc.vector.tensor_tensor(score[:, 2], losses[:, 0], c01_23[:, 1], ALU.subtract)
                nc.vector.tensor_tensor(score[:, 3], losses[:, 1], c01_23[:, 1], ALU.add).then_inc(steps, 1)
                dve.wait_ge(steps, 3 * t + 3)
                for w, (op, bound) in enumerate(((ALU.is_ge, 2.0), (ALU.is_ge, 1.0), (ALU.is_le, 0.0), (ALU.is_le, 1.0))):
                    last = nc.vector.scalar_tensor_tensor(hq[:, w], score[:, w], bound, hq[:, w], op, ALU.mult)
                last.then_inc(sparse, 1)

            def add(t):
                dve.wait_ge(out_done, t + 1)
                nc.vector.scalar_tensor_tensor(xres[:, bass.ds(t, 1), :], out_ps[:].unsqueeze(1), 0.5,
                                               xres[:, bass.ds(t, 1), :], ALU.mult, ALU.add).then_inc(added, 1)

            def body(t, b):
                first, last = static(t) and t == 0, static(t) and t == TT - 1
                product(t, b, 0)
                if not first:
                    turned_low(t - 1)
                product(t, b, 1)
                if not last:
                    x_low(t + 1, 1 - b)
                sparsify(t, b)
                if not first:
                    add(t - 1)

            normalize(0, 0)
            normalize(1, 1)
            x_low(0, 0)
            dve.wait_ge(w_hi_done, 2)
            nc.vector.tensor_tensor(w_lo["up"][:], w_raw["up"][:], f32(w_hi["up"][:]), ALU.subtract).then_inc(w_lo_done["up"], 1)
            for t in range(3):
                body(t, t % 2)
                normalize(t + 2, t % 2)
            with dve.Fori(1, TT // 2 - 2) as i:
                for b in (1, 0):
                    body(2 * i + 2 - b, b)
                    normalize(2 * i + 4 - b, b)
            for t in range(TT - 3, TT):
                body(t, t % 2)
                if t + 2 < TT:
                    normalize(t + 2, t % 2)
            turned_low(TT - 1)
            add(TT - 1)
            dve.wait_ge(added, TT)

        @block.scalar
        def _(act):
            def split(n):
                act.wait_ge(loaded[n], 16)
                nc.scalar.copy(w_hi[n][:], w_raw[n][:]).then_inc(w_hi_done, 1)

            act.wait_ge(mv_done, TT)
            nc.scalar.activation(std[:], mv[:, :, 1], ACT.Sqrt, bias=eps[:]).then_inc(std_done, 1)
            split("gate")

            def x_high(t, b):
                act.wait_ge(x_turned, t + 1)
                nc.scalar.copy(xT_hi[b][:], xT_ps[:]).then_inc(x_hi_done, 1)

            def turned_high(t):
                for c in range(2):
                    act.wait_ge(h_turned, 2 * t + c + 1)
                    if not static(t) or t >= 1:
                        act.wait_ge(out_done, t)
                    nc.scalar.copy(hT_hi[:, 4 * c:4 * c + 4, :], hT_ps[c][:]).then_inc(hT_hi_done, 1)

            x_high(0, 0)
            split("up")

            def body(t, b):
                first, last = static(t) and t == 0, static(t) and t == TT - 1
                for c in range(2):
                    act.wait_ge(gate_done, 2 * t + c + 1)
                    if not first:
                        act.wait_ge(h_done, 2 * t - 1 + c)
                    nc.scalar.activation(g[c][:], gate_ps[c][:], ACT.Silu).then_inc(silu_done, 1)
                    if c == 0 and first:
                        split("down")
                    if c == 0 and not first:
                        turned_high(t - 1)
                if not last:
                    x_high(t + 1, 1 - b)
                act.wait_ge(h_done, 2 * t + 2)
                if not first:
                    act.wait_ge(sparse, t)
                nc.scalar.activation(mag[:], h[b][:], ACT.Abs).then_inc(mag_done, 1)

            tiles(act, body)
            turned_high(TT - 1)

        @block.tensor
        def _(pe):
            def turn_x(t, b):
                pe.wait_ge(xn_done, t + 1)
                if not static(t) or t >= 1:
                    pe.wait_ge(x_lo_done, t)
                for k in range(KD):
                    last = nc.tensor.transpose(xT_ps[:, k, :], xn[b][:, k * P:(k + 1) * P], ident)
                last.then_inc(x_turned, 1)

            def ups(t, b, c, between=lambda: None):
                pe.wait_ge(x_lo_done, t + 1)
                if not (static(t) and t == 0):
                    pe.wait_ge(silu_done, 2 * t - 1 + c)
                    pe.wait_ge(h_done, 2 * t - 1 + c)
                for n, bank, done in (("gate", gate_ps[c], gate_done), ("up", up_ps[c], up_done)):
                    if static(t) and t == 0 and c == 0:
                        pe.wait_ge(w_lo_done[n], 1)
                    for k in range(KD):
                        cols = slice(c * BANK, (c + 1) * BANK)
                        last = matmul3(nc, bank[:], (xT_hi[b][:, k, :], xT_lo[b][:, k, :]),
                                       (w_hi[n][:, k, cols], w_lo[n][:, k, cols]), start=(k == 0), stop=(k == KD - 1))
                    last.then_inc(done, 1)
                    if n == "gate":
                        between()

            def turn_h(t, b):
                pe.wait_ge(sparse, t + 1)
                if not static(t) or t >= 1:
                    pe.wait_ge(hT_lo_done, 2 * t)
                for c in range(2):
                    for k in range(4):
                        at = (4 * c + k) * P
                        last = nc.tensor.transpose(hT_ps[c][:, k, :], h[b][:, at:at + P], ident)
                    last.then_inc(h_turned, 1)

            def down(t):
                pe.wait_ge(hT_lo_done, 2 * t + 2)
                if static(t) and t == 0:
                    pe.wait_ge(w_lo_done["down"], 1)
                else:
                    pe.wait_ge(added, t)
                for k in range(KF):
                    last = matmul3(nc, out_ps[:], (hT_hi[:, k, :], hT_lo[:, k, :]),
                                   (w_hi["down"][:, k, :], w_lo["down"][:, k, :]), start=(k == 0), stop=(k == KF - 1))
                last.then_inc(out_done, 1)

            def body(t, b):
                first, last = static(t) and t == 0, static(t) and t == TT - 1
                ups(t, b, 0)
                ups(t, b, 1, lambda: None if first else turn_h(t - 1, 1 - b))
                if not last:
                    turn_x(t + 1, 1 - b)
                if not first:
                    down(t - 1)

            turn_x(0, 0)
            tiles(pe, body)
            turn_h(TT - 1, 1)
            down(TT - 1)


HM = 32
PD = 128
NS_ = 128
G = 8
IN = HM * PD
TAPS = 4
CONV_TILES = (IN + 2 * G * NS_) // P
X0, B0, C0, DT0 = IN, 2 * IN, 2 * IN + G * NS_, 2 * IN + 2 * G * NS_
NORM_HEADS = IN // G // PD
NC = S // P
NORM_EPS = 1e-6
MASKED = -1e30


def conv_scalar(nc, out, ps, w, bias):
    return nc.scalar.activation(out, ps, ACT.Identity, bias=bias, scale=w(TAPS - 1))


def conv_tap(nc, out, ps, w, k):
    shift = TAPS - 1 - k
    return nc.vector.scalar_tensor_tensor(out[:, shift:], ps[:, :S - shift], w(k), out[:, shift:], ALU.mult, ALU.add)


def mamba_layer(nc, xres, ident, triangle, mask, in_w, conv_w, conv_b, dt_bias, a_log, d_skip, norm_w, out_w, tag):
    with ExitStack() as ctx:
        sp = Space(nc, ctx, tag)
        keep = dict(
            xhi=sp.sb("xnT_hi", [P, KD, S], F32R), xlo=sp.sb("xnT_lo", [P, KD, S], F32R),
            cT=sp.sb("cT", [P, G, S]),
            b_tok=sp.sb("b_tok", [P, G, NC - 1, NS_]),
            cb=sp.sb("cb", [P, G, NC, P]),
            dt=sp.sb("dt", [P, NC, HM]), ncum=sp.sb("neg_cum", [P, NC, HM]),
            to_end=sp.sb("decay_to_end", [P, NC, HM]), chunk_decay=sp.sb("chunk_decay", [P, NC, HM]),
            cumT=sp.sb("cumT", [P, S], F32R),
            w_conv=sp.sb("w_conv", [P, CONV_TILES, TAPS]), b_conv=sp.sb("b_conv", [P, CONV_TILES]),
            d_skip=sp.sb("d_skip", [P, HM]), norm_w=sp.sb("norm_w", [P, HM]),
        )
        prepare(nc, xres, ident, triangle, in_w, conv_w, conv_b, dt_bias, a_log, d_skip, norm_w, keep, tag + "_prep")
        scan_heads(nc, xres, ident, mask, in_w, out_w, keep, tag + "_scan")


def prepare(nc, xres, ident, triangle, in_w, conv_w, conv_b, dt_bias, a_log, d_skip, norm_w, keep, tag):
    with ExitStack() as ctx:
        sp = Space(nc, ctx, tag)
        cT, b_tok, cb = keep["cT"], keep["b_tok"], keep["cb"]
        dt, ncum, w_conv, b_conv = keep["dt"], keep["ncum"], keep["w_conv"], keep["b_conv"]
        wdt = sp.sb("w_dt", [P, KD, HM])
        wdt_hi = sp.sb("w_dt_hi", [P, KD, HM], F32R)
        wdt_lo = sp.sb("w_dt_lo", [P, KD, HM], F32R)
        bias = sp.sb("dt_bias", [P, HM])
        alog = sp.sb("a_log", [P, HM])
        a = sp.sb("a", [P, HM])
        tri = sp.sb("triangle", [P, P])
        ones = sp.sb("ones", [P, P])
        z = sp.sb("z", [P, NC, HM])
        z2 = sp.sb("z2", [P, NC, HM])
        adt = sp.sb("a_dt", [P, NC, HM])
        total = sp.sb("total", [P, NC, HM])
        cstack = sp.sb("cum_stack", [P, NC, P])
        w_raw = [sp.sb(f"w_bc{b}", [P, KD, 2, P]) for b in range(2)]
        w_hi = [sp.sb(f"w_bc_hi{b}", [P, KD, 2, P], F32R) for b in range(2)]
        w_lo = [sp.sb(f"w_bc_lo{b}", [P, KD, 2, P], F32R) for b in range(2)]
        pre = [sp.sb(f"conv{n}", [P, S]) for n in range(2)]
        bT = [sp.sb(f"bT{b}", [P, S]) for b in range(2)]
        proj_ps = [sp.ps(f"proj{n}", [P, S]) for n in range(2)]
        turn_ps = [sp.ps(f"turn{n}", [P, 4, P]) for n in range(2)]
        cb_ps = [sp.ps(f"cb{n}", [P, 4, P]) for n in range(2)]
        ln = LayerNorm(sp, [turn_ps_flat(t) for t in turn_ps + cb_ps], keep_f32=False, parts=(keep["xhi"], keep["xlo"]))

        small_in, wdt_in, wdt_split = sp.sem("small_in"), sp.sem("w_dt_in"), sp.sem("w_dt_split")
        w_in = [sp.sem(f"w_in{b}") for b in range(2)]
        w_hi_done, w_lo_done = sp.sem("w_hi_done"), sp.sem("w_lo_done")
        dt_mm, cum_mm, cum_turned = sp.sem("dt_mm"), sp.sem("cum_mm"), sp.sem("cum_turned")
        step, act_step, cumT_done = sp.sem("vector_step"), sp.sem("scalar_step"), sp.sem("cumT_done")
        consts = sp.sem("consts")
        projected, first_tap, tapped, silu_done = (sp.sem(n) for n in ("projected", "first_tap", "tapped", "silu_done"))
        b_turned, b_copied, cb_mm, cb_copied = (sp.sem(n) for n in ("b_turned", "b_copied", "cb_mm", "cb_copied"))
        ctx.callback(sp.clear_sems)
        block = ctx.enter_context(nc.Block())

        def edge(g):
            return (isinstance(g, int) and g == 0), (isinstance(g, int) and g == G - 1)

        def is_group(g, k):
            return isinstance(g, int) and g == k

        def groups(eng, body):
            for g in range(3):
                body(g, g % 2)
            with eng.Fori(1, G // 2 - 1) as i:
                for b in (1, 0):
                    body(2 * i + 2 - b, b)
            body(G - 1, 1)

        @block.sync
        def _(sync):
            sync.dma_start(wdt[:], in_w[:, DT0:DT0 + HM].rearrange("(k p) n -> p k n", p=P)).then_inc(wdt_in, 16)
            small = ((bias[:], dt_bias.partition_broadcast(P)), (alog[:], a_log.partition_broadcast(P)),
                     (keep["d_skip"][:], d_skip.partition_broadcast(P)), (tri[:], triangle),
                     (w_conv[:], conv_w), (b_conv[:], conv_b), (keep["norm_w"][:], norm_w))
            for dst, src in small:
                sync.dma_start(dst, src).then_inc(small_in, 16)

            def load(g, b):
                for n, col in enumerate((B0, C0)):
                    src = in_w[:, bass.ds(col + g * NS_, NS_)].rearrange("(k p) n -> p k n", p=P)
                    sync.dma_start(w_raw[b][:, :, n, :], src).then_inc(w_in[b], 16)

            load(0, 0)
            load(1, 1)
            with sync.Fori(0, G // 2 - 1) as i:
                for b in range(2):
                    sync.wait_ge(w_lo_done, 2 * i + b + 1)
                    load(2 * i + b + 2, b)

        @block.gpsimd
        def _(pool):
            nc.gpsimd.memset(ones[:], 1.0).then_inc(consts, 1)
            nc.gpsimd.memset(cstack[:], 0.0).then_inc(consts, 1)
            pool.wait_ge(wdt_split, 1)
            nc.gpsimd.tensor_tensor(wdt_lo[:], wdt[:], f32(wdt_hi[:]), ALU.subtract).then_inc(wdt_split, 1)

            def low(g, b):
                pool.wait_ge(w_hi_done, g + 1)
                nc.gpsimd.tensor_tensor(w_lo[b][:], w_raw[b][:], f32(w_hi[b][:]), ALU.subtract).then_inc(w_lo_done, 1)

            with pool.Fori(0, G // 2) as i:
                for b in range(2):
                    low(2 * i + b, b)

        @block.vector
        def _(dve):
            ln.vector(nc, xres)
            heads = [P, NC, HM]
            n = 0

            def then(ins):
                nonlocal n
                n += 1
                ins.then_inc(step, 1)
                dve.wait_ge(step, n)

            def step_sizes():
                dve.wait_ge(small_in, 7 * 16)
                dve.wait_ge(dt_mm, 1)
                then(nc.vector.tensor_tensor(z[:], cb_ps[0][:, 0:2, :].rearrange("p c (e h) -> p (c e) h", h=HM),
                                             bias[:].unsqueeze(1).broadcast_to(heads), ALU.add))
                then(nc.vector.scalar_tensor_tensor(z2[:], z[:], -1.0, z[:], ALU.mult, ALU.min))
                dve.wait_ge(act_step, 2)
                then(nc.vector.scalar_tensor_tensor(dt[:], z[:], 0.0, z2[:], ALU.max, ALU.add))
                then(nc.vector.scalar_tensor_tensor(adt[:], dt[:], -1.0, a[:].unsqueeze(1).broadcast_to(heads), ALU.mult, ALU.mult))

            def decays():
                dve.wait_ge(cum_mm, 1)
                flat = cb_ps[1][:].rearrange("p c n -> p (c n)")
                cum = flat[:, 0:NC * HM].rearrange("p (c h) -> p c h", h=HM)
                tot = flat[:, NC * HM:2 * NC * HM].rearrange("p (c h) -> p c h", h=HM)
                dve.wait_ge(consts, 2)
                then(nc.vector.tensor_scalar(ncum[:], cum, -1.0, None, ALU.mult))
                nc.vector.tensor_copy(total[:], tot)
                nc.vector.tensor_copy(cstack[:, :, 0:HM].bitcast(F32R), cum)
                then(nc.vector.tensor_tensor(z2[:], tot, ncum[:], ALU.add))
                then(nc.vector.tensor_tensor(cstack[:, :, HM:2 * HM], cum, cstack[:, :, 0:HM], ALU.subtract))

            def w(tile):
                return lambda k: w_conv[:, bass.ds(tile, 1), k]

            def taps(g, n):
                tile = HM + G * n + g
                for k in (2, 1, 0):
                    dve.wait_ge(first_tap, 2 * g + n + 1) if k == 2 else dve.wait_ge(tapped, 6 * g + 3 * n + 2 - k)
                    conv_tap(nc, pre[n][:], proj_ps[n][:], w(tile), k).then_inc(tapped, 1)

            def body(g, b):
                taps(g, 0)
                if is_group(g, 1):
                    decays()
                taps(g, 1)
                if is_group(g, 0):
                    step_sizes()

            groups(dve, body)
            dve.wait_ge(step, 7)

        @block.scalar
        def _(act):
            act.wait_ge(wdt_in, 16)
            nc.scalar.copy(wdt_hi[:], wdt[:]).then_inc(wdt_split, 1)

            def high(g, b):
                act.wait_ge(w_in[b], 32 * (g // 2 + 1) if isinstance(g, int) else 16 * (g - b) + 32)
                if not isinstance(g, int) or g >= 2:
                    act.wait_ge(projected, 2 * (g - 1))
                nc.scalar.copy(w_hi[b][:], w_raw[b][:]).then_inc(w_hi_done, 1)

            ln.scalar(nc, before_copies=lambda: high(0, 0))
            act.wait_ge(small_in, 7 * 16)

            def step_sizes():
                act.wait_ge(step, 2)
                nc.scalar.activation(z2[:], z2[:], ACT.Exp).then_inc(act_step, 1)
                act.wait_ge(consts, 1)
                act.wait_ge(act_step, 1)
                nc.scalar.activation(a[:], alog[:], ACT.Exp)
                nc.scalar.activation(z2[:], z2[:], ACT.Ln, bias=ones[:, 0:1]).then_inc(act_step, 1)

            def decays():
                act.wait_ge(step, 6)
                nc.scalar.activation(keep["to_end"][:], z2[:], ACT.Exp)
                nc.scalar.activation(keep["chunk_decay"][:], total[:], ACT.Exp)
                for half in range(2):
                    act.wait_ge(cum_turned, half + 1)
                    nc.scalar.copy(keep["cumT"][:, half * BANK:(half + 1) * BANK],
                                   turn_ps[half][:].rearrange("p c n -> p (c n)")).then_inc(cumT_done, 1)

            def tap(g, n):
                tile = HM + G * n + g
                act.wait_ge(projected, 2 * g + n + 1)
                if not edge(g)[0]:
                    act.wait_ge(silu_done, 2 * g - 1 + n)
                conv_scalar(nc, pre[n][:].unsqueeze(1), proj_ps[n][:].unsqueeze(1), lambda k: w_conv[:, bass.ds(tile, 1), k],
                            b_conv[:, bass.ds(tile, 1)]).then_inc(first_tap, 1)

            def silu(g, b, n):
                act.wait_ge(tapped, 6 * g + 3 * n + 3)
                if n == 0:
                    if not isinstance(g, int) or g >= 2:
                        act.wait_ge(cb_mm, 2 * (g - 1))
                    out = bT[b][:].unsqueeze(1)
                else:
                    out = cT[:, bass.ds(g, 1), :]
                nc.scalar.activation(out, pre[n][:].unsqueeze(1), ACT.Silu).then_inc(silu_done, 1)

            def copy_b(g):
                for half in range(2):
                    act.wait_ge(b_turned, 2 * g + half + 1)
                    c = 4 - half
                    nc.scalar.copy(b_tok[:, bass.ds(g, 1), 4 * half:4 * half + c, :],
                                   turn_ps[half][:, 0:c, :].unsqueeze(1)).then_inc(b_copied, 1)

            def copy_cb(g):
                for half in range(2):
                    act.wait_ge(cb_mm, 2 * g + half + 1)
                    nc.scalar.copy(cb[:, bass.ds(g, 1), 4 * half:4 * half + 4, :], cb_ps[half][:].unsqueeze(1)).then_inc(cb_copied, 1)

            def body(g, b):
                first, last = edge(g)
                tap(g, 0)
                if not first:
                    silu(g - 1, 1 - b, 1)
                tap(g, 1)
                if not last:
                    high(g + 1, 1 - b)
                if not first:
                    copy_b(g - 1)
                if is_group(g, 1):
                    decays()
                silu(g, b, 0)
                if not first:
                    copy_cb(g - 1)
                if first:
                    step_sizes()

            groups(act, body)
            silu(G - 1, 1, 1)
            copy_b(G - 1)
            copy_cb(G - 1)

        @block.tensor
        def _(pe):
            ln.tensor(nc, ident)
            def project(g, b, n):
                pe.wait_ge(w_lo_done, g + 1)
                pe.wait_ge(tapped, 6 * g - 3 + 3 * n) if not edge(g)[0] else None
                for half in range(2):
                    cols = slice(half * BANK, (half + 1) * BANK)
                    if edge(g)[0]:
                        ln.ready(pe, cols.stop)
                    for k in range(KD):
                        last = matmul3(nc, proj_ps[n][:, cols], (w_hi[b][:, k, n, :], w_lo[b][:, k, n, :]),
                                       ln.parts(k, cols), start=(k == 0), stop=(k == KD - 1))
                last.then_inc(projected, 1)

            def turn_b(g, b):
                pe.wait_ge(silu_done, 2 * g + 1)
                if is_group(g, 1):
                    pe.wait_ge(cumT_done, 2)
                elif not edge(g)[0]:
                    pe.wait_ge(b_copied, 2 * g)
                for half in range(2):
                    for c in range(4 - half):
                        at = (4 * half + c) * P
                        last = nc.tensor.transpose(turn_ps[half][:, c, :], bT[b][:, at:at + P], ident)
                    last.then_inc(b_turned, 1)

            def products(g, b):
                pe.wait_ge(silu_done, 2 * g + 2)
                if not edge(g)[0]:
                    pe.wait_ge(cb_copied, 2 * g)
                for half in range(2):
                    for c in range(4):
                        at = (4 * half + c) * P
                        last = nc.tensor.matmul(cb_ps[half][:, c, :].unsqueeze(1), bT[b][:, at:at + P],
                                                cT[:, bass.ds(g, 1), at:at + P], start=True, stop=True)
                    last.then_inc(cb_mm, 1)

            def step_sizes():
                pe.wait_ge(wdt_split, 2)
                flat = cb_ps[0][:].rearrange("p c n -> p (c n)")
                for c in range(NC):
                    for k in range(KD):
                        last = matmul3(nc, flat[:, c * HM:(c + 1) * HM], ln.parts(k, slice(c * P, (c + 1) * P)),
                                       (wdt_hi[:, k, :], wdt_lo[:, k, :]), start=(k == 0), stop=(k == KD - 1))
                last.then_inc(dt_mm, 1)

            def running_sums():
                pe.wait_ge(consts, 1)
                pe.wait_ge(step, 4)
                flat = cb_ps[1][:].rearrange("p c n -> p (c n)")
                rhs = adt[:].rearrange("p c h -> p (c h)")
                nc.tensor.matmul(flat[:, 0:NC * HM], tri[:], rhs, start=True, stop=True)
                nc.tensor.matmul(flat[:, NC * HM:2 * NC * HM], ones[:], rhs, start=True, stop=True).then_inc(cum_mm, 1)

            def turn_sums():
                pe.wait_ge(step, 7)
                pe.wait_ge(b_copied, 2)
                for half in range(2):
                    for c in range(4):
                        last = nc.tensor.transpose(turn_ps[half][:, c, :], cstack[:, 4 * half + c, :], ident)
                    last.then_inc(cum_turned, 1)

            def body(g, b):
                first, last = edge(g)
                project(g, b, 0)
                if is_group(g, 1):
                    running_sums()
                if not first:
                    turn_b(g - 1, 1 - b)
                project(g, b, 1)
                if is_group(g, 1):
                    turn_sums()
                if not first:
                    products(g - 1, 1 - b)
                if first:
                    step_sizes()

            groups(pe, body)
            turn_b(G - 1, 1)
            products(G - 1, 1)


def turn_ps_flat(t):
    return t[:].rearrange("p c n -> p (c n)")


def scan_heads(nc, xres, ident, mask, in_w, out_w, keep, tag):
    with ExitStack() as ctx:
        sp = Space(nc, ctx, tag)
        xhi, xlo, cT, b_tok, cb = (keep[n] for n in ("xhi", "xlo", "cT", "b_tok", "cb"))
        dt, ncum, to_end, chunk_decay = (keep[n] for n in ("dt", "ncum", "to_end", "chunk_decay"))
        cumT, w_conv, b_conv, d_skip, norm_w = (keep[n] for n in ("cumT", "w_conv", "b_conv", "d_skip", "norm_w"))
        w_hi = [sp.sb(f"w_in_hi{b}", [P, KD, 2, P], F32R) for b in range(2)]
        w_lo = [sp.sb(f"w_in_lo{b}", [P, KD, 2, P], F32R) for b in range(2)]
        w_raw = sp.sb("w_in", [P, KD, 2, P])
        w_out = sp.sb("w_out", [P, NORM_HEADS, D])
        xs = [sp.sb(f"x{b}", [P, S]) for b in range(2)]
        gs = [sp.sb(f"gate{b}", [P, S]) for b in range(2)]
        xdt = sp.sb("x_dt", [P, NC, PD])
        xend = sp.sb("x_to_end", [P, NC - 1, PD])
        sel = sp.sb("select", [P, P], F32R)
        grow = sp.sb("exp_cum", [P, S])
        cgrow = sp.sb("c_exp_cum", [P, S - P])
        decay = sp.sb("decay", [P, NC, P])
        states = sp.sb("states", [P, NC - 1, PD])
        v = sp.sb("v", [P, NORM_HEADS + 2, S])
        squares = sp.sb("squares", [P, S])
        ones = sp.sb("ones", [P, 2])
        eps = sp.sb("eps", [P, 1])
        sums = sp.sb("sums", [P, TT])
        std = sp.sb("std", [P, TT])
        rnorm = sp.sb("rnorm", [P, TT])
        bmask = sp.sb("mask", [P, P], BF16)
        bident = sp.sb("ident_bf16", [P, P], BF16)
        mask_f32 = decay[:, 0, :]
        proj_ps = sp.ps("proj", [P, S])
        turn_ps = [sp.ps(f"turn{n}", [P, 4, P]) for n in range(2)]
        y_ps = sp.ps("y", [P, S])
        cum_ps = sp.ps("cum", [P, 4, P])
        out_ps = sp.ps("out", [P, 2, D])

        tail_ps = [out_ps] + [proj_ps[:, n * BANK:(n + 1) * BANK].rearrange("p (m d) -> p m d", m=2) for n in range(2)]
        tail_ps.append(cum_ps[:].rearrange("p (m c) n -> p m (c n)", m=2))

        names = ("w_hi_done", "w_lo_done", "w_out_scaled", "consts", "selected", "x_projected", "first_tap", "tapped",
                 "x_done", "gate_projected", "gate_done", "x_turned", "xdt_done", "xend_done", "cum_spread",
                 "grow_done", "cum_masked", "decay_done", "cgrow_done", "weighed", "in_chunk", "state_mm",
                 "state_done", "y_mm", "y_done", "v_done", "squared", "summed", "norm_mm", "sums_done", "std_done",
                 "rnorm_done", "out_mm", "added")
        q = {n: sp.sem(n) for n in names}
        w_in = [sp.sem(f"w_in{b}") for b in range(2)]
        w_out_in = sp.sem("w_out_in")
        mask_in = sp.sem("mask_in")
        ctx.callback(sp.clear_sems)
        block = ctx.enter_context(nc.Block())
        LAST = HM - 1
        PAIRS = TT // 2
        OUT_PAIRS = ((0, None), (1, 2), (3, None), (None, None))
        SUMS = NORM_HEADS - 1

        def is_at(n, k):
            return isinstance(n, int) and n == k

        def after(n, k):
            return not isinstance(n, int) or n >= k

        def v_row(j):
            jn = j % NORM_HEADS
            return jn + 2 if jn >= 2 else 2 * (j // NORM_HEADS) + jn

        def heads(eng, body):
            for n in range(G):
                body(n, n, n // NORM_HEADS)
            with eng.Fori(1, HM // G - 1) as i:
                for j in range(G):
                    body(i * G + j, j, i * (G // NORM_HEADS) + j // NORM_HEADS)
            for n in range(HM - G, HM):
                body(n, n % G, n // NORM_HEADS)

        @block.sync
        def _(sync):
            sync.dma_start(mask_f32, mask).then_inc(mask_in, 16)

            def load(n, b):
                if after(n, 1):
                    sync.wait_ge(q["w_lo_done"], n)
                for m, col in enumerate((X0, 0)):
                    src = in_w[:, bass.ds(col + n * PD, PD)].rearrange("(k p) n -> p k n", p=P)
                    sync.dma_start(w_raw[:, :, m, :], src).then_inc(w_in[b], 16)

            def load_out(gw):
                if after(gw, 1):
                    sync.wait_ge(q["out_mm"], PAIRS * gw)
                src = out_w[bass.ds(gw * NORM_HEADS * PD, NORM_HEADS * PD), :].rearrange("(j p) d -> p j d", p=P)
                sync.dma_start(w_out[:], src).then_inc(w_out_in, 16)

            for n in range(G):
                load(n, n % 2)
                if n == NORM_HEADS + 1:
                    load_out(0)
            with sync.Fori(1, HM // G) as i:
                for j in range(G):
                    load(i * G + j, j % 2)
                    if j % NORM_HEADS == 1:
                        load_out(2 * i - 1 + j // NORM_HEADS)
            load_out(G - 1)

        @block.gpsimd
        def _(pool):
            nc.gpsimd.memset(ones[:], 1.0).then_inc(q["consts"], 1)
            nc.gpsimd.memset(eps[:], NORM_EPS).then_inc(q["consts"], 1)
            nc.gpsimd.tensor_copy(bident[:], ident).then_inc(q["consts"], 1)
            pool.wait_ge(mask_in, 16)
            nc.gpsimd.tensor_copy(bmask[:], mask_f32).then_inc(q["consts"], 1)

            def low(n, b):
                pool.wait_ge(q["w_hi_done"], n + 1)
                nc.gpsimd.tensor_tensor(w_lo[b][:], w_raw[:], f32(w_hi[b][:]), ALU.subtract).then_inc(q["w_lo_done"], 1)

            def select(n):
                if after(n, 1):
                    pool.wait_ge(q["cum_spread"], 2 * n)
                nc.gpsimd.tensor_tensor(sel[:], ident[:, bass.ds(n, 1)].broadcast_to([P, P]),
                                        ident[:, bass.ds(n + HM, 1)].broadcast_to([P, P]), ALU.add).then_inc(q["selected"], 1)

            def cgrow_of(n, g):
                pool.wait_ge(q["grow_done"], 2 * n + 2)
                if after(n, 1):
                    pool.wait_ge(q["y_mm"], n)
                nc.gpsimd.tensor_tensor(cgrow[:], cT[:, g, P:], grow[:, P:], ALU.mult).then_inc(q["cgrow_done"], 1)

            def xend_of(n):
                if after(n, 1):
                    pool.wait_ge(q["state_mm"], n)
                for half in range(2):
                    cs = slice(4 * half, min(4 * half + 4, NC - 1))
                    pool.wait_ge(q["xdt_done"], 2 * n + half + 1)
                    nc.gpsimd.tensor_tensor(xend[:, cs, :], xdt[:, cs, :], to_end[:, cs, bass.ds(n, 1)]
                                            .broadcast_to([P, cs.stop - cs.start, PD]), ALU.mult).then_inc(q["xend_done"], 1)

            def sum_squares(n, j, gw):
                jn = j % NORM_HEADS
                if jn:
                    pool.wait_ge(q["squared"], n + 1)
                    pool.wait_ge(q["summed"], SUMS * gw + jn - 1)
                    nc.gpsimd.tensor_tensor(squares[:], squares[:], gs[j % 2][:], ALU.add).then_inc(q["summed"], 1)

            def scale_out(gw):
                pool.wait_ge(w_out_in, 16 * (gw + 1))
                nc.gpsimd.tensor_tensor(w_out[:], w_out[:], norm_w[:, bass.ds(gw * NORM_HEADS, NORM_HEADS)]
                                        .unsqueeze(2).broadcast_to([P, NORM_HEADS, D]), ALU.mult).then_inc(q["w_out_scaled"], 1)

            def body(n, j, gw):
                if not (is_at(n, LAST) or is_at(n, LAST - 1)):
                    low(n + 2, j % 2)
                    select(n + 2)
                if j % NORM_HEADS == NORM_HEADS - 1:
                    scale_out(gw)
                if not is_at(n, LAST):
                    cgrow_of(n + 1, (j + 1) % G)
                    xend_of(n + 1)
                sum_squares(n, j, gw)

            low(0, 0)
            low(1, 1)
            select(0)
            cgrow_of(0, 0)
            select(1)
            xend_of(0)
            heads(pool, body)

        @block.vector
        def _(dve):
            def w(n):
                return lambda k: w_conv[:, bass.ds(n, 1), k]

            def tap(n, j, k):
                if k == 2:
                    dve.wait_ge(q["first_tap"], n + 1)
                else:
                    dve.wait_ge(q["tapped"], 3 * n + 2 - k)
                conv_tap(nc, xs[j % 2][:], proj_ps[:], w(n), k).then_inc(q["tapped"], 1)

            def scale_x(n):
                for half in range(2):
                    dve.wait_ge(q["x_turned"], 2 * n + half + 1)
                    if after(n, 1):
                        dve.wait_ge(q["state_mm"], n)
                        dve.wait_ge(q["xend_done"], 2 * n)
                    nc.vector.tensor_tensor(xdt[:, 4 * half:4 * half + 4, :], turn_ps[half][:],
                                            dt[:, 4 * half:4 * half + 4, bass.ds(n, 1)].broadcast_to([P, 4, PD]),
                                            ALU.mult).then_inc(q["xdt_done"], 1)

            def weigh(n, g, half):
                cs = slice(4 * half, 4 * half + 4)
                dve.wait_ge(q["decay_done"], 2 * n + half + 1)
                nc.vector.tensor_tensor(decay[:, cs, :], decay[:, cs, :], cb[:, g, cs, :], ALU.mult).then_inc(q["weighed"], 1)

            def scan_state(n, c):
                new = turn_ps[c // 4][:, c % 4, :]
                if c == 0:
                    dve.wait_ge(q["state_mm"], n + 1)
                    if after(n, 1):
                        dve.wait_ge(q["y_mm"], n)
                    nc.vector.tensor_copy(states[:, 0, :], new).then_inc(q["state_done"], 1)
                else:
                    dve.wait_ge(q["state_done"], (NC - 1) * n + c)
                    nc.vector.scalar_tensor_tensor(states[:, c, :], states[:, c - 1, :],
                                                   chunk_decay[:, c, bass.ds(n, 1)], new,
                                                   ALU.mult, ALU.add).then_inc(q["state_done"], 1)

            def finish(n, j, gw):
                b, jn = j % 2, j % NORM_HEADS
                dve.wait_ge(q["y_mm"], n + 1)
                nc.vector.scalar_tensor_tensor(xs[b][:], xs[b][:], d_skip[:, bass.ds(n, 1)], y_ps[:],
                                               ALU.mult, ALU.add).then_inc(q["y_done"], 1)
                dve.wait_ge(q["y_done"], n + 1)
                dve.wait_ge(q["gate_done"], n + 1)
                if jn == 2 and after(gw, 1):
                    dve.wait_ge(q["out_mm"], PAIRS * gw)
                nc.vector.tensor_tensor(v[:, v_row(j), :], xs[b][:], gs[b][:], ALU.mult).then_inc(q["v_done"], 1)

            def copy_sums(gw):
                dve.wait_ge(q["norm_mm"], gw + 1)
                if after(gw, 1):
                    dve.wait_ge(q["std_done"], gw)
                nc.vector.tensor_copy(sums[:], turn_ps[1][:, 3, 0:TT]).then_inc(q["sums_done"], 1)

            def norm(gw):
                dve.wait_ge(q["std_done"], gw + 1)
                nc.vector.reciprocal(rnorm[:], std[:]).then_inc(q["rnorm_done"], 1)
                dve.wait_ge(q["rnorm_done"], gw + 1)

            def add_out(gw, p, out=out_ps):
                if p is None:
                    return
                dve.wait_ge(q["out_mm"], PAIRS * gw + p + 1)
                for m in range(2):
                    t = 2 * p + m
                    last = nc.vector.scalar_tensor_tensor(xres[:, t, :], out[:, m, :], rnorm[:, t:t + 1],
                                                          xres[:, t, :], ALU.mult, ALU.add)
                last.then_inc(q["added"], 1)

            def body(n, j, gw):
                pairs = OUT_PAIRS[j % NORM_HEADS] if after(gw, 1) else (None, None)
                more = not is_at(n, LAST)
                if more:
                    tap(n + 1, j + 1, 2)
                    tap(n + 1, j + 1, 1)
                for c in range(NC - 1):
                    scan_state(n, c)
                    if more and c == 1:
                        tap(n + 1, j + 1, 0)
                    if more and c == 3:
                        weigh(n + 1, (j + 1) % G, 0)
                if pairs[0] == 0:
                    copy_sums(gw - 1)
                if pairs[1] is not None:
                    add_out(gw - 1, pairs[0])
                if more:
                    weigh(n + 1, (j + 1) % G, 1)
                finish(n, j, gw)
                if not is_at(n, LAST):
                    scale_x(n + 1)
                if pairs[0] == 0:
                    norm(gw - 1)
                add_out(gw - 1, pairs[0] if pairs[1] is None else pairs[1])

            for k in (2, 1, 0):
                tap(0, 0, k)
            scale_x(0)
            for half in range(2):
                weigh(0, 0, half)
            heads(dve, body)
            copy_sums(G - 1)
            norm(G - 1)
            for p in range(PAIRS):
                add_out(G - 1, p, tail_ps[p])
            dve.wait_ge(q["added"], PAIRS * G)

        @block.scalar
        def _(act):
            def high(n, b):
                act.wait_ge(w_in[b], 32 * (n // 2 + 1) if isinstance(n, int) else 16 * (n - b) + 32)
                if after(n, 2):
                    act.wait_ge(q["gate_projected"], n - 1)
                nc.scalar.copy(w_hi[b][:], w_raw[:]).then_inc(q["w_hi_done"], 1)

            def tap(n, j):
                act.wait_ge(q["x_projected"], n + 1)
                if after(n, 2):
                    act.wait_ge(q["v_done"], n - 1)
                conv_scalar(nc, xs[j % 2][:].unsqueeze(1), proj_ps[:].unsqueeze(1), lambda k: w_conv[:, bass.ds(n, 1), k],
                            b_conv[:, bass.ds(n, 1)]).then_inc(q["first_tap"], 1)

            def x_of(n, j):
                act.wait_ge(q["tapped"], 3 * n + 3)
                nc.scalar.activation(xs[j % 2][:], xs[j % 2][:], ACT.Silu).then_inc(q["x_done"], 1)

            def gate_of(n, j, gw):
                act.wait_ge(q["gate_projected"], n + 1)
                jn2 = (j - 2) % NORM_HEADS
                if after(n, 2):
                    if jn2 == 0:
                        act.wait_ge(q["v_done"], n - 1)
                    else:
                        act.wait_ge(q["summed"], SUMS * (gw - (j % NORM_HEADS < 2)) + jn2)
                nc.scalar.activation(gs[j % 2][:], proj_ps[:], ACT.Silu).then_inc(q["gate_done"], 1)

            def grow_of(n, half):
                act.wait_ge(q["cum_spread"], 2 * n + half + 1)
                if after(n, 1):
                    act.wait_ge(q["cgrow_done"], n)
                nc.scalar.activation(grow[:, half * BANK:(half + 1) * BANK], cum_ps[:].rearrange("p c n -> p (c n)"),
                                     ACT.Exp).then_inc(q["grow_done"], 1)

            def decay_of(n, half):
                act.wait_ge(q["cum_masked"], 2 * n + half + 1)
                if after(n, 1):
                    act.wait_ge(q["in_chunk"], n)
                for c in range(4):
                    m = 4 * half + c
                    last = nc.scalar.activation(decay[:, m, :], cum_ps[:, c, :], ACT.Exp, bias=ncum[:, m, bass.ds(n, 1)])
                last.then_inc(q["decay_done"], 1)

            def square(n, j, gw):
                jn = j % NORM_HEADS
                act.wait_ge(q["v_done"], n + 1)
                if jn == 0 and after(n, 1):
                    act.wait_ge(q["norm_mm"], gw)
                nc.scalar.activation((gs[j % 2] if jn else squares)[:], v[:, v_row(j), :], ACT.Square).then_inc(q["squared"], 1)

            def norm(gw):
                act.wait_ge(q["sums_done"], gw + 1)
                if after(gw, 1):
                    act.wait_ge(q["rnorm_done"], gw)
                nc.scalar.activation(std[:], sums[:], ACT.Sqrt, bias=eps[:], scale=1.0 / (NORM_HEADS * PD)).then_inc(q["std_done"], 1)

            def ahead(n, j, gw, norm_of=None):
                tap(n, j)
                for half in range(2):
                    grow_of(n, half)
                    decay_of(n, half)
                if norm_of is not None:
                    norm(norm_of)
                if after(n, 1) and not is_at(n, LAST):
                    high(n + 1, 1 - j % 2)
                x_of(n, j)
                gate_of(n, j, gw)

            def body(n, j, gw):
                if not is_at(n, LAST):
                    ahead(n + 1, j + 1, gw + (j % NORM_HEADS == NORM_HEADS - 1), gw - 1 if j % NORM_HEADS == 0 and after(n, 1) else None)
                square(n, j, gw)

            high(0, 0)
            high(1, 1)
            act.wait_ge(q["consts"], 4)
            ahead(0, 0, 0)
            heads(act, body)
            norm(G - 1)

        @block.tensor
        def _(pe):
            def project(n, j, m):
                b = j % 2
                if m == 0:
                    pe.wait_ge(q["w_lo_done"], n + 1)
                    if after(n, 1):
                        pe.wait_ge(q["gate_done"], n)
                else:
                    pe.wait_ge(q["tapped"], 3 * n + 3)
                for half in range(2):
                    cols = slice(half * BANK, (half + 1) * BANK)
                    for k in range(KD):
                        last = matmul3(nc, proj_ps[:, cols], (w_hi[b][:, k, m, :], w_lo[b][:, k, m, :]),
                                       (xhi[:, k, cols], xlo[:, k, cols]), start=(k == 0), stop=(k == KD - 1))
                last.then_inc(q[("x_projected", "gate_projected")[m]], 1)

            def spread(n, half):
                if half == 0:
                    pe.wait_ge(q["selected"], n + 1)
                if half or after(n, 1):
                    pe.wait_ge(q["decay_done"], 2 * n + half)
                nc.tensor.matmul(cum_ps[:].rearrange("p c n -> p (c n)"), sel[:], cumT[:, half * BANK:(half + 1) * BANK],
                                 start=True, stop=True).then_inc(q["cum_spread"], 1)

            def mask_out(n, half):
                pe.wait_ge(q["grow_done"], 2 * n + half + 1)
                nc.tensor.matmul(cum_ps[:], bident[:], bmask[:].unsqueeze(1).broadcast_to([P, 4, P]),
                                 start=False, stop=True, skip_group_check=True).then_inc(q["cum_masked"], 1)

            def turn(n, j, gw):
                pe.wait_ge(q["x_done"], n + 1)
                if after(gw, 1) and (j - 1) % NORM_HEADS == 0:
                    pe.wait_ge(q["sums_done"], gw)
                if after(n, 1):
                    pe.wait_ge(q["state_done"], (NC - 1) * n)
                for half in range(2):
                    for c in range(4):
                        at = (4 * half + c) * P
                        last = nc.tensor.transpose(turn_ps[half][:, c, :], xs[j % 2][:, at:at + P], ident)
                    last.then_inc(q["x_turned"], 1)

            def in_chunks(n):
                if after(n, 1):
                    pe.wait_ge(q["y_done"], n)
                for c in range(NC):
                    if c % 4 == 0:
                        pe.wait_ge(q["weighed"], 2 * n + c // 4 + 1)
                        pe.wait_ge(q["xdt_done"], 2 * n + c // 4 + 1)
                    last = nc.tensor.matmul(y_ps[:, c * P:(c + 1) * P], xdt[:, c, :], decay[:, c, :],
                                            start=(c % 4 == 0), stop=False, skip_group_check=True)
                last.then_inc(q["in_chunk"], 1)

            def new_states(n, g, sums_of):
                for c in range(NC - 1):
                    if c % 4 == 0:
                        pe.wait_ge(q["xend_done"], 2 * n + c // 4 + 1)
                    if c == NC - 2 and sums_of is not None:
                        norm_sums(sums_of)
                    last = nc.tensor.matmul(turn_ps[c // 4][:, c % 4, :], b_tok[:, g, c, :], xend[:, c, :],
                                            start=True, stop=True)
                last.then_inc(q["state_mm"], 1)

            def from_states(n):
                pe.wait_ge(q["state_done"], (NC - 1) * (n + 1))
                pe.wait_ge(q["cgrow_done"], n + 1)
                for c in range(1, NC):
                    last = nc.tensor.matmul(y_ps[:, c * P:(c + 1) * P], states[:, c - 1, :], cgrow[:, (c - 1) * P:c * P],
                                            start=False, stop=True, skip_group_check=True)
                last.then_inc(q["y_mm"], 1)

            def norm_sums(gw):
                pe.wait_ge(q["summed"], SUMS * (gw + 1))
                for t in range(TT):
                    last = nc.tensor.matmul(turn_ps[1][:, 3, t:t + 1], squares[:, t * P:(t + 1) * P], ones[:, 0:1],
                                            start=True, stop=True)
                last.then_inc(q["norm_mm"], 1)

            def project_out(gw, b, p, m, out=out_ps):
                if p is None:
                    return
                if p == 0 and m == 0:
                    pe.wait_ge(q["w_out_scaled"], gw + 1)
                    pe.wait_ge(q["v_done"], NORM_HEADS * (gw + 1))
                if m == 0 and out is out_ps and (p or after(gw, 1)):
                    pe.wait_ge(q["added"], PAIRS * gw + p)
                cols = slice((2 * p + m) * P, (2 * p + m + 1) * P)
                for jn in range(NORM_HEADS):
                    last = nc.tensor.matmul(out[:, m, :], v[:, v_row(b * NORM_HEADS + jn), cols],
                                            w_out[:, jn, :], start=(jn == 0), stop=(jn == NORM_HEADS - 1))
                if m == 1:
                    last.then_inc(q["out_mm"], 1)

            def body(n, j, gw):
                b = (j // NORM_HEADS + 1) % 2
                pairs = OUT_PAIRS[j % NORM_HEADS] if after(gw, 1) else (None, None)
                more = not is_at(n, LAST)
                if more:
                    project(n + 1, j + 1, 0)
                    spread(n + 1, 0)
                in_chunks(n)
                new_states(n, j, gw - 1 if pairs[0] == 0 else None)
                if more:
                    mask_out(n + 1, 0)
                project_out(gw - 1, b, pairs[0], 0)
                if more:
                    spread(n + 1, 1)
                project_out(gw - 1, b, pairs[0], 1)
                if more:
                    mask_out(n + 1, 1)
                    project(n + 1, j + 1, 1)
                for m in range(2):
                    project_out(gw - 1, b, pairs[1], m)
                from_states(n)
                if more:
                    turn(n + 1, j + 1, gw)

            pe.wait_ge(q["consts"], 4)
            project(0, 0, 0)
            for half in range(2):
                spread(0, half)
                mask_out(0, half)
            project(0, 0, 1)
            turn(0, 0, 0)
            heads(pe, body)
            for p in range(PAIRS):
                for m in range(2):
                    project_out(G - 1, (G - 1) % 2, p, m, tail_ps[p])
                if p == 0:
                    norm_sums(G - 1)


def macaron_kernel(nc, x, out, ident_in, triangle, mask, places, cos_t, sin_t, moe_gate, moe_w1, moe_w3, moe_w2,
                   w_qkv, w_o, ffn_gate, ffn_up, ffn_down, in_w, conv_w, conv_b, dt_bias, a_log, d_skip, norm_w, out_w):
    with ExitStack() as ctx:
        sp = Space(nc, ctx, "main")
        xres = sp.sb("residual", [P, TT, D])
        ident = sp.sb("ident", [P, P])
        iota8 = sp.sb("places", [P, EXPERTS])
        loaded, stored = sp.sem("loaded"), sp.sem("stored")
        with nc.Block() as block:
            @block.sync
            def _(sync):
                sync.dma_start(xres[:], x.rearrange("b (t p) d -> p (b t) d", p=P)).then_inc(loaded, 16)
                sync.dma_start(ident[:], ident_in).then_inc(loaded, 16)
                sync.dma_start(iota8[:], places.partition_broadcast(P)).then_inc(loaded, 16)
                sync.wait_ge(loaded, 48)

        moe_layer(nc, xres[:], ident[:], iota8[:], moe_gate, moe_w1, moe_w3, moe_w2, "moe0")
        attention_layer(nc, xres[:], ident[:], cos_t, sin_t, w_qkv, w_o, "attn")
        moe_layer(nc, xres[:], ident[:], iota8[:], moe_gate, moe_w1, moe_w3, moe_w2, "moe1")
        sparse_ffn_layer(nc, xres[:], ident[:], ffn_gate, ffn_up, ffn_down, "ffn0")
        mamba_layer(nc, xres[:], ident[:], triangle, mask, in_w, conv_w, conv_b, dt_bias, a_log, d_skip, norm_w,
                    out_w, "ssm")
        sparse_ffn_layer(nc, xres[:], ident[:], ffn_gate, ffn_up, ffn_down, "ffn1")

        with nc.Block() as block:
            @block.sync
            def _(sync):
                sync.dma_start(out.rearrange("b (t p) d -> p (b t) d", p=P), xres[:]).then_inc(stored, 16)
                sync.wait_ge(stored, 16)


def kernel(**inputs):
    import numpy as np
    import concourse.bacc as bacc
    from concourse.bass_utils import run_bass_kernel_spmd

    given = {name: np.asarray(value) for name, value in inputs.items()}
    rows = np.arange(P, dtype=np.float32)
    half = np.arange(ROT, dtype=np.float32)
    inv_freq = (np.float32(1.0) / np.float32(10000.0) ** (half / np.float32(ROT))).astype(np.float32)
    angle = np.arange(S, dtype=np.float32)[:, None] * inv_freq[None, :]
    arrays = {
        "x": given["L0_attn_x"],
        "identity": np.eye(P, dtype=np.float32),
        "triangle": (rows[:, None] <= rows[None, :]).astype(np.float32),
        "mask": np.where(rows[None, :] < rows[:, None], np.float32(MASKED), np.float32(0.0)),
        "places": np.arange(EXPERTS, dtype=np.float32),
        "cos": np.cos(angle), "sin": np.sin(angle),
        "moe_gate": given["L0_ffn_w_gate"], "moe_w1": given["L0_ffn_w1"], "moe_w3": given["L0_ffn_w3"],
        "moe_w2": given["L0_ffn_w2"],
        "w_qkv": np.concatenate([given["L0_attn_Wq"], given["L0_attn_Wk"], given["L0_attn_Wv"]], axis=0).T,
        "w_o": given["L0_attn_Wo"].T,
        "ffn_gate": given["L1_ffn_w_gate"], "ffn_up": given["L1_ffn_w_up"], "ffn_down": given["L1_ffn_w_down"],
        "in_w": given["L1_attn_in_proj_w"].T,
        "conv_w": given["L1_attn_conv_w"].reshape(CONV_TILES, P, TAPS).transpose(1, 0, 2),
        "conv_b": given["L1_attn_conv_b"].reshape(CONV_TILES, P).T,
        "dt_bias": given["L1_attn_dt_bias"], "a_log": given["L1_attn_A_log"], "d_skip": given["L1_attn_D"],
        "norm_w": given["L1_attn_norm_w"].reshape(HM, PD).T,
        "out_w": given["L1_attn_out_proj_w"].T,
    }
    nc = bacc.Bacc("TRN2", target_bir_lowering=False, num_devices=1)
    aps, in_map = {}, {}
    for name, a in arrays.items():
        in_map[f"in_{name}"] = np.ascontiguousarray(a)
        aps[name] = nc.dram_tensor(f"in_{name}", a.shape, mybir.dt.from_np(a.dtype), kind="ExternalInput").ap()
    out = nc.dram_tensor("out_0", (1, S, D), F32, kind="ExternalOutput").ap()
    x = aps.pop("x")
    macaron_kernel(nc, x, out, *aps.values())
    result = run_bass_kernel_spmd(nc, [in_map], core_ids=[0])
    return result.results[0]["out_0"]
```
